# Optimizing a Trainium2 kernel written in Bass

```python
import numpy as np
import jax
import jax.numpy as jnp

def _softmax(x, axis=-1):
    return jax.nn.softmax(x, axis=axis)

def _gelu(x):
    return jax.nn.gelu(x, approximate=True)

def _silu(x):
    return jax.nn.silu(x)

def _sigmoid(x):
    return jax.nn.sigmoid(x)

def _layernorm(x, axis=-1, eps=1e-05):
    m = jnp.mean(x, axis=axis, keepdims=True)
    v = jnp.var(x, axis=axis, keepdims=True)
    return (x - m) / jnp.sqrt(v + eps)

def _scatter_add(tgt, idx, src, axis=0):
    return tgt.at[idx].add(src)

def _segment_sum(src, seg, n):
    return jax.ops.segment_sum(src, seg, n)
kernel_name = 'mk_lm_tower_d2_tok_ids512_r4_35aa5e'

def setup_inputs(seed: int=0):
    np.random.seed(seed)
    _w = jnp.asarray

    def _rec_inputs():
        import jax
        import jax.numpy as jnp
        _rk = jax.random.key(seed)
        x = jax.random.randint(jax.random.fold_in(_rk, 1), (2, 1024), 0, 16, jnp.int32)
        return x
    x = _rec_inputs()

    def _L0_tok_setup():
        import jax, jax.numpy as jnp
        import numpy as np
        VOCAB = 16
        D_MODEL = 128
        D_EMB = int(D_MODEL * 0.7)
        D_STFT = D_MODEL - D_EMB
        N_FFT = 64
        HOP = 64
        N_FREQ = N_FFT // 2 + 1
        B, L = (4, 2048)

        def _stft_mag(signal):
            pad = N_FFT // 2
            padded = jnp.pad(signal, ((0, 0), (pad, pad)), mode='reflect')
            n_frames = signal.shape[1] // HOP + 1
            idx = jnp.arange(n_frames)[:, None] * HOP + jnp.arange(N_FFT)[None, :]
            window = 0.5 - 0.5 * jnp.cos(2.0 * jnp.pi * jnp.arange(N_FFT) / N_FFT)
            frames = padded[:, idx] * window.astype(signal.dtype)
            return jnp.abs(jnp.fft.rfft(frames, axis=-1))
        key = jax.random.key(seed)
        k1, k2, k3, k4 = jax.random.split(key, 4)
        input_ids = jax.random.randint(k1, (B, L), 0, VOCAB)
        emb_table = jax.random.normal(k2, (VOCAB, D_EMB), dtype=jnp.float32) * 0.02
        proj_w = jax.random.normal(k3, (VOCAB * N_FREQ, D_STFT), dtype=jnp.float32) * 0.02
        proj_b = jnp.zeros((D_STFT,), dtype=jnp.float32)
        return {'input_ids': input_ids, 'emb_table': emb_table, 'proj_w': proj_w, 'proj_b': proj_b}
    _L0_tok_all = _L0_tok_setup()
    _L0_tok_in = {k: v for k, v in _L0_tok_all.items() if k in ('emb_table', 'proj_w', 'proj_b')}
    del _L0_tok_all

    def _L0_attn_setup():
        import jax, jax.numpy as jnp
        import numpy as np
        N_HEADS = 8
        D_K = 64
        NEG = 1000000000.0
        key = jax.random.key(seed)
        k1, k2, k3 = jax.random.split(key, 3)
        B, L, C = (4, 512, 128)
        x = jax.random.normal(k1, (B, L, C), dtype=jnp.float32)
        W_in = jax.random.normal(k2, (C, N_HEADS * D_K * 3), dtype=jnp.float32) * C ** (-0.5)
        b_in = jnp.zeros((N_HEADS * D_K * 3,), dtype=jnp.float32)
        W_out = jax.random.normal(k3, (N_HEADS * D_K, C), dtype=jnp.float32) * (N_HEADS * D_K) ** (-0.5)
        b_out = jnp.zeros((C,), dtype=jnp.float32)
        return {'x': x, 'W_in': W_in, 'b_in': b_in, 'W_out': W_out, 'b_out': b_out}
    _L0_attn_all = _L0_attn_setup()
    _L0_attn_in = {k: v for k, v in _L0_attn_all.items() if k in ('W_in', 'b_in', 'W_out', 'b_out')}
    del _L0_attn_all

    def _L0_ffn_setup():
        import jax, jax.numpy as jnp
        import numpy as np
        D_MODEL = 128
        D_FF = 512
        N_EXPERTS = 8
        TOP_K = 2
        SEQ = 1024
        BATCH = 8
        FREQ_D = 2 * D_MODEL
        LN_EPS = 1e-05
        key = jax.random.key(seed)
        ks = jax.random.split(key, 12)
        s = 0.02
        return {'x': jax.random.normal(ks[0], (BATCH, SEQ, D_MODEL), dtype=jnp.float32), 'pin_w': jax.random.normal(ks[1], (FREQ_D, D_MODEL), dtype=jnp.float32) * s, 'pin_b': jax.random.normal(ks[2], (D_MODEL,), dtype=jnp.float32) * s, 'router_w': jax.random.normal(ks[3], (D_MODEL, N_EXPERTS), dtype=jnp.float32) * s, 'router_b': jax.random.normal(ks[4], (N_EXPERTS,), dtype=jnp.float32) * s, 'w1': jax.random.normal(ks[5], (N_EXPERTS, D_MODEL, D_FF), dtype=jnp.float32) * s, 'b1': jax.random.normal(ks[6], (N_EXPERTS, D_FF), dtype=jnp.float32) * s, 'w2': jax.random.normal(ks[7], (N_EXPERTS, D_FF, D_MODEL), dtype=jnp.float32) * s, 'b2': jax.random.normal(ks[8], (N_EXPERTS, D_MODEL), dtype=jnp.float32) * s, 'pout_w': jax.random.normal(ks[9], (D_MODEL, FREQ_D), dtype=jnp.float32) * s, 'pout_b': jax.random.normal(ks[10], (FREQ_D,), dtype=jnp.float32) * s, 'ln_g': jnp.ones((D_MODEL,), dtype=jnp.float32), 'ln_b': jnp.zeros((D_MODEL,), dtype=jnp.float32)}
    _L0_ffn_all = _L0_ffn_setup()
    _L0_ffn_in = {k: v for k, v in _L0_ffn_all.items() if k in ('pin_w', 'pin_b', 'router_w', 'router_b', 'w1', 'b1', 'w2', 'b2', 'pout_w', 'pout_b', 'ln_g', 'ln_b')}
    del _L0_ffn_all

    def _L1_attn_setup():
        import jax, jax.numpy as jnp
        import numpy as np
        key = jax.random.key(seed)
        x = jax.random.normal(key, (8, 512, 128), dtype=jnp.float32)
        return {'x': x}
    _L1_attn_all = _L1_attn_setup()
    _L1_attn_in = {k: v for k, v in _L1_attn_all.items() if k in ()}
    del _L1_attn_all

    def _L1_ffn_setup():
        import jax, jax.numpy as jnp
        import numpy as np
        NUM_EXPERTS = 8
        TOP_K = 2
        key = jax.random.key(seed)
        k0, k1, k2, k3, k4 = jax.random.split(key, 5)
        sl, bs, hs, ffn = (512, 2, 128, 512)
        T = sl * bs
        x = jax.random.normal(k0, (sl, bs, hs), jnp.float32)
        expert_weights = jax.random.uniform(k1, (T, TOP_K), jnp.float32)
        expert_indices = jax.random.randint(k2, (T, TOP_K), 0, NUM_EXPERTS)
        w1 = jax.random.normal(k3, (NUM_EXPERTS, hs, ffn), jnp.float32) * hs ** (-0.5)
        w2 = jax.random.normal(k4, (NUM_EXPERTS, ffn, hs), jnp.float32) * ffn ** (-0.5)
        return dict(x=x, expert_weights=expert_weights, expert_indices=expert_indices, w1=w1, w2=w2)
    _L1_ffn_all = _L1_ffn_setup()
    _L1_ffn_in = {k: v for k, v in _L1_ffn_all.items() if k in ('expert_weights', 'expert_indices', 'w1', 'w2')}
    del _L1_ffn_all
    return {'x': x, 'L0_tok_emb_table': _L0_tok_in['emb_table'], 'L0_tok_proj_w': _L0_tok_in['proj_w'], 'L0_tok_proj_b': _L0_tok_in['proj_b'], 'L0_attn_W_in': _L0_attn_in['W_in'], 'L0_attn_b_in': _L0_attn_in['b_in'], 'L0_attn_W_out': _L0_attn_in['W_out'], 'L0_attn_b_out': _L0_attn_in['b_out'], 'L0_ffn_pin_w': _L0_ffn_in['pin_w'], 'L0_ffn_pin_b': _L0_ffn_in['pin_b'], 'L0_ffn_router_w': _L0_ffn_in['router_w'], 'L0_ffn_router_b': _L0_ffn_in['router_b'], 'L0_ffn_w1': _L0_ffn_in['w1'], 'L0_ffn_b1': _L0_ffn_in['b1'], 'L0_ffn_w2': _L0_ffn_in['w2'], 'L0_ffn_b2': _L0_ffn_in['b2'], 'L0_ffn_pout_w': _L0_ffn_in['pout_w'], 'L0_ffn_pout_b': _L0_ffn_in['pout_b'], 'L0_ffn_ln_g': _L0_ffn_in['ln_g'], 'L0_ffn_ln_b': _L0_ffn_in['ln_b'], 'L1_ffn_expert_weights': _L1_ffn_in['expert_weights'], 'L1_ffn_expert_indices': _L1_ffn_in['expert_indices'], 'L1_ffn_w1': _L1_ffn_in['w1'], 'L1_ffn_w2': _L1_ffn_in['w2']}

def reference(x, L0_tok_emb_table, L0_tok_proj_w, L0_tok_proj_b, L0_attn_W_in, L0_attn_b_in, L0_attn_W_out, L0_attn_b_out, L0_ffn_pin_w, L0_ffn_pin_b, L0_ffn_router_w, L0_ffn_router_b, L0_ffn_w1, L0_ffn_b1, L0_ffn_w2, L0_ffn_b2, L0_ffn_pout_w, L0_ffn_pout_b, L0_ffn_ln_g, L0_ffn_ln_b, L1_ffn_expert_weights, L1_ffn_expert_indices, L1_ffn_w1, L1_ffn_w2):
    import jax
    import jax.numpy as jnp

    def _L0_tok_ref(input_ids, emb_table, proj_w, proj_b):
        import jax, jax.numpy as jnp
        import numpy as np
        VOCAB = 16
        D_MODEL = 128
        D_EMB = int(D_MODEL * 0.7)
        D_STFT = D_MODEL - D_EMB
        N_FFT = 64
        HOP = 64
        N_FREQ = N_FFT // 2 + 1
        B, L = (4, 2048)

        def _stft_mag(signal):
            pad = N_FFT // 2
            padded = jnp.pad(signal, ((0, 0), (pad, pad)), mode='reflect')
            n_frames = signal.shape[1] // HOP + 1
            idx = jnp.arange(n_frames)[:, None] * HOP + jnp.arange(N_FFT)[None, :]
            window = 0.5 - 0.5 * jnp.cos(2.0 * jnp.pi * jnp.arange(N_FFT) / N_FFT)
            frames = padded[:, idx] * window.astype(signal.dtype)
            return jnp.abs(jnp.fft.rfft(frames, axis=-1))
        b, seq_len = input_ids.shape
        word_embeds = emb_table[input_ids]
        onehot = jax.nn.one_hot(input_ids, VOCAB, dtype=jnp.float32)
        signal = onehot.transpose(0, 2, 1).reshape(b * VOCAB, seq_len)
        spec = _stft_mag(signal)
        n_frames = spec.shape[1]
        stft_mag = spec.reshape(b, VOCAB, n_frames, N_FREQ).transpose(0, 1, 3, 2)
        stft_to_up = stft_mag.transpose(0, 2, 1, 3).reshape(b, N_FREQ * VOCAB, n_frames)
        up_idx = jnp.arange(seq_len) * n_frames // seq_len
        stft_up = stft_to_up[:, :, up_idx]
        feats = stft_up.transpose(0, 2, 1)
        stft_enc = jnp.einsum('bli,io->blo', feats, proj_w) + proj_b
        return jnp.concatenate([word_embeds, stft_enc], axis=-1)

    def _L0_attn_ref(x, W_in, b_in, W_out, b_out):
        import jax, jax.numpy as jnp
        import numpy as np
        N_HEADS = 8
        D_K = 64
        NEG = 1000000000.0
        B, L, C = x.shape
        H, Dk = (N_HEADS, D_K)
        scale = Dk ** (-0.5)
        qkv = x @ W_in + b_in
        qkv = qkv.reshape(B, L, H, 3 * Dk)
        q, k, v = jnp.split(qkv, 3, axis=-1)
        attn = jnp.einsum('bihd,bjhd->bijh', q, k) * scale
        mask = jnp.tril(jnp.ones((L, L), dtype=x.dtype))[None, :, :, None]
        attn = attn * mask - NEG * (1.0 - mask)
        attn = jax.nn.softmax(attn, axis=2)
        res = jnp.einsum('bijh,bjhd->bihd', attn, v)
        res = res.reshape(B, L, H * Dk)
        res = res @ W_out + b_out
        return res + x

    def _L0_ffn_ref(x, pin_w, pin_b, router_w, router_b, w1, b1, w2, b2, pout_w, pout_b, ln_g, ln_b):
        import jax, jax.numpy as jnp
        import numpy as np
        D_MODEL = 128
        D_FF = 512
        N_EXPERTS = 8
        TOP_K = 2
        SEQ = 1024
        BATCH = 8
        FREQ_D = 2 * D_MODEL
        LN_EPS = 1e-05
        B, S, D = x.shape
        residual = x
        xf = jnp.fft.rfft(x, axis=1, norm='ortho')
        xf_ri = jnp.concatenate([xf.real, xf.imag], axis=-1)
        h = xf_ri @ pin_w + pin_b
        logits = h @ router_w + router_b
        topk_logits, topk_idx = jax.lax.top_k(logits, TOP_K)
        topk_w = jax.nn.softmax(topk_logits, axis=-1)
        hid = jax.nn.gelu(jnp.einsum('bfd,edh->befh', h, w1) + b1[None, :, None, :], approximate=False)
        all_out = jnp.einsum('befh,ehd->befd', hid, w2) + b2[None, :, None, :]
        all_out = jnp.swapaxes(all_out, 1, 2)
        sel = jnp.take_along_axis(all_out, topk_idx[..., None], axis=2)
        moe_out = jnp.sum(sel * topk_w[..., None], axis=2)
        of = moe_out @ pout_w + pout_b
        oc = jax.lax.complex(of[:, :, :D], of[:, :, D:])
        ot = jnp.fft.irfft(oc, n=S, axis=1, norm='ortho')
        mu = jnp.mean(ot, axis=-1, keepdims=True)
        var = jnp.mean(jnp.square(ot - mu), axis=-1, keepdims=True)
        ot = (ot - mu) * jax.lax.rsqrt(var + LN_EPS) * ln_g + ln_b
        return ot + residual

    def _L1_attn_ref(x):
        import jax, jax.numpy as jnp
        import numpy as np
        scores = jnp.einsum('btd,bsd->bts', x, x)
        w = jax.nn.softmax(scores, axis=-1)
        return jnp.einsum('bts,bsd->btd', w, x)

    def _L1_ffn_ref(x, expert_weights, expert_indices, w1, w2):
        import jax, jax.numpy as jnp
        import numpy as np
        NUM_EXPERTS = 8
        TOP_K = 2
        'Dropless MoE: sort assignments by expert, gather tokens, grouped MLP,\n            scatter-combine with top-k router weights (megablocks gather/scatter semantics).'
        in_shape = x.shape
        hs = in_shape[-1]
        x_flat = x.reshape(-1, hs)
        T = x_flat.shape[0]
        flat_ids = expert_indices.reshape(-1)
        order = jnp.argsort(flat_ids)
        bin_ids = flat_ids[order]
        token_ids = order // TOP_K
        xg = x_flat[token_ids]
        y = jnp.zeros_like(xg)
        for e in range(NUM_EXPERTS):
            h = jax.nn.gelu(xg @ w1[e], approximate=False)
            y = jnp.where((bin_ids == e)[:, None], h @ w2[e], y)
        w = expert_weights.reshape(-1)[order][:, None]
        out = jnp.zeros((T, hs), x.dtype).at[token_ids].add(w * y)
        return out.reshape(in_shape)
    h = _L0_tok_ref(x, L0_tok_emb_table, L0_tok_proj_w, L0_tok_proj_b)
    h = h + _L0_attn_ref(_layernorm(h, axis=-1), L0_attn_W_in, L0_attn_b_in, L0_attn_W_out, L0_attn_b_out)
    h = h + _L0_ffn_ref(_layernorm(h, axis=-1), L0_ffn_pin_w, L0_ffn_pin_b, L0_ffn_router_w, L0_ffn_router_b, L0_ffn_w1, L0_ffn_b1, L0_ffn_w2, L0_ffn_b2, L0_ffn_pout_w, L0_ffn_pout_b, L0_ffn_ln_g, L0_ffn_ln_b)
    h = h + _L1_attn_ref(_layernorm(h, axis=-1))
    h = h + _L1_ffn_ref(_layernorm(h, axis=-1), L1_ffn_expert_weights, L1_ffn_expert_indices, L1_ffn_w1, L1_ffn_w2)
    return h

_drawn_inputs = setup_inputs


def setup_inputs(seed=0):
    import zlib

    import numpy as np

    out = dict(_drawn_inputs(seed))
    spreads = {'L0_tok_proj_b': (0.0, 0.1),
     'L0_attn_b_in': (0.0, 0.1),
     'L0_attn_b_out': (0.0, 0.1),
     'L0_ffn_ln_g': (1.0, 0.2),
     'L0_ffn_ln_b': (0.0, 0.1)}
    factors = {'L0_ffn_b1': 2.976}
    for name, (base, spread) in spreads.items():
        noise = np.random.default_rng([zlib.crc32(name.encode()), seed]).standard_normal(out[name].shape)
        drawn = base * np.exp(spread * noise) if base else spread * noise
        out[name] = jnp.asarray(drawn.astype(out[name].dtype))
    for name, factor in factors.items():
        out[name] = (out[name] * factor).astype(out[name].dtype)
    return out
```

```python
from contextlib import ExitStack

import numpy as np

import concourse.bass as bass
from concourse import mybir

P = 128
B, L, D = 2, 1024, 128
VOCAB, D_EMB, D_STFT = 16, 89, 39
N_FFT, N_FREQ, N_FRAMES = 64, 33, 17
NFR = B * N_FRAMES
H, DK = 8, 64
LN_EPS = 1e-5
TB = L // P
NT = B * TB
HALF = 512
SEL_K = 80
VOCAB_AT = 64
VW = 96
QK = DK + 1
NEG = -1.0e9
E, FF = 8, 512
FC = FF // P
RES = 8
M64 = L // 2 // RES
NYQ = B * RES * M64
NF = NYQ + B
FT = 9
FCH = NF // 3
C8 = float(np.sqrt(0.5))
POOL_CONSTS = 12
FOURIER_LOADS = 15
RING = (3, 4)
LOADS = (48, 32)

F32 = mybir.dt.float32
BF16 = mybir.dt.bfloat16
I32 = mybir.dt.int32
U32 = mybir.dt.uint32
ALU = mybir.AluOpType
ACT = mybir.ActivationFunctionType
AX = mybir.AxisListType


def max_chunks():
    return [(j, c, min(HALF, P * (j + 1) - HALF * c)) for j in range(TB) for c in range(2)
            if P * (j + 1) > HALF * c]


def score_chunks():
    out = []
    for half in range(2):
        for i in range(TB):
            first = max(P * i, HALF * half)
            if first < HALF * (half + 1):
                out.append((half, i, first, HALF * (half + 1) - first))
    return out


def tower(nc, a, out):
    m_chunks = max_chunks()
    s_chunks = score_chunks()
    NM, NS = len(m_chunks), len(s_chunks)
    s_first = [sum(c[3] for c in s_chunks[:n]) for n in range(NS + 1)]
    chunk_of = {(half, i): n for n, (half, i, _, _) in enumerate(s_chunks)}

    with ExitStack() as ctx:
        def sb(name, shape, dt=F32):
            return ctx.enter_context(nc.sbuf_tensor(name, shape, dt))

        def sem(name):
            return ctx.enter_context(nc.semaphore(name))

        bank = [ctx.enter_context(nc.psum_tensor(f"bank{i}", [P, HALF], F32)) for i in range(8)]

        h = sb("h", [P, NT, D])
        ln = sb("ln", [P, NT, D])
        ln_t = sb("ln_t", [P, B * L])
        base = sb("base", [P, NT, D])
        ident = sb("ident", [P, P])
        stats = sb("stats", [P, NT, 6])
        mv = sb("mv", [P, NT, 2])
        var_eps = sb("var_eps", [P, NT])
        minus_half = sb("minus_half", [P, NT])
        rstd = sb("rstd", [P, NT])

        ARENA = 29184
        arena = sb("arena", [P, ARENA])

        def part(first, *shape, rows=slice(0, P)):
            n = int(np.prod(shape))
            assert first + n <= ARENA, (first, shape)
            view = arena[rows, first:first + n]
            if len(shape) == 2:
                view = view.rearrange("p (a b) -> p a b", b=shape[1])
            if len(shape) == 3:
                view = view.rearrange("p (a b c) -> p a b c", b=shape[1], c=shape[2])
            return view

        v_all = part(0, NT, H * DK)
        o_all = part(8192, NT, H * DK)
        p_t = part(16384, s_first[NS])
        v_head = [part(20992 + 768 * i, TB, VW) for i in range(2)]
        q_t = [part(22528 + 1024 * i, L) for i in range(2)]
        k_t = [part(24576 + 1024 * i, L) for i in range(2)]
        max_pad = part(26624, TB, QK)
        o_t = [part(27264 + 512 * i, HALF) for i in range(2)]
        w_v = part(28288, H * DK)
        tok_sel = part(8192, B * L, rows=slice(0, SEL_K))
        tok_tab = part(10240, D, rows=slice(0, SEL_K))
        seen = part(10368, VOCAB, NFR, rows=slice(0, N_FFT))
        re_sq = part(10912, VOCAB * NFR, rows=slice(0, N_FREQ))
        im_sq = part(11456, VOCAB * NFR, rows=slice(0, N_FREQ))
        mag = part(12000, VOCAB, NFR, rows=slice(0, N_FREQ))
        proj_w = part(12544, VOCAB, D_STFT, rows=slice(0, N_FREQ))
        proj_b = part(13184, D_STFT, rows=slice(0, NFR))
        dft64 = part(13248, 2, N_FREQ, rows=slice(0, N_FFT))
        b_v = part(13376, H * DK)
        mask_f = part(13888, P)
        ids_i = part(14016, B * L, rows=slice(VOCAB_AT, SEL_K)).bitcast(I32)
        frames_i = part(16064, NFR, rows=slice(0, N_FFT)).bitcast(I32)

        vocab_row = sb("vocab_row", [N_FFT, VOCAB])
        vocab_col = sb("vocab_col", [P, 1])
        w_head = sb("w_head", [P, 2 * QK])
        b_head = sb("b_head", [QK, 2])
        w_out = sb("w_out", [P, 4, D])
        b_out = sb("b_out", [P, D])
        mask_b = sb("mask_b", [P, P], BF16)
        ident_b = sb("ident_b", [P, P], BF16)
        max_part = sb("max_part", [P, TB])
        o_scale = sb("o_scale", [P, TB])

        y = part(0, 6, B, D)
        sum4 = part(1536, B, 4, D)
        dif4 = part(2560, B, 4, D)
        ev2 = part(3584, B, 2, D)
        od2 = part(4096, B, 2, D)
        dd = part(4608, B, D)
        gg = part(4864, B, D)
        xf = part(5632, 2, NF)
        h_t = part(7688, FT * P)
        hid_f = [part(8840 + 4104 * i, FC, NF) for i in range(2)]
        acc_f = part(17048, FT, D)
        moe_t = part(18200, FT * P)
        wsel_t = part(19352, FT * P, rows=slice(0, E))
        of = part(20504, RES, B, D)
        comb = part(22552, 8, B, D)
        ot = part(24600, NT, D)
        inv = part(0, 12, B, D)
        p_2 = [part(8192 * i, TB, L) for i in range(2)]
        z_one = part(16384, NT, 130)
        hid_g = [part(19000 + 4096 * i, FC, L) for i in range(2)]
        acc_g = part(27192, TB, D)

        fwd_single = sb("fwd_single", [P, 258])
        fwd_pair = sb("fwd_pair", [P, 6, 256])
        inverse = sb("inverse", [P, 14, P])
        w1 = [sb(f"w1_{i}", [P, FF]) for i in range(2)]
        w2 = [sb(f"w2_{i}", [P, FC, D]) for i in range(2)]
        b1 = [sb(f"b1_{i}", [P, FC]) for i in range(2)]
        pin_w = sb("pin_w", [P, 2, D])
        pin_b = sb("pin_b", [P, 1])
        router_w = sb("router_w", [P, E])
        router_b = sb("router_b", [P, E])
        b2 = sb("b2", [E, D])
        pout_w = sb("pout_w", [P, 2, D])
        pout_b = sb("pout_b", [P, 2, D])
        ln_g = sb("ln_g", [P, D])
        ln_b = sb("ln_b", [P, D])
        expert_no = sb("expert_no", [P, E])
        logits = sb("logits", [P, FT, E])
        top8 = sb("top8", [P, FT, 8])
        idx8 = sb("idx8", [P, FT, 8], U32)
        choice = sb("choice", [P, FT, 2])
        gap = sb("gap", [P, FT, 1])
        odds = sb("odds", [P, FT, 1])
        odds1 = sb("odds1", [P, FT, 1])
        share = sb("share", [P, FT, 2])
        pick = [sb(f"pick{i}", [P, FT, E]) for i in range(2)]
        wsel_f = sb("wsel_f", [P, FT, E])
        gate_w = sb("gate_w", [P, TB, 2])
        gate_i = sb("gate_i", [P, TB, 2], I32)
        gate_no = sb("gate_no", [P, TB, 2])
        wsel_g = sb("wsel_g", [P, TB, E])
        neg_row = sb("neg_row", [P, L], BF16)
        ones_b = sb("ones_b", [P, P], BF16)
        max2 = sb("max2", [P, TB, 2])
        neg_max = sb("neg_max", [P, TB, 1])
        den2 = sb("den2", [P, NT])

        ids_loaded = sem("ids_loaded")
        tok_loaded = sem("tok_loaded")
        attn_loaded = sem("attn_loaded")
        w_head_loaded = sem("w_head_loaded")
        pool_const = sem("pool_const")
        tok_cleared = sem("tok_cleared")
        seen_ready = sem("seen_ready")
        dft_done = sem("dft_done")
        squares = sem("squares")
        power_ready = sem("power_ready")
        mag_ready = sem("mag_ready")
        enc_done = sem("enc_done")
        tab_ready = sem("tab_ready")
        sel_ready = sem("sel_ready")
        tok_done = sem("tok_done")
        h_ready = sem("h_ready")
        stats_done = sem("stats_done")
        mean_done = sem("mean_done")
        var_ready = sem("var_ready")
        rstd_ready = sem("rstd_ready")
        ln_ready = sem("ln_ready")
        turned = sem("turned")
        ln_t_ready = sem("ln_t_ready")
        consts_b = sem("consts_b")
        v_done = sem("v_done")
        v_ready = sem("v_ready")
        v_head_ready = sem("v_head_ready")
        q_done = sem("q_done")
        k_done = sem("k_done")
        q_ready = sem("q_ready")
        k_ready = sem("k_ready")
        rows_done = sem("rows_done")
        rows_used = sem("rows_used")
        max_ready = sem("max_ready")
        max_turned = sem("max_turned")
        max_row_ready = sem("max_row_ready")
        scores_done = sem("scores_done")
        probs_ready = sem("probs_ready")
        pv_done = [sem("pv_done0"), sem("pv_done1")]
        den_ready = [sem("den_ready0"), sem("den_ready1")]
        o_ready = [sem("o_ready0"), sem("o_ready1")]
        base_ready = sem("base_ready")
        o_turned = sem("o_turned")
        o_t_ready = sem("o_t_ready")
        out_done = sem("out_done")
        stored = sem("stored")
        fourier_loaded = sem("fourier_loaded")
        pad_cleared = sem("pad_cleared")
        base_f_ready = sem("base_f_ready")
        fold1 = sem("fold1")
        fold2 = sem("fold2")
        fold3 = sem("fold3")
        y_ready = sem("y_ready")
        spec_done = sem("spec_done")
        spec_ready_a = sem("spec_ready_a")
        spec_ready_v = sem("spec_ready_v")
        pin_done = sem("pin_done")
        h_t_ready = sem("h_t_ready")
        router_done = sem("router_done")
        logits_ready = sem("logits_ready")
        top_ready = sem("top_ready")
        idx_ready = sem("idx_ready")
        gap_ready = sem("gap_ready")
        odds_ready = sem("odds_ready")
        route = sem("route")
        wsel_ready = sem("wsel_ready")
        wsel_turned = sem("wsel_turned")
        wsel_t_ready = sem("wsel_t_ready")
        bias_done = sem("bias_done")
        moe_turned = sem("moe_turned")
        moe_t_ready = sem("moe_t_ready")
        of_done = sem("of_done")
        of_ready = sem("of_ready")
        inv_done = sem("inv_done")
        comb_ready_a = sem("comb_ready_a")
        comb_ready_v = sem("comb_ready_v")
        unfold1 = sem("unfold1")
        unfold2 = sem("unfold2")
        unfold3 = sem("unfold3")
        ot_ready = sem("ot_ready")
        ot_norm = sem("ot_norm")
        ot_scaled = sem("ot_scaled")
        h2_ready = sem("h2_ready")
        experts_loaded = [[sem(f"experts_loaded{n}_{i}") for i in range(2)] for n in range(2)]
        hidden_done = [sem("hidden_done0"), sem("hidden_done1")]
        hidden_ready = [sem("hidden_ready0"), sem("hidden_ready1")]
        expert_done = [sem("expert_done0"), sem("expert_done1")]
        acc_ready = [sem("acc_ready0"), sem("acc_ready1")]
        z_ready = sem("z_ready")
        rows2_done = sem("rows2_done")
        rows2_used = sem("rows2_used")
        neg_max_ready = sem("neg_max_ready")
        max2_turned = sem("max2_turned")
        neg_row_ready = sem("neg_row_ready")
        scores2_done = sem("scores2_done")
        probs2_ready = sem("probs2_ready")
        pv2_done = sem("pv2_done")
        den2_ready = sem("den2_ready")
        h3_ready = sem("h3_ready")
        gates = sem("gates")

        pj, sm, st, pv = bank[0:2], bank[2:4], bank[4:6], bank[6:8]

        def spectrum(copy, eng, b, ready):
            grouped = xf[:, :, 0:NYQ].rearrange("p c (g m) -> p c g m", m=M64)
            eng.wait_ge(spec_done, 4 * b + 1)
            copy(grouped[:, :, b * RES, :], bank[4 * b][:, 0:2 * M64].rearrange("p (c m) -> p c m", c=2)).then_inc(ready, 1)
            copy(grouped[:, :, b * RES + 4, :], bank[4 * b][:, 256:256 + 2 * M64].rearrange("p (c m) -> p c m", c=2)).then_inc(ready, 1)
            copy(xf[:, :, NYQ + b:NYQ + b + 1], bank[4 * b][:, 2 * M64:2 * M64 + 2].unsqueeze(2)).then_inc(ready, 1)
            for r in range(1, 4):
                eng.wait_ge(spec_done, 4 * b + r + 1)
                pair = grouped[:, :, b * RES + r:b * RES + 9 - r:8 - 2 * r, :]
                copy(pair, bank[4 * b + r][:, 0:4 * M64].rearrange("p (k c m) -> p c k m", k=2, c=2)).then_inc(ready, 1)

        block = ctx.enter_context(nc.Block())

        @block.sync
        def _(sp):
            sp.dma_start(frames_i, a["ids_frames"]).then_inc(ids_loaded, 16)
            sp.dma_start(vocab_row[:], a["vocab_row"]).then_inc(ids_loaded, 16)
            sp.dma_start(dft64, a["dft64"]).then_inc(ids_loaded, 16)
            sp.dma_start(ids_i, a["ids_bcast"]).then_inc(ids_loaded, 16)
            sp.dma_start(vocab_col[:], a["vocab_col"]).then_inc(ids_loaded, 16)
            sp.dma_start(proj_w, a["proj_w"].rearrange("(f v) o -> f v o", v=VOCAB)).then_inc(tok_loaded, 16)
            sp.dma_start(proj_b, a["proj_b"]).then_inc(tok_loaded, 16)
            sp.wait_ge(tok_cleared, 2)
            sp.dma_start(tok_tab[VOCAB_AT:SEL_K, 0:D_EMB], a["emb_table"]).then_inc(tok_loaded, 16)
            sp.dma_start(tok_sel[0:NFR, :], a["upsample"]).then_inc(tok_loaded, 16)
            sp.dma_start(ident[:], a["ident"]).then_inc(attn_loaded, 16)
            sp.dma_start(mask_f, a["mask"]).then_inc(attn_loaded, 16)
            sp.dma_start(w_v, a["w_v"]).then_inc(attn_loaded, 16)
            sp.dma_start(b_v, a["b_v"]).then_inc(attn_loaded, 16)
            sp.dma_start(w_out[:], a["w_out"].rearrange("(c p) d -> p c d", p=P)).then_inc(attn_loaded, 16)
            sp.dma_start(b_out[:], a["b_out"]).then_inc(attn_loaded, 16)
            sp.dma_start(w_head[:], a["w_qk"][0]).then_inc(w_head_loaded, 16)
            sp.dma_start(b_head[:], a["b_qk"][0]).then_inc(w_head_loaded, 16)
            for to, name in ((fwd_single[:], "fwd_single"), (fwd_pair[:], "fwd_pair"), (inverse[:], "inverse"),
                             (pin_b[:], "pin_b"), (router_w[:], "router_w"), (router_b[:], "router_b"), (b2[:], "b2"),
                             (pout_b[:], "pout_b"), (ln_g[:], "ln_g"), (ln_b[:], "ln_b"), (expert_no[:], "expert_no"),
                             (gate_w[:], "gate_w"), (gate_i[:], "gate_i")):
                sp.dma_start(to, a[name]).then_inc(fourier_loaded, 16)
            sp.dma_start(pin_w[:], a["pin_w"].rearrange("(c p) d -> p c d", p=P)).then_inc(fourier_loaded, 16)
            sp.dma_start(pout_w[:], a["pout_w"].rearrange("p (c d) -> p c d", d=D)).then_inc(fourier_loaded, 16)
            with sp.Fori(0, H - 1) as hd:
                sp.wait_ge(k_done, hd * 4 + 4)
                sp.dma_start(w_head[:], a["w_qk"][bass.ds(hd + 1, 1)].rearrange("o p n -> (o p) n")).then_inc(w_head_loaded, 16)
                sp.wait_ge(q_ready, hd * 4 + 4)
                sp.wait_ge(k_ready, hd * 4 + 4)
                sp.dma_start(b_head[:], a["b_qk"][bass.ds(hd + 1, 1)].rearrange("o p n -> (o p) n")).then_inc(w_head_loaded, 16)

            def load_expert(layer, e, i, bias):
                w1_from, w2_from = (a["w1_f"], a["w2_f"]) if layer == 0 else (a["w1_g"], a["w2_g"])
                sp.dma_start(w1[i][:], w1_from[bass.ds(e, 1)].rearrange("o d f -> (o d) f")).then_inc(experts_loaded[layer][i], 16)
                sp.dma_start(w2[i][:], w2_from[bass.ds(e, 1)].rearrange("o (c p) d -> (o p) c d", p=P)).then_inc(experts_loaded[layer][i], 16)
                if bias:
                    sp.dma_start(b1[i][:], a["b1_f"][bass.ds(e, 1)].rearrange("o p c -> (o p) c")).then_inc(experts_loaded[layer][i], 16)

            def buffers_read(layer, groups, tiles, e):
                sp.wait_ge(hidden_ready[layer], e * groups + groups)
                sp.wait_ge(expert_done[layer], e * tiles + tiles)

            for i in range(2):
                load_expert(0, i, i, True)
            with sp.Fori(0, E - 3, 2) as e:
                for i in range(2):
                    buffers_read(0, FC * 3, FT, e + i)
                    load_expert(0, e + i + 2, i, True)
            for i in range(2):
                buffers_read(0, FC * 3, FT, E - 2 + i)
                load_expert(1, i, i, False)
            sp.wait_ge(h3_ready, NT)
            sp.dma_start(out[L:, :].rearrange("(t p) d -> p t d", p=P), h[:, TB:, :]).then_inc(stored, 16)
            with sp.Fori(0, E - 3, 2) as e:
                for i in range(2):
                    buffers_read(1, FC * 2, TB, e + i)
                    load_expert(1, e + i + 2, i, False)
            sp.wait_ge(acc_ready[1], TB * (E + 1))
            sp.dma_start(out[0:L, :].rearrange("(t p) d -> p t d", p=P), acc_g).then_inc(stored, 16)
            sp.wait_ge(stored, 2 * 16)

        @block.gpsimd
        def _(pool):
            pool.memset(tok_sel[32:VOCAB_AT, :], 0.0).then_inc(tok_cleared, 1)
            pool.wait_ge(tok_cleared, 1)
            pool.memset(tok_tab, 0.0).then_inc(tok_cleared, 1)
            pool.wait_ge(tok_cleared, 2)
            pool.memset(minus_half[:], -0.5).then_inc(pool_const, 1)
            pool.wait_ge(pool_const, 1)
            pool.memset(max_pad, 0.0).then_inc(pool_const, 1)
            for i in range(2):
                pool.wait_ge(pool_const, 5 * i + 2)
                pool.memset(q_t[i][DK:P, :], 0.0).then_inc(pool_const, 1)
                pool.wait_ge(pool_const, 5 * i + 3)
                pool.memset(k_t[i][DK:P, :], 0.0).then_inc(pool_const, 1)
                pool.wait_ge(pool_const, 5 * i + 4)
                pool.memset(v_head[i][:, :, QK:VW], 0.0).then_inc(pool_const, 1)
                pool.wait_ge(pool_const, 5 * i + 5)
                pool.memset(v_head[i][:, :, DK:QK], 1.0).then_inc(pool_const, 2)

            def inverse_roots(n):
                b = n % B
                pool.wait_ge(var_ready, n + 1)
                tiles = slice(b * TB, (b + 1) * TB)
                pool.tensor_tensor(rstd[:, tiles], var_eps[:, tiles], minus_half[:, tiles], ALU.pow).then_inc(rstd_ready, 1)

            inverse_roots(0)
            inverse_roots(1)
            pool.wait_ge(ln_ready, NT)
            pool.wait_ge(attn_loaded, 6 * 16)
            pool.tensor_tensor(base[:], h[:], ln[:], ALU.add).then_inc(base_ready, 1)
            pool.wait_ge(base_ready, 1)
            pool.tensor_tensor(base[:], base[:], b_out[:].unsqueeze(1).broadcast_to([P, NT, D]), ALU.add).then_inc(base_ready, 1)

            def copy_values(hd, b):
                pool.tensor_copy(v_head[b][:, :, 0:DK], v_all[:, b * TB:(b + 1) * TB, bass.ds(hd * DK, DK)]).then_inc(v_head_ready, 1)

            def next_values(hd, b):
                pool.wait_ge(pv_done[1], hd * B + b + 1)
                copy_values(hd + b, 1 - b)

            pool.wait_ge(v_ready, NT)
            copy_values(0, 0)
            with pool.Fori(0, H - 1) as hd:
                next_values(hd, 0)
                next_values(hd, 1)
            next_values(H - 1, 0)

            inverse_roots(2)
            inverse_roots(3)
            pool.memset(h_t[:, NF:FT * P], 0.0).then_inc(pad_cleared, 1)
            pool.wait_ge(pad_cleared, 1)
            pool.memset(neg_row[:], 0.0).then_inc(pad_cleared, 1)
            pool.wait_ge(pad_cleared, 2)
            pool.memset(ones_b[:], 1.0).then_inc(pad_cleared, 1)
            pool.wait_ge(ln_ready, 2 * NT)
            pool.wait_ge(fourier_loaded, FOURIER_LOADS * 16)
            pool.tensor_tensor(base[:], h[:], ln[:], ALU.add).then_inc(base_f_ready, 1)
            pool.wait_ge(base_f_ready, 1)
            pool.tensor_tensor(base[:], base[:], ln_b[:].unsqueeze(1).broadcast_to([P, NT, D]), ALU.add).then_inc(base_f_ready, 1)
            inverse_roots(4)
            inverse_roots(5)

            inverse_roots(6)
            inverse_roots(7)
            for b in range(B):
                tiles = slice(b * TB, (b + 1) * TB)
                pool.wait_ge(ln_ready, 2 * NT + (b + 1) * TB)
                if b:
                    pool.wait_ge(z_ready, 2)
                pool.tensor_copy(z_one[:, tiles, 0:D], ln[:, tiles, :]).then_inc(z_ready, 1)
                pool.wait_ge(z_ready, 2 * b + 1)
                pool.memset(z_one[:, tiles, D:D + 1], 1.0).then_inc(z_ready, 1)
            inverse_roots(8)

        @block.scalar
        def _(act):
            for i in range(4):
                act.wait_ge(dft_done, i + 1)
                half = i % 2
                to = (re_sq, im_sq)[i // 2][:, half * 272:(half + 1) * 272]
                act.activation(to, bank[i][0:N_FREQ, 0:272], ACT.Square).then_inc(squares, 1)
            act.wait_ge(power_ready, 1)
            act.activation(mag.rearrange("p v n -> p (v n)"), re_sq, ACT.Sqrt).then_inc(mag_ready, 1)
            for i in range(4):
                act.wait_ge(tok_done, i + 1)
                act.copy(h[:, 4 * i:4 * i + 4, :], bank[i].rearrange("p (t d) -> p t d", d=D)).then_inc(h_ready, 1)

            def features_down(n):
                for i in range(2):
                    act.wait_ge(turned, 2 * n + i + 1)
                    first = (n % B) * L + HALF * i
                    act.copy(ln_t[:, first:first + HALF], bank[4 + i][:]).then_inc(ln_t_ready, 1)

            features_down(0)
            features_down(1)

            def queries(hd, b):
                n = hd * B + b
                for c in range(2):
                    act.wait_ge(q_done, n * 2 + c + 1)
                    act.activation(q_t[b][0:QK, HALF * c:HALF * (c + 1)], pj[c][0:QK, :], ACT.Identity, bias=b_head[:, 0:1]).then_inc(q_ready, 1)

            def exp_head(hd, b, last=False):
                n = hd * B + b
                if not last:
                    queries(hd + b, 1 - b)
                for c, (half, i, first, width) in enumerate(s_chunks):
                    if c == 0 or s_chunks[c - 1][0] != half:
                        act.wait_ge(pv_done[half], n + 1)
                    act.wait_ge(scores_done, n * NS + c + 1)
                    act.activation(p_t[:, s_first[c]:s_first[c] + width], st[c % 2][:, 0:width], ACT.Exp, scale=DK ** -0.5).then_inc(probs_ready, 1)

            act.wait_ge(attn_loaded, 6 * 16)
            act.wait_ge(pool_const, POOL_CONSTS)
            queries(0, 0)
            with act.Fori(0, H - 1) as hd:
                exp_head(hd, 0)
                exp_head(hd, 1)
            exp_head(H - 1, 0)
            exp_head(H - 1, 1, last=True)

            for t in range(NT):
                act.wait_ge(o_turned, t + 1)
                if t >= 2:
                    act.wait_ge(out_done, t - 1)
                act.copy(o_t[t % 2], bank[t % 2][:]).then_inc(o_t_ready, 1)

            act.wait_ge(fourier_loaded, FOURIER_LOADS * 16)
            spectrum(act.copy, act, 0, spec_ready_a)
            for i in range(3):
                act.wait_ge(pin_done, i + 1)
                act.activation(h_t[:, FCH * i:FCH * (i + 1)], bank[i][:, 0:FCH], ACT.Identity, bias=pin_b[:]).then_inc(h_t_ready, 1)
            act.wait_ge(gap_ready, 1)
            act.activation(odds[:], gap[:], ACT.Exp).then_inc(odds_ready, 1)
            for i in range(3):
                act.wait_ge(wsel_turned, i + 1)
                n = min(4, FT - 4 * i) * P
                act.copy(wsel_t[:, 4 * i * P:4 * i * P + n], bank[4 + i][0:E, 0:n]).then_inc(wsel_t_ready, 1)

            def hidden(layer, e, i, groups, width):
                for g in range(groups[0]):
                    act.wait_ge(hidden_done[layer], e * groups[0] + g + 1)
                    c, k = g % FC, g // FC
                    to = (hid_f if layer == 0 else hid_g)[i][:, c, width * k:width * (k + 1)]
                    bias = {"bias": b1[i][:, c:c + 1]} if layer == 0 else {}
                    act.activation(to, bank[g % 2][:, 0:width], ACT.Gelu, **bias).then_inc(hidden_ready[layer], 1)

            def hidden_layer(layer, groups, width):
                hidden(layer, 0, 0, groups, width)
                hidden(layer, 1, 1, groups, width)
                with act.Fori(0, E - 3, 2) as e:
                    for i in range(2):
                        act.wait_ge(expert_done[layer], (e + i) * groups[1] + groups[1])
                        hidden(layer, e + i + 2, i, groups, width)

            hidden_layer(0, (FC * 3, FT), FCH)
            for i in range(3):
                act.wait_ge(moe_turned, i + 1)
                n = min(4 * P, NF - 4 * i * P)
                act.copy(moe_t[:, 4 * i * P:4 * i * P + n], bank[i][:, 0:n]).then_inc(moe_t_ready, 1)
            for i in range(2):
                act.wait_ge(inv_done, i + 1)
                act.copy(comb[:, 2 * i:2 * i + 2], bank[4 + i].rearrange("p (o b d) -> p o b d", o=2, b=B)).then_inc(comb_ready_a, 1)

            features_down(2)
            features_down(3)
            for b in range(B):
                for c in range(2 * TB):
                    act.wait_ge(scores2_done, b * 2 * TB + c + 1)
                    act.activation(p_2[b][:, c % TB, HALF * (c // TB):HALF * (c // TB + 1)], bank[c % 2][:], ACT.Exp).then_inc(probs2_ready, 1)
            features_down(4)
            hidden_layer(1, (FC * 2, TB), HALF)

        @block.vector
        def _(dve):
            dve.wait_ge(ids_loaded, 5 * 16)
            dve.tensor_tensor(seen, frames_i.unsqueeze(1).broadcast_to([N_FFT, VOCAB, NFR]), vocab_row[:].unsqueeze(2).broadcast_to([N_FFT, VOCAB, NFR]), ALU.is_equal).then_inc(seen_ready, 1)
            dve.tensor_scalar(tok_sel[VOCAB_AT:SEL_K, :], ids_i, vocab_col[VOCAB_AT:SEL_K, :], None, ALU.is_equal).then_inc(sel_ready, 1)
            dve.wait_ge(squares, 4)
            dve.scalar_tensor_tensor(out=re_sq, in0=re_sq, scalar=1e-33, in1=im_sq, op0=ALU.max, op1=ALU.add).then_inc(power_ready, 1)
            dve.wait_ge(tok_loaded, 4 * 16)
            dve.wait_ge(enc_done, 1)
            dve.tensor_tensor(tok_tab[0:NFR, D_EMB:D], bank[4][0:NFR, 0:D_STFT], proj_b, ALU.add).then_inc(tab_ready, 1)

            def statistics(n, rows=h):
                b = n % B
                for t in range(b * TB, (b + 1) * TB):
                    dve.bn_stats(stats[:, t, :], rows[:, t, :]).then_inc(stats_done, 1)
                for i, t in enumerate(range(b * TB, (b + 1) * TB)):
                    dve.wait_ge(stats_done, TB * n + i + 1)
                    dve.bn_aggr(mv[:, t, :], stats[:, t, :]).then_inc(mean_done, 1)
                dve.wait_ge(mean_done, TB * (n + 1))
                tiles = slice(b * TB, (b + 1) * TB)
                dve.tensor_scalar(var_eps[:, tiles], mv[:, tiles, 1], LN_EPS, None, ALU.add).then_inc(var_ready, 1)

            def normalise(n, rows=h, to=ln, ready=ln_ready):
                b = n % B
                dve.wait_ge(rstd_ready, n + 1)
                for t in range(b * TB, (b + 1) * TB):
                    dve.tensor_scalar(to[:, t, :], rows[:, t, :], mv[:, t, 0:1], rstd[:, t:t + 1], ALU.subtract, ALU.mult).then_inc(ready, 1)

            dve.wait_ge(h_ready, 2)
            statistics(0)
            dve.wait_ge(h_ready, 4)
            statistics(1)
            normalise(0)
            normalise(1)

            dve.wait_ge(attn_loaded, 6 * 16)
            dve.tensor_copy(mask_b[:], mask_f).then_inc(consts_b, 1)
            dve.tensor_copy(ident_b[:], ident[:]).then_inc(consts_b, 1)
            for t in range(NT):
                dve.wait_ge(v_done, t + 1)
                dve.tensor_tensor(v_all[:, t, :], bank[t % 4][:], b_v, ALU.add).then_inc(v_ready, 1)

            def keys(hd, b):
                n = hd * B + b
                for c in range(2):
                    dve.wait_ge(k_done, n * 2 + c + 1)
                    dve.tensor_scalar(k_t[b][0:QK, HALF * c:HALF * (c + 1)], pj[c][0:QK, :], b_head[:, 1:2], None, ALU.add).then_inc(k_ready, 1)

            def maxima(hd, b):
                n = hd * B + b
                for m, (j, c, width) in enumerate(m_chunks):
                    dve.wait_ge(rows_done, n * NM + m + 1)
                    if j < 4:
                        to = max_pad[:, j, DK:QK]
                    else:
                        to = max_part[:, 2 * (j - 4) + c:2 * (j - 4) + c + 1]
                    dve.tensor_reduce(to, sm[m % 2][:, 0:width], AX.X, ALU.max, negate=True).then_inc(rows_used, 1)
                dve.wait_ge(rows_used, n * NM + NM)
                pairs = max_part[:].rearrange("p (j c) -> p j c", c=2)
                dve.tensor_tensor(max_pad[:, 4:TB, DK:QK], pairs[:, :, 0:1], pairs[:, :, 1:2], ALU.min).then_inc(max_ready, 1)

            def max_rows(hd, b):
                n = hd * B + b
                for c in range(2):
                    dve.wait_ge(max_turned, n * 2 + c + 1)
                    dve.tensor_copy(q_t[b][DK:QK, HALF * c:HALF * (c + 1)], pj[c][DK:QK, :]).then_inc(max_row_ready, 1)

            def divide(hd, b, half):
                n = hd * B + b
                dve.wait_ge(pv_done[half], n + 2)
                got = pv[half][:, 0:4 * VW].rearrange("p (t w) -> p t w", w=VW)
                scale = o_scale[:, 4 * half:4 * half + 4].unsqueeze(2)
                dve.reciprocal(scale, got[:, :, DK:QK]).then_inc(den_ready[half], 1)
                dve.wait_ge(den_ready[half], n + 1)
                to = o_all[:, b * TB + 4 * half:b * TB + 4 * half + 4, bass.ds(hd * DK, DK)]
                dve.tensor_tensor(to, got[:, :, 0:DK], scale.broadcast_to([P, 4, DK]), ALU.mult).then_inc(o_ready[half], 1)

            def vector_head(hd, b, last=False):
                if not last:
                    keys(hd + b, 1 - b)
                divide(hd, b, 0)
                if not last:
                    maxima(hd + b, 1 - b)
                    max_rows(hd + b, 1 - b)
                divide(hd, b, 1)

            for half in range(2):
                dve.memset(o_scale[:, 4 * half:4 * half + 4], 1.0).then_inc(o_ready[half], 1)
            dve.wait_ge(pool_const, POOL_CONSTS)
            keys(0, 0)
            maxima(0, 0)
            max_rows(0, 0)
            with dve.Fori(0, H - 1) as hd:
                vector_head(hd, 0)
                vector_head(hd, 1)
            vector_head(H - 1, 0)
            vector_head(H - 1, 1, last=True)

            dve.wait_ge(base_ready, 2)
            for i in range(4):
                dve.wait_ge(out_done, 4 * i + 4)
                dve.tensor_tensor(h[:, 4 * i:4 * i + 4, :], bank[4 + i].rearrange("p (t d) -> p t d", d=D), base[:, 4 * i:4 * i + 4, :], ALU.add).then_inc(h_ready, 1)
            dve.wait_ge(h_ready, 6)
            statistics(2)
            dve.wait_ge(h_ready, 8)
            statistics(3)
            normalise(2)
            normalise(3)

            dve.wait_ge(ln_ready, 2 * NT)
            x8 = ln[:].rearrange("p (b j) d -> p b j d", b=B)
            dve.tensor_tensor(sum4, x8[:, :, 0:4], x8[:, :, 4:8], ALU.add).then_inc(fold1, 1)
            dve.tensor_tensor(dif4, x8[:, :, 0:4], x8[:, :, 4:8], ALU.subtract).then_inc(fold1, 1)
            dve.wait_ge(fold1, 2)
            dve.tensor_tensor(ev2, sum4[:, :, 0:2], sum4[:, :, 2:4], ALU.add).then_inc(fold2, 1)
            dve.tensor_tensor(od2, sum4[:, :, 0:2], sum4[:, :, 2:4], ALU.subtract).then_inc(fold2, 1)
            dve.tensor_tensor(dd, dif4[:, :, 1], dif4[:, :, 3], ALU.subtract).then_inc(fold2, 1)
            dve.tensor_tensor(gg, dif4[:, :, 1], dif4[:, :, 3], ALU.add).then_inc(fold2, 1)
            dve.wait_ge(fold2, 4)
            dve.tensor_tensor(y[:, 0], ev2[:, :, 0], ev2[:, :, 1], ALU.add).then_inc(y_ready, 1)
            dve.tensor_tensor(y[:, 1], ev2[:, :, 0], ev2[:, :, 1], ALU.subtract).then_inc(y_ready, 1)
            for i, (pair, sign, rest) in enumerate(((dd, C8, 0), (dd, -C8, 0), (gg, C8, 2), (gg, -C8, 2))):
                dve.scalar_tensor_tensor(out=y[:, 2 + i], in0=pair, scalar=sign, in1=dif4[:, :, rest], op0=ALU.mult, op1=ALU.add).then_inc(y_ready, 1)
            spectrum(dve.tensor_copy, dve, 1, spec_ready_v)

            dve.wait_ge(fourier_loaded, FOURIER_LOADS * 16)
            dve.wait_ge(router_done, 1)
            dve.tensor_tensor(logits[:], bank[3][:, 0:FT * E].rearrange("p (t e) -> p t e", e=E), router_b[:].unsqueeze(1).broadcast_to([P, FT, E]), ALU.add).then_inc(logits_ready, 1)
            dve.wait_ge(logits_ready, 1)
            for t in range(FT):
                dve.max(top8[:, t, :], logits[:, t, :]).then_inc(top_ready, 1)
            dve.wait_ge(top_ready, FT)
            dve.tensor_tensor(gap[:], top8[:, :, 1:2], top8[:, :, 0:1], ALU.subtract).then_inc(gap_ready, 1)
            for t in range(FT):
                dve.max_index(idx8[:, t, :], top8[:, t, :], logits[:, t, :]).then_inc(idx_ready, 1)
            dve.wait_ge(idx_ready, FT)
            dve.tensor_copy(choice[:], idx8[:, :, 0:2]).then_inc(route, 1)
            dve.wait_ge(odds_ready, 1)
            dve.tensor_scalar(odds1[:], odds[:], 1.0, None, ALU.add).then_inc(route, 1)
            dve.wait_ge(route, 2)
            dve.reciprocal(share[:, :, 0:1], odds1[:]).then_inc(route, 1)
            dve.wait_ge(route, 3)
            dve.tensor_tensor(share[:, :, 1:2], odds[:], share[:, :, 0:1], ALU.mult).then_inc(route, 1)
            dve.wait_ge(route, 4)

            def weights_of(chosen, shares, nt, to, sig, first, ready):
                numbers = expert_no[:].unsqueeze(1).broadcast_to([P, nt, E])
                for k in range(2):
                    dve.tensor_tensor(pick[k][:, 0:nt], numbers, chosen[:, :, k:k + 1].broadcast_to([P, nt, E]), ALU.is_equal).then_inc(sig, 1)
                for k in range(2):
                    dve.wait_ge(sig, first + k + 1)
                    dve.tensor_tensor(pick[k][:, 0:nt], pick[k][:, 0:nt], shares[:, :, k:k + 1].broadcast_to([P, nt, E]), ALU.mult).then_inc(sig, 1)
                dve.wait_ge(sig, first + 4)
                dve.tensor_tensor(to[:], pick[0][:, 0:nt], pick[1][:, 0:nt], ALU.add).then_inc(ready, 1)

            weights_of(choice[:], share[:], FT, wsel_f, route, 4, wsel_ready)
            for t in range(FT):
                dve.wait_ge(bias_done, t + 1)
                dve.tensor_copy(acc_f[:, t, :], bank[t % 2][:, 0:D]).then_inc(acc_ready[0], 1)

            def accumulate(layer, e, nt, acc, wsel):
                for t in range(nt):
                    rows = 2 if layer == 0 and t == FT - 1 else P
                    dve.wait_ge(acc_ready[layer], e * nt + t + 1)
                    dve.wait_ge(expert_done[layer], e * nt + t + 1)
                    dve.scalar_tensor_tensor(out=acc[0:rows, t, :], in0=bank[2 + t % RING[layer]][0:rows, 0:D], scalar=wsel[0:rows, t, bass.ds(e, 1)], in1=acc[0:rows, t, :], op0=ALU.mult, op1=ALU.add).then_inc(acc_ready[layer], 1)

            dve.wait_ge(wsel_ready, 1)
            with dve.Fori(0, E) as e:
                accumulate(0, e, FT, acc_f, wsel_f)

            for i in range(4):
                dve.wait_ge(of_done, i + 1)
                for k in range(2):
                    which = 0 if i == 0 and k == 0 else 1
                    dve.tensor_tensor(of[:, 2 * i + k], bank[i][:, 256 * k:256 * (k + 1)].rearrange("p (b d) -> p b d", b=B), pout_b[:, which, :].unsqueeze(1).broadcast_to([P, B, D]), ALU.add).then_inc(of_ready, 1)
            for i in range(2, 4):
                dve.wait_ge(inv_done, i + 1)
                dve.tensor_copy(comb[:, 2 * i:2 * i + 2], bank[4 + i].rearrange("p (o b d) -> p o b d", o=2, b=B)).then_inc(comb_ready_v, 1)
            dve.wait_ge(comb_ready_a, 2)
            dve.wait_ge(comb_ready_v, 2)
            a0, a4, a1, b1_, a2, b2_, a3, b3_ = (comb[:, i] for i in range(8))
            for i, (u, v, op) in enumerate(((a0, a4, ALU.add), (a0, a4, ALU.subtract), (a1, a3, ALU.add), (b3_, b1_, ALU.subtract), (a1, a3, ALU.subtract), (b1_, b3_, ALU.add))):
                dve.tensor_tensor(inv[:, i], u, v, op).then_inc(unfold1, 1)
            dve.wait_ge(unfold1, 6)
            p0, m0, d0, d2, u0, v0 = (inv[:, i] for i in range(6))
            for i, (u, v, op) in enumerate(((p0, a2, ALU.add), (m0, b2_, ALU.subtract), (p0, a2, ALU.subtract), (m0, b2_, ALU.add), (u0, v0, ALU.subtract), (u0, v0, ALU.add))):
                dve.tensor_tensor(inv[:, 6 + i], u, v, op).then_inc(unfold2, 1)
            dve.wait_ge(unfold2, 6)
            e0, e1, e2, e3, d1, d3 = (inv[:, i] for i in range(6, 12))
            o8 = ot.rearrange("p (b j) d -> p b j d", b=B)
            for j, (even, odd, scale) in enumerate(((e0, d0, 1.0), (e1, d1, C8), (e2, d2, 1.0), (e3, d3, -C8))):
                dve.scalar_tensor_tensor(out=o8[:, :, j], in0=odd, scalar=scale, in1=even, op0=ALU.mult, op1=ALU.add).then_inc(ot_ready, 1)
                dve.scalar_tensor_tensor(out=o8[:, :, j + 4], in0=odd, scalar=-scale, in1=even, op0=ALU.mult, op1=ALU.add).then_inc(ot_ready, 1)
            dve.wait_ge(ot_ready, 8)
            statistics(4, ot)
            statistics(5, ot)
            normalise(4, ot, ot, ot_norm)
            normalise(5, ot, ot, ot_norm)
            dve.wait_ge(ot_norm, NT)
            dve.tensor_tensor(ot, ot, ln_g[:].unsqueeze(1).broadcast_to([P, NT, D]), ALU.mult).then_inc(ot_scaled, 1)
            dve.wait_ge(ot_scaled, 1)
            dve.wait_ge(base_f_ready, 2)
            dve.tensor_tensor(h[:], ot, base[:], ALU.add).then_inc(h2_ready, 1)

            dve.wait_ge(h2_ready, 1)
            statistics(6)
            statistics(7)
            normalise(6)
            normalise(7)
            for b in range(B):
                for m in range(2 * TB):
                    dve.wait_ge(rows2_done, b * 2 * TB + m + 1)
                    dve.tensor_reduce(max2[:, m // 2, m % 2:m % 2 + 1], bank[2 + m % 2][:], AX.X, ALU.max, negate=True).then_inc(rows2_used, 1)
                dve.wait_ge(rows2_used, (b + 1) * 2 * TB)
                dve.tensor_tensor(neg_max[:], max2[:, :, 0:1], max2[:, :, 1:2], ALU.min).then_inc(neg_max_ready, 1)
                for c in range(2):
                    dve.wait_ge(max2_turned, 2 * b + c + 1)
                    dve.tensor_copy(neg_row[0:1, HALF * c:HALF * (c + 1)], bank[6 + c][0:1, :]).then_inc(neg_row_ready, 1)
                for j in range(TB):
                    t = b * TB + j
                    dve.wait_ge(pv2_done, t + 1)
                    dve.reciprocal(den2[:, t:t + 1], bank[4 + j % 2][:, D:D + 1]).then_inc(den2_ready, 1)
                    dve.wait_ge(den2_ready, t + 1)
                    dve.scalar_tensor_tensor(out=h[:, t, :], in0=bank[4 + j % 2][:, 0:D], scalar=den2[:, t:t + 1], in1=h[:, t, :], op0=ALU.mult, op1=ALU.add).then_inc(h3_ready, 1)

            dve.wait_ge(h3_ready, NT)
            statistics(8)
            normalise(8)
            dve.tensor_copy(gate_no[:], gate_i[:]).then_inc(gates, 1)
            dve.wait_ge(gates, 1)
            weights_of(gate_no[:], gate_w[:], TB, wsel_g, gates, 1, wsel_ready)
            for t in range(TB):
                dve.tensor_copy(acc_g[:, t, :], h[:, t, :]).then_inc(acc_ready[1], 1)
            dve.wait_ge(wsel_ready, 2)
            with dve.Fori(0, E) as e:
                accumulate(1, e, TB, acc_g, wsel_g)

        @block.tensor
        def _(pe):
            pe.wait_ge(seen_ready, 1)
            for i in range(4):
                half = i % 2
                pe.matmul(bank[i][0:N_FREQ, 0:272], dft64[:, i // 2, :], seen[:, 8 * half:8 * half + 8, :], start=True, stop=True).then_inc(dft_done, 1)
            pe.wait_ge(mag_ready, 1)
            pe.wait_ge(tok_loaded, 4 * 16)
            for v in range(VOCAB):
                mm = pe.matmul(bank[4][0:NFR, 0:D_STFT], mag[:, v, :], proj_w[:, v, :], start=(v == 0), stop=(v == VOCAB - 1))
            mm.then_inc(enc_done, 1)
            pe.wait_ge(tab_ready, 1)
            pe.wait_ge(sel_ready, 1)
            for t in range(NT):
                mm = pe.matmul(bank[t // 4][:, D * (t % 4):D * (t % 4 + 1)], tok_sel[:, P * t:P * (t + 1)], tok_tab, start=True, stop=True)
                if t % 4 == 3:
                    mm.then_inc(tok_done, 1)

            def turn_rows(n, batch):
                for i in range(2):
                    if n >= 1:
                        pe.wait_ge(ln_t_ready, 2 * n + i - 1)
                    for k in range(4):
                        t = (n % B) * TB + 4 * i + k
                        pe.wait_ge(ln_ready, TB * batch + 4 * i + k + 1)
                        mm = pe.transpose(bank[4 + i][:, P * k:P * (k + 1)], ln[:, t, :], ident[:])
                    mm.then_inc(turned, 1)

            pe.wait_ge(attn_loaded, 6 * 16)
            turn_rows(0, 0)
            turn_rows(1, 1)
            pe.wait_ge(h_ready, 4)
            for t in range(NT):
                pe.wait_ge(ln_t_ready, t // 4 + 1)
                if t >= 4:
                    pe.wait_ge(v_ready, t - 3)
                pe.matmul(bank[t % 4][:], ln_t[:, P * t:P * (t + 1)], w_v, start=True, stop=True).then_inc(v_done, 1)

            def project_q(hd, b, first=False):
                n = hd * B + b
                for c in range(2):
                    if not first:
                        pe.wait_ge(max_row_ready, n * 2 + c - 1)
                    pe.matmul(pj[c][0:QK, :], w_head[:, 0:QK], ln_t[:, b * L + HALF * c:b * L + HALF * (c + 1)], start=True, stop=True).then_inc(q_done, 1)

            def project_k(hd, b, c):
                n = hd * B + b
                pe.wait_ge(q_ready, n * 2 + c + 1)
                pe.matmul(pj[c][0:QK, :], w_head[:, QK:2 * QK], ln_t[:, b * L + HALF * c:b * L + HALF * (c + 1)], start=True, stop=True).then_inc(k_done, 1)

            def score_rows(hd, b, m, first=False):
                n = hd * B + b
                j, c, width = m_chunks[m]
                if m == 0:
                    pe.wait_ge(k_ready, n * 2 + 2)
                if m >= 2 or not first:
                    pe.wait_ge(rows_used, n * NM + m - 1)
                to = sm[m % 2]
                on_diag = P * j < HALF * c + width and P * j >= HALF * c
                mm = pe.matmul(to[:, 0:width], q_t[b][:, P * j:P * (j + 1)], k_t[b][:, HALF * c:HALF * c + width], start=True, stop=not on_diag)
                if on_diag:
                    mm = pe.matmul(to[:, width - P:width], ident_b[:], mask_b[:], start=False, stop=True)
                mm.then_inc(rows_done, 1)

            def turn_maxima(hd, b, c, first=False):
                n = hd * B + b
                pe.wait_ge(max_ready, n + 1)
                for k in range(4):
                    mm = pe.transpose(pj[c][0:QK, P * k:P * (k + 1)], max_pad[:, 4 * c + k, :], ident[:])
                    if first and k == 0:
                        mm.then_inc(pv_done[c], 1)
                mm.then_inc(max_turned, 1)

            def scores(hd, b, c):
                n = hd * B + b
                half, i, first, width = s_chunks[c]
                if c == 0 or s_chunks[c - 1][0] != half:
                    pe.wait_ge(max_row_ready, n * 2 + half + 1)
                if c >= 2:
                    pe.wait_ge(probs_ready, n * NS + c - 1)
                mm = pe.matmul(st[c % 2][:, 0:width], k_t[b][:, P * i:P * (i + 1)], q_t[b][:, first:first + width], start=True, stop=first != P * i)
                if first == P * i:
                    mm = pe.matmul(st[c % 2][:, 0:P], mask_b[:], ident_b[:], start=False, stop=True)
                mm.then_inc(scores_done, 1)

            def weigh(hd, b, j):
                n = hd * B + b
                half = j // 4
                if j == 0:
                    pe.wait_ge(v_head_ready, n + 1)
                if j % 4 == 0:
                    pe.wait_ge(o_ready[half], n + 1)
                c = chunk_of[half, j]
                pe.wait_ge(probs_ready, n * NS + c + 1)
                for i in range(j + 1):
                    c = chunk_of[half, i]
                    at = s_first[c] + P * j - s_chunks[c][2]
                    mm = pe.matmul(pv[half][:, VW * (j % 4):VW * (j % 4 + 1)], p_t[:, at:at + P], v_head[b][:, i, :], start=(i == 0), stop=(i == j))
                if j % 4 == 3:
                    mm.then_inc(pv_done[half], 1)

            def tensor_head(hd, b, last=False):
                nh, nb = hd + b, 1 - b
                if not last:
                    if b == 1:
                        pe.wait_ge(w_head_loaded, nh * 32 + 32)
                    project_q(nh, nb)
                scores(hd, b, 0)
                scores(hd, b, 1)
                if not last:
                    project_k(nh, nb, 0)
                scores(hd, b, 2)
                if not last:
                    project_k(nh, nb, 1)
                scores(hd, b, 3)
                scores(hd, b, 4)
                weigh(hd, b, 0)
                weigh(hd, b, 1)
                scores(hd, b, 5)
                weigh(hd, b, 2)
                scores(hd, b, 6)
                weigh(hd, b, 3)
                rows = 0
                for c in range(7, NS):
                    scores(hd, b, c)
                    share = 3 if c < 9 else 2
                    if not last:
                        for m in range(rows, rows + share):
                            score_rows(nh, nb, m)
                    rows += share
                weigh(hd, b, 4)
                weigh(hd, b, 5)
                if not last:
                    turn_maxima(nh, nb, 0)
                weigh(hd, b, 6)
                if not last:
                    turn_maxima(nh, nb, 1)
                weigh(hd, b, 7)

            pe.wait_ge(w_head_loaded, 32)
            pe.wait_ge(v_ready, NT)
            pe.wait_ge(pool_const, POOL_CONSTS)
            pe.wait_ge(consts_b, 2)
            project_q(0, 0, first=True)
            for c in range(2):
                project_k(0, 0, c)
            for m in range(NM):
                score_rows(0, 0, m, first=True)
            for c in range(2):
                turn_maxima(0, 0, c, first=True)
            with pe.Fori(0, H - 1) as hd:
                tensor_head(hd, 0)
                tensor_head(hd, 1)
            tensor_head(H - 1, 0)
            tensor_head(H - 1, 1, last=True)

            def turn_heads(t):
                pe.wait_ge(o_ready[(t % TB) // 4], (H - 1) * B + t // TB + 2)
                if t >= 2:
                    pe.wait_ge(o_t_ready, t - 1)
                for k in range(4):
                    mm = pe.transpose(bank[t % 2][:, P * k:P * (k + 1)], o_all[:, t, P * k:P * (k + 1)], ident[:])
                mm.then_inc(o_turned, 1)

            turn_heads(0)
            for t in range(NT):
                if t + 1 < NT:
                    turn_heads(t + 1)
                pe.wait_ge(o_t_ready, t + 1)
                for k in range(4):
                    mm = pe.matmul(bank[4 + t // 4][:, D * (t % 4):D * (t % 4 + 1)], o_t[t % 2][:, P * k:P * (k + 1)], w_out[:, k, :], start=(k == 0), stop=(k == 3))
                mm.then_inc(out_done, 1)


            pe.wait_ge(h_ready, 8)
            pe.wait_ge(fourier_loaded, FOURIER_LOADS * 16)
            pe.wait_ge(y_ready, 6)
            for b in range(B):
                pe.matmul(bank[4 * b][:, 0:130], y[:, 0, b, :], fwd_single[:, 0:130], start=True, stop=True)
                pe.matmul(bank[4 * b][:, 256:384], y[:, 1, b, :], fwd_single[:, 130:258], start=True, stop=True).then_inc(spec_done, 1)
                for r, (re, im) in enumerate(((y[:, 2, b], y[:, 4, b]), (od2[:, b, 0], od2[:, b, 1]), (y[:, 3, b], y[:, 5, b]))):
                    pe.matmul(bank[4 * b + 1 + r][:, 0:256], re, fwd_pair[:, 2 * r, :], start=True, stop=False)
                    pe.matmul(bank[4 * b + 1 + r][:, 0:256], im, fwd_pair[:, 2 * r + 1, :], start=False, stop=True).then_inc(spec_done, 1)
            pe.wait_ge(spec_ready_a, 6)
            pe.wait_ge(spec_ready_v, 6)
            for i in range(3):
                cols = slice(FCH * i, FCH * (i + 1))
                pe.matmul(bank[i][:, 0:FCH], pin_w[:, 0, :], xf[:, 0, cols], start=True, stop=False)
                pe.matmul(bank[i][:, 0:FCH], pin_w[:, 1, :], xf[:, 1, cols], start=False, stop=True).then_inc(pin_done, 1)
            pe.wait_ge(h_t_ready, 3)
            pe.wait_ge(pad_cleared, 3)
            for t in range(FT):
                mm = pe.matmul(bank[3][:, E * t:E * (t + 1)], h_t[:, P * t:P * (t + 1)], router_w[:], start=True, stop=True)
            mm.then_inc(router_done, 1)
            pe.wait_ge(wsel_ready, 1)
            for t in range(FT):
                mm = pe.transpose(bank[4 + t // 4][0:E, P * (t % 4):P * (t % 4 + 1)], wsel_f[:, t, :], ident[:])
                if t % 4 == 3 or t == FT - 1:
                    mm.then_inc(wsel_turned, 1)
            pe.wait_ge(wsel_t_ready, 3)
            for t in range(FT):
                if t >= 2:
                    pe.wait_ge(acc_ready[0], t - 1)
                pe.matmul(bank[t % 2][:, 0:D], wsel_t[:, P * t:P * (t + 1)], b2[:], start=True, stop=True).then_inc(bias_done, 1)
            pe.wait_ge(acc_ready[0], FT)

            def up(layer, e, i, g, ng, width, x_t, first=False):
                c, k = g % FC, g // FC
                if g == 0:
                    pe.wait_ge(experts_loaded[layer][i], e * (LOADS[layer] // 2) + (2 - i) * (LOADS[layer] // 2))
                if g >= 2 or not first:
                    pe.wait_ge(hidden_ready[layer], e * ng + g - 1)
                pe.matmul(bank[g % 2][:, 0:width], w1[i][:, P * c:P * (c + 1)], x_t[:, width * k:width * (k + 1)], start=True, stop=True).then_inc(hidden_done[layer], 1)

            def down(layer, e, i, t, ng, nt):
                if t == 0:
                    pe.wait_ge(hidden_ready[layer], e * ng + ng)
                pe.wait_ge(acc_ready[layer], e * nt + nt + t + 1 - RING[layer])
                hid = (hid_f if layer == 0 else hid_g)[i]
                rows = 2 if layer == 0 and t == FT - 1 else P
                for c in range(FC):
                    mm = pe.matmul(bank[2 + t % RING[layer]][0:rows, 0:D], hid[:, c, P * t:P * t + rows], w2[i][:, c, :], start=(c == 0), stop=(c == FC - 1))
                mm.then_inc(expert_done[layer], 1)

            def experts(layer, ng, nt, width, x_t):
                def step(e, i, last=False):
                    for g in range(max(ng, nt)):
                        if g < ng and not last:
                            up(layer, e + 1, 1 - i, g, ng, width, x_t)
                        if g < nt:
                            down(layer, e, i, g, ng, nt)

                for g in range(ng):
                    up(layer, 0, 0, g, ng, width, x_t, first=True)
                with pe.Fori(0, E - 3, 2) as e:
                    step(e, 0)
                    step(e + 1, 1)
                step(E - 2, 0)
                step(E - 1, 1, last=True)

            experts(0, FC * 3, FT, FCH, h_t)

            pe.wait_ge(acc_ready[0], FT * (E + 1))
            for t in range(FT):
                rows = 2 if t == FT - 1 else P
                mm = pe.transpose(bank[t // 4][:, P * (t % 4):P * (t % 4) + rows], acc_f[0:rows, t, :], ident[0:rows, 0:rows])
                if t % 4 == 3 or t == FT - 1:
                    mm.then_inc(moe_turned, 1)
            pe.wait_ge(moe_t_ready, 3)
            for r in range(RES):
                for b in range(B):
                    at = (r % 2) * B * D + b * D
                    rows = moe_t[:, (b * RES + r) * M64:(b * RES + r + 1) * M64]
                    pe.matmul(bank[r // 2][0:M64, at:at + D], rows, pout_w[:, 0, :], start=True, stop=True)
                    mm = pe.matmul(bank[r // 2][M64:P, at:at + D], rows, pout_w[:, 1, :], start=True, stop=True)
                    if r == 0:
                        mm = pe.matmul(bank[0][M64:M64 + 1, at:at + D], moe_t[:, NYQ + b:NYQ + b + 1], pout_w[:, 0, :], start=True, stop=True)
                if r % 2:
                    mm.then_inc(of_done, 1)

            pe.wait_ge(of_ready, 8)
            plan = [[(0, 0)], [(1, 4)]] + [[(2 + 4 * (r - 1) + 2 * k + s, (r, 8 - r)[s]) for s in range(2)] for r in range(1, 4) for k in range(2)]
            for o, terms in enumerate(plan):
                for n, (table, r) in enumerate(terms):
                    mm = pe.matmul(bank[4 + o // 2][:, 256 * (o % 2):256 * (o % 2 + 1)], inverse[:, table, :], of[:, r], start=(n == 0), stop=(n == len(terms) - 1))
                if o % 2:
                    mm.then_inc(inv_done, 1)

            pe.wait_ge(comb_ready_a, 2)
            pe.wait_ge(comb_ready_v, 2)
            turn_rows(2, 4)
            turn_rows(3, 5)

            def score_rows2(b, m):
                if m >= 2 or b:
                    pe.wait_ge(rows2_used, b * 2 * TB + m - 1)
                first = b * L
                pe.matmul(bank[2 + m % 2][:], ln_t[:, first + P * (m // 2):first + P * (m // 2 + 1)], ln_t[:, first + HALF * (m % 2):first + HALF * (m % 2 + 1)], start=True, stop=True).then_inc(rows2_done, 1)

            def turn_maxima2(b):
                pe.wait_ge(neg_max_ready, b + 1)
                for c in range(2):
                    for k in range(4):
                        mm = pe.transpose(bank[6 + c][0:1, P * k:P * (k + 1)], neg_max[:, 4 * c + k, :], ident[:])
                    mm.then_inc(max2_turned, 1)

            def scores2(b, c):
                half, i = c // TB, c % TB
                pe.wait_ge(neg_row_ready, 2 * b + half + 1)
                if c >= 2 or b:
                    pe.wait_ge(probs2_ready, b * 2 * TB + c - 1)
                first = b * L
                pe.matmul(bank[c % 2][:], ln_t[:, first + P * i:first + P * (i + 1)], ln_t[:, first + HALF * half:first + HALF * (half + 1)], start=True, stop=False)
                pe.matmul(bank[c % 2][:], ones_b[:], neg_row[:, HALF * half:HALF * (half + 1)], start=False, stop=True).then_inc(scores2_done, 1)

            def weigh2(b, j):
                t = b * TB + j
                pe.wait_ge(probs2_ready, b * 2 * TB + TB * (j // 4 + 1))
                pe.wait_ge(z_ready, 2 * (b + 1))
                if j >= 2 or b:
                    pe.wait_ge(h3_ready, t - 1)
                for i in range(TB):
                    mm = pe.matmul(bank[4 + j % 2][:, 0:D + 1], p_2[b][:, i, P * j:P * (j + 1)], z_one[:, b * TB + i, 0:D + 1], start=(i == 0), stop=(i == TB - 1))
                mm.then_inc(pv2_done, 1)

            pe.wait_ge(ln_t_ready, 8)
            for b in range(B):
                for m in range(2 * TB):
                    score_rows2(b, m)
                turn_maxima2(b)
                for c in range(2 * TB):
                    scores2(b, c)
                for j in range(TB):
                    weigh2(b, j)

            pe.wait_ge(h3_ready, NT)
            turn_rows(4, 6)
            pe.wait_ge(ln_t_ready, 10)
            pe.wait_ge(acc_ready[1], TB)
            experts(1, FC * 2, TB, HALF, ln_t)


def frame_tables():
    w = np.arange(N_FFT)
    window = 0.5 - 0.5 * np.cos(2 * np.pi * w / N_FFT)
    angle = 2 * np.pi * np.outer(w, np.arange(N_FREQ)) / N_FFT
    return np.stack([window[:, None] * np.cos(angle), window[:, None] * -np.sin(angle)], 1).astype(np.float32)


def fourier_tables():
    p = np.arange(P)
    m = np.arange(M64)
    angle = lambda k: 2 * np.pi * np.outer(p, k) / L
    cos = lambda r: np.cos(angle(RES * m + r))
    sin = lambda r: np.sin(angle(RES * m + r))
    norm = 1 / np.sqrt(L)
    nyq = np.stack([(-1.0) ** p, 0 * p], 1)
    single = np.concatenate([cos(0), -sin(0), nyq, cos(4), -sin(4)], 1)
    pair = []
    for r in range(1, 4):
        q = RES - r
        s = 1.0 if r == 3 else -1.0
        pair.append(np.concatenate([cos(r), -sin(r), cos(q), -sin(q)], 1))
        pair.append(s * np.concatenate([sin(r), cos(r), -sin(q), -cos(q)], 1))
    weight = lambda r: np.where((m == 0) & (r == 0), 1.0, 2.0)

    def part_a(r):
        top, low = weight(r) * cos(r), -weight(r) * sin(r)
        if r == 0:
            low[:, 0] = nyq[:, 0]
        return np.concatenate([top, low], 1).T

    def part_b(r, sign):
        return sign * np.concatenate([weight(r) * sin(r), weight(r) * cos(r)], 1).T

    inv = [part_a(0), part_a(4)]
    for r in range(1, 4):
        inv += [part_a(r), part_a(RES - r), part_b(r, 1.0), part_b(RES - r, -1.0)]
    f = lambda v: np.ascontiguousarray(norm * v).astype(np.float32)
    return f(single), f(np.stack(pair, 1)), f(np.stack(inv, 1))


def constants():
    sel = np.zeros((NFR, B * L), np.float32)
    for b in range(B):
        l = np.arange(L)
        sel[b * N_FRAMES + l * N_FRAMES // L, b * L + l] = 1
    single, pair, inv = fourier_tables()
    return {
        "fwd_single": single, "fwd_pair": pair, "inverse": inv,
        "expert_no": np.tile(np.arange(E, dtype=np.float32), (P, 1)),
        "vocab_row": np.tile(np.arange(VOCAB, dtype=np.float32), (N_FFT, 1)),
        "vocab_col": (np.arange(P, dtype=np.float32) - VOCAB_AT)[:, None].copy(),
        "dft64": frame_tables(),
        "upsample": sel,
        "ident": np.eye(P, dtype=np.float32),
        "mask": np.triu(np.full((P, P), NEG, np.float32), 1),
    }


def layouts(x):
    c = np.ascontiguousarray
    ids = np.asarray(x["x"])
    pad = N_FFT // 2
    padded = np.pad(ids, ((0, 0), (pad, pad)), mode="reflect")
    frames = np.stack([padded[b, N_FFT * f:N_FFT * (f + 1)] for b in range(B) for f in range(N_FRAMES)], 1)
    w_in = np.asarray(x["L0_attn_W_in"]).reshape(D, H, 3, DK)
    w_qk = np.zeros((H, P, 2 * QK), w_in.dtype)
    b_in = np.asarray(x["L0_attn_b_in"]).reshape(H, 3, DK)
    b_qk = np.zeros((H, QK, 2), b_in.dtype)
    b_qk[:, DK, 1] = 1.0
    for part in range(2):
        w_qk[:, :, QK * part:QK * part + DK] = w_in[:, :, part, :].transpose(1, 0, 2)
        b_qk[:, :DK, part] = b_in[:, part, :]
    rows = lambda v: np.tile(np.asarray(v).reshape(1, -1), (P, 1))
    real, imag = np.asarray(x["L0_ffn_pout_b"]).reshape(2, D)
    pout_b = np.stack([np.stack([real] * (M64 + 1) + [imag] * (M64 - 1)), np.stack([real] * M64 + [imag] * M64)], 1)
    return {
        "ids_frames": c(frames),
        "ids_bcast": np.tile(ids.reshape(1, -1), (VOCAB, 1)),
        "proj_w": x["L0_tok_proj_w"],
        "proj_b": rows(x["L0_tok_proj_b"])[:NFR],
        "emb_table": x["L0_tok_emb_table"],
        "w_qk": w_qk, "b_qk": b_qk,
        "w_v": c(w_in[:, :, 2, :].reshape(D, H * DK)),
        "b_v": rows(b_in[:, 2, :]),
        "w_out": x["L0_attn_W_out"],
        "b_out": rows(x["L0_attn_b_out"]),
        "pin_w": x["L0_ffn_pin_w"], "pin_b": np.asarray(x["L0_ffn_pin_b"]).reshape(P, 1),
        "router_w": x["L0_ffn_router_w"], "router_b": rows(x["L0_ffn_router_b"]),
        "w1_f": x["L0_ffn_w1"], "w2_f": x["L0_ffn_w2"], "b2": x["L0_ffn_b2"],
        "b1_f": c(np.asarray(x["L0_ffn_b1"]).reshape(E, FC, P).transpose(0, 2, 1)),
        "pout_w": x["L0_ffn_pout_w"], "pout_b": pout_b,
        "ln_g": rows(x["L0_ffn_ln_g"]), "ln_b": rows(x["L0_ffn_ln_b"]),
        "gate_w": c(np.asarray(x["L1_ffn_expert_weights"]).reshape(TB, P, 2).transpose(1, 0, 2)),
        "gate_i": c(np.asarray(x["L1_ffn_expert_indices"]).reshape(TB, P, 2).transpose(1, 0, 2)),
        "w1_g": x["L1_ffn_w1"], "w2_g": x["L1_ffn_w2"],
    }


def kernel(**inputs):
    import concourse.bacc as bacc
    from concourse.bass_utils import run_bass_kernel_spmd

    nc = bacc.Bacc("TRN2", target_bir_lowering=False, num_devices=1)
    arrays = {k: np.ascontiguousarray(v) for k, v in (layouts(inputs) | constants()).items()}
    aps = {k: nc.dram_tensor("in_" + k, v.shape, mybir.dt.from_np(v.dtype), kind="ExternalInput").ap() for k, v in arrays.items()}
    out = nc.dram_tensor("hidden", (B * L, D), F32, kind="ExternalOutput").ap()
    tower(nc, aps, out)
    got = run_bass_kernel_spmd(nc, [{"in_" + k: v for k, v in arrays.items()}], core_ids=[0])
    return got.results[0]["hidden"].reshape(B, L, D)
```

```python
from contextlib import ExitStack

import numpy as np

import concourse.bass as bass
from concourse import mybir

P = 128
B, L, D = 2, 1024, 128
VOCAB, D_EMB, D_STFT = 16, 89, 39
N_FFT, N_FREQ, N_FRAMES = 64, 33, 17
NFR = B * N_FRAMES
H, DK = 8, 64
LN_EPS = 1e-5
TB = L // P
NT = B * TB
HALF = 512
SEL_K = 80
VOCAB_AT = 64
VW = 96
MAX_AT = 64
MAX_END = MAX_AT + TB
NEG = -1.0e9
E, FF = 8, 512
FC = FF // P
RES = 8
M64 = L // 2 // RES
NYQ = B * RES * M64
NF = NYQ + B
FT = 9
FCH = NF // 3
C8 = float(np.sqrt(0.5))
POOL_CONSTS = 12
KEYS_BEFORE = (4, 5)
FOURIER_LOADS = 15
TILES = (FT, TB)
COLS = (FCH, HALF)
GROUPS = (FC * 3, FC * 2)
RING = (3, 4)

F32 = mybir.dt.float32
F32R = mybir.dt.float32r
BF16 = mybir.dt.bfloat16
I32 = mybir.dt.int32
U32 = mybir.dt.uint32
ALU = mybir.AluOpType
ACT = mybir.ActivationFunctionType
AX = mybir.AxisListType


def max_chunks():
    return [(j, c, min(HALF, P * (j + 1) - HALF * c)) for j in range(TB) for c in range(2)
            if P * (j + 1) > HALF * c]


def score_chunks():
    out = []
    for half in range(2):
        for i in range(TB):
            first = max(P * i, HALF * half)
            if first < HALF * (half + 1):
                out.append((half, i, first, HALF * (half + 1) - first))
    return out


def tower(nc, a, out):
    m_chunks = max_chunks()
    s_chunks = score_chunks()
    NM, NS = len(m_chunks), len(s_chunks)
    s_first = [sum(c[3] for c in s_chunks[:n]) for n in range(NS + 1)]
    chunk_of = {(half, i): n for n, (half, i, _, _) in enumerate(s_chunks)}

    with ExitStack() as ctx:
        def sb(name, shape, dt=F32):
            return ctx.enter_context(nc.sbuf_tensor(name, shape, dt))

        def sem(name):
            return ctx.enter_context(nc.semaphore(name))

        bank = [ctx.enter_context(nc.psum_tensor(f"bank{i}", [P, HALF], F32)) for i in range(8)]

        h = sb("h", [P, NT, D])
        ln = sb("ln", [P, NT, D])
        ln_hi = sb("ln_hi", [P, B * L], F32R)
        ln_lo = sb("ln_lo", [P, B * L], F32R)
        base = sb("base", [P, NT, D])
        ident = sb("ident", [P, P])
        stats = sb("stats", [P, NT, 6])
        mv = sb("mv", [P, NT, 2])
        var_eps = sb("var_eps", [P, NT])
        minus_half = sb("minus_half", [P, NT])
        zero = sb("zero", [P, 1])
        one = sb("one", [P, 1])
        rstd = sb("rstd", [P, NT])

        ARENA = 22528
        arena = sb("arena", [P, ARENA])

        def part(first, *shape, rows=slice(0, P)):
            n = int(np.prod(shape))
            assert first + n <= ARENA, (first, shape)
            view = arena[rows, first:first + n]
            if len(shape) == 2:
                view = view.rearrange("p (a b) -> p a b", b=shape[1])
            if len(shape) == 3:
                view = view.rearrange("p (a b c) -> p a b c", b=shape[1], c=shape[2])
            return view

        arena_r = sb("arena_r", [P, 8 * L], F32R)

        v_all = part(0, NT, H * DK)
        o_all = part(8192, NT, H * DK)
        p_t = part(16384, s_first[NS])
        v_head = [part(20992 + 768 * i, TB, VW) for i in range(2)]
        query_hh = [arena_r[:, L * i:L * (i + 1)] for i in range(0, 2)]
        query_lm = [arena_r[:, L * i:L * (i + 1)] for i in range(2, 4)]
        key_hl = [arena_r[:, L * i:L * (i + 1)] for i in range(4, 6)]
        key_h1 = [arena_r[:, L * i:L * (i + 1)] for i in range(6, 8)]
        o_t = [part(16384 + 512 * i, HALF) for i in range(2)]
        tok_sel = part(8192, B * L, rows=slice(0, SEL_K))
        tok_tab = part(10240, D, rows=slice(0, SEL_K))
        seen = part(10368, VOCAB, NFR, rows=slice(0, N_FFT))
        re_sq = part(10912, VOCAB * NFR, rows=slice(0, N_FREQ))
        im_sq = part(11456, VOCAB * NFR, rows=slice(0, N_FREQ))
        mag = part(12000, VOCAB, NFR, rows=slice(0, N_FREQ))
        proj_w = part(12544, VOCAB, D_STFT, rows=slice(0, N_FREQ))
        proj_b = part(13184, D_STFT, rows=slice(0, NFR))
        dft64 = part(13248, 2, N_FREQ, rows=slice(0, N_FFT))
        w_v = part(16384, H * DK)
        b_v = part(16896, H * DK)
        mask_f = part(17408, P)
        w_v_hi = arena_r[:, 0:HALF]
        w_v_lo = arena_r[:, HALF:L]
        ids_i = part(14016, B * L, rows=slice(VOCAB_AT, SEL_K)).bitcast(I32)
        frames_i = part(16064, NFR, rows=slice(0, N_FFT)).bitcast(I32)

        vocab_row = sb("vocab_row", [N_FFT, VOCAB])
        vocab_col = sb("vocab_col", [P, 1])
        w_head = sb("w_head", [P, 2 * P])
        w_head_hi = sb("w_head_hi", [P, 2 * P], F32R)
        w_head_lo = sb("w_head_lo", [P, 2 * P], F32R)
        b_head = sb("b_head", [P, 2])
        max_cols = sb("max_cols", [P, MAX_END])
        w_out = sb("w_out", [P, 4, D])
        b_out = sb("b_out", [P, D])
        mask_b = sb("mask_b", [P, P], BF16)
        ident_b = sb("ident_b", [P, P], BF16)
        max_part = sb("max_part", [P, TB])
        o_scale = sb("o_scale", [P, TB])

        y = part(0, 6, B, D)
        sum4 = part(1536, B, 4, D)
        dif4 = part(2560, B, 4, D)
        ev2 = part(3584, B, 2, D)
        od2 = part(4096, B, 2, D)
        dd = part(4608, B, D)
        gg = part(4864, B, D)
        xf = part(5632, 2, NF)
        h_hi = arena_r[:, 0:FT * P]
        h_lo = arena_r[:, FT * P:2 * FT * P]
        hid_f = [part(8840 + 4104 * i, FC, NF) for i in range(2)]
        acc_f = part(17048, FT, D)
        moe_t = part(18200, FT * P)
        wsel_t = part(19352, FT * P, rows=slice(0, E))
        of = part(8840, RES, B, D)
        comb = part(10888, 8, B, D)
        ot = part(12936, NT, D)
        inv = part(0, 12, B, D)
        p_2 = [part(8192 * i, TB, L) for i in range(2)]
        z_one = part(16384, NT, 130)
        hid_g = [part(4096 * i, FC, L) for i in range(2)]
        acc_g = part(18464, TB, D)

        fwd_single = sb("fwd_single", [P, 258])
        fwd_pair = sb("fwd_pair", [P, 6, 256])
        inverse = sb("inverse", [P, 14, P])
        w1 = [sb(f"w1_{i}", [P, FF]) for i in range(2)]
        w1_hi = [sb(f"w1_hi_{i}", [P, FF], F32R) for i in range(2)]
        w1_lo = [sb(f"w1_lo_{i}", [P, FF], F32R) for i in range(2)]
        w2 = [sb(f"w2_{i}", [P, FC, D]) for i in range(2)]
        b1 = [sb(f"b1_{i}", [P, FC]) for i in range(2)]
        pin_w = sb("pin_w", [P, 2, D])
        pin_b = sb("pin_b", [P, 1])
        router_w = sb("router_w", [P, E])
        router_b = sb("router_b", [P, E])
        b2 = sb("b2", [E, D])
        pout_w = sb("pout_w", [P, 2, D])
        pout_b = sb("pout_b", [P, 2, D])
        ln_g = sb("ln_g", [P, D])
        ln_b = sb("ln_b", [P, D])
        expert_no = sb("expert_no", [P, E])
        logits = sb("logits", [P, FT, E])
        top8 = sb("top8", [P, FT, 8])
        idx8 = sb("idx8", [P, FT, 8], U32)
        choice = sb("choice", [P, FT, 2])
        gap = sb("gap", [P, FT, 1])
        odds = sb("odds", [P, FT, 1])
        odds1 = sb("odds1", [P, FT, 1])
        share = sb("share", [P, FT, 2])
        pick = [sb(f"pick{i}", [P, FT, E]) for i in range(2)]
        wsel_f = sb("wsel_f", [P, FT, E])
        gate_w = sb("gate_w", [P, TB, 2])
        gate_i = sb("gate_i", [P, TB, 2], I32)
        gate_no = sb("gate_no", [P, TB, 2])
        wsel_g = sb("wsel_g", [P, TB, E])
        minus_shift = sb("minus_shift", [P, 1])
        den2 = sb("den2", [P, NT])

        ids_loaded = sem("ids_loaded")
        tok_loaded = sem("tok_loaded")
        attn_loaded = sem("attn_loaded")
        w_head_loaded = sem("w_head_loaded")
        pool_const = sem("pool_const")
        zero_ready = sem("zero_ready")
        tok_cleared = sem("tok_cleared")
        seen_ready = sem("seen_ready")
        dft_done = sem("dft_done")
        squares = sem("squares")
        power_ready = sem("power_ready")
        mag_ready = sem("mag_ready")
        enc_done = sem("enc_done")
        tab_ready = sem("tab_ready")
        sel_ready = sem("sel_ready")
        tok_done = sem("tok_done")
        h_ready = sem("h_ready")
        stats_done = sem("stats_done")
        mean_done = sem("mean_done")
        var_ready = sem("var_ready")
        rstd_ready = sem("rstd_ready")
        ln_ready = sem("ln_ready")
        turned = sem("turned")
        ln_hi_ready = sem("ln_hi_ready")
        ln_lo_ready = sem("ln_lo_ready")
        consts_b = sem("consts_b")
        v_done = sem("v_done")
        v_ready = sem("v_ready")
        v_head_ready = sem("v_head_ready")
        q_done = sem("q_done")
        k_done = sem("k_done")
        q_high = sem("q_high")
        q_low = sem("q_low")
        k_high = sem("k_high")
        k_low = sem("k_low")
        k_copied = sem("k_copied")
        w_v_split = sem("w_v_split")
        w_head_split = sem("w_head_split")
        rows_done = sem("rows_done")
        rows_used = sem("rows_used")
        max_ready = sem("max_ready")
        max_turned = sem("max_turned")
        max_row_ready = sem("max_row_ready")
        scores_done = sem("scores_done")
        probs_ready = sem("probs_ready")
        pv_done = [sem("pv_done0"), sem("pv_done1")]
        den_ready = [sem("den_ready0"), sem("den_ready1")]
        o_ready = [sem("o_ready0"), sem("o_ready1")]
        base_ready = sem("base_ready")
        o_turned = sem("o_turned")
        o_t_ready = sem("o_t_ready")
        out_done = sem("out_done")
        stored = sem("stored")
        fourier_loaded = sem("fourier_loaded")
        pad_cleared = sem("pad_cleared")
        base_f_ready = sem("base_f_ready")
        fold1 = sem("fold1")
        fold2 = sem("fold2")
        fold3 = sem("fold3")
        y_ready = sem("y_ready")
        spec_done = sem("spec_done")
        spec_ready_a = sem("spec_ready_a")
        spec_ready_v = sem("spec_ready_v")
        pin_done = sem("pin_done")
        h_hi_ready = sem("h_hi_ready")
        h_lo_ready = sem("h_lo_ready")
        router_done = sem("router_done")
        logits_ready = sem("logits_ready")
        top_ready = sem("top_ready")
        idx_ready = sem("idx_ready")
        gap_ready = sem("gap_ready")
        odds_ready = sem("odds_ready")
        route = sem("route")
        wsel_ready = sem("wsel_ready")
        wsel_turned = sem("wsel_turned")
        wsel_t_ready = sem("wsel_t_ready")
        bias_done = sem("bias_done")
        moe_turned = sem("moe_turned")
        moe_t_ready = sem("moe_t_ready")
        of_done = sem("of_done")
        of_ready = sem("of_ready")
        inv_done = sem("inv_done")
        comb_ready_a = sem("comb_ready_a")
        comb_ready_v = sem("comb_ready_v")
        unfold1 = sem("unfold1")
        unfold2 = sem("unfold2")
        unfold3 = sem("unfold3")
        ot_ready = sem("ot_ready")
        ot_norm = sem("ot_norm")
        ot_scaled = sem("ot_scaled")
        h2_ready = sem("h2_ready")
        w1_loaded = [sem("w1_loaded0"), sem("w1_loaded1")]
        w2_loaded = [sem("w2_loaded0"), sem("w2_loaded1")]
        b1_loaded = [sem("b1_loaded0"), sem("b1_loaded1")]
        w1_split = sem("w1_split")
        hidden_done = [sem("hidden_done0"), sem("hidden_done1")]
        hidden_ready = [sem("hidden_ready0"), sem("hidden_ready1")]
        expert_done = [sem("expert_done0"), sem("expert_done1")]
        acc_ready = [sem("acc_ready0"), sem("acc_ready1")]
        z_ready = sem("z_ready")
        scores2_done = sem("scores2_done")
        probs2_ready = sem("probs2_ready")
        pv2_done = sem("pv2_done")
        den2_ready = sem("den2_ready")
        h3_ready = sem("h3_ready")
        gates = sem("gates")

        pj, sm, st, pv = bank[0:2], bank[2:4], bank[4:6], bank[6:8]

        def spectrum(copy, eng, b, ready):
            grouped = xf[:, :, 0:NYQ].rearrange("p c (g m) -> p c g m", m=M64)
            eng.wait_ge(spec_done, 4 * b + 1)
            copy(grouped[:, :, b * RES, :], bank[4 * b][:, 0:2 * M64].rearrange("p (c m) -> p c m", c=2)).then_inc(ready, 1)
            copy(grouped[:, :, b * RES + 4, :], bank[4 * b][:, 256:256 + 2 * M64].rearrange("p (c m) -> p c m", c=2)).then_inc(ready, 1)
            copy(xf[:, :, NYQ + b:NYQ + b + 1], bank[4 * b][:, 2 * M64:2 * M64 + 2].unsqueeze(2)).then_inc(ready, 1)
            for r in range(1, 4):
                eng.wait_ge(spec_done, 4 * b + r + 1)
                pair = grouped[:, :, b * RES + r:b * RES + 9 - r:8 - 2 * r, :]
                copy(pair, bank[4 * b + r][:, 0:4 * M64].rearrange("p (k c m) -> p c k m", k=2, c=2)).then_inc(ready, 1)

        block = ctx.enter_context(nc.Block())

        @block.sync
        def _(sp):
            sp.dma_start(frames_i, a["ids_frames"]).then_inc(ids_loaded, 16)
            sp.dma_start(vocab_row[:], a["vocab_row"]).then_inc(ids_loaded, 16)
            sp.dma_start(dft64, a["dft64"]).then_inc(ids_loaded, 16)
            sp.dma_start(ids_i, a["ids_bcast"]).then_inc(ids_loaded, 16)
            sp.dma_start(vocab_col[:], a["vocab_col"]).then_inc(ids_loaded, 16)
            sp.dma_start(proj_w, a["proj_w"].rearrange("(f v) o -> f v o", v=VOCAB)).then_inc(tok_loaded, 16)
            sp.dma_start(proj_b, a["proj_b"]).then_inc(tok_loaded, 16)
            sp.wait_ge(tok_cleared, 2)
            sp.dma_start(tok_tab[VOCAB_AT:SEL_K, 0:D_EMB], a["emb_table"]).then_inc(tok_loaded, 16)
            sp.dma_start(tok_sel[0:NFR, :], a["upsample"]).then_inc(tok_loaded, 16)
            sp.dma_start(ident[:], a["ident"]).then_inc(attn_loaded, 16)
            sp.dma_start(mask_f, a["mask"]).then_inc(attn_loaded, 16)
            sp.dma_start(w_v, a["w_v"]).then_inc(attn_loaded, 16)
            sp.dma_start(b_v, a["b_v"]).then_inc(attn_loaded, 16)
            sp.dma_start(w_out[:], a["w_out"].rearrange("(c p) d -> p c d", p=P)).then_inc(attn_loaded, 16)
            sp.dma_start(b_out[:], a["b_out"]).then_inc(attn_loaded, 16)
            sp.dma_start(w_head[:], a["w_qk"][0]).then_inc(w_head_loaded, 16)
            sp.dma_start(b_head[:], a["b_qk"][0]).then_inc(w_head_loaded, 16)
            for to, name in ((fwd_single[:], "fwd_single"), (fwd_pair[:], "fwd_pair"), (inverse[:], "inverse"),
                             (pin_b[:], "pin_b"), (router_w[:], "router_w"), (router_b[:], "router_b"), (b2[:], "b2"),
                             (pout_b[:], "pout_b"), (ln_g[:], "ln_g"), (ln_b[:], "ln_b"), (expert_no[:], "expert_no"),
                             (gate_w[:], "gate_w"), (gate_i[:], "gate_i")):
                sp.dma_start(to, a[name]).then_inc(fourier_loaded, 16)
            sp.dma_start(pin_w[:], a["pin_w"].rearrange("(c p) d -> p c d", p=P)).then_inc(fourier_loaded, 16)
            sp.dma_start(pout_w[:], a["pout_w"].rearrange("p (c d) -> p c d", d=D)).then_inc(fourier_loaded, 16)
            with sp.Fori(0, H - 1) as hd:
                sp.wait_ge(w_head_split, hd * 2 + 2)
                sp.dma_start(w_head[:], a["w_qk"][bass.ds(hd + 1, 1)].rearrange("o p n -> (o p) n")).then_inc(w_head_loaded, 16)
                sp.wait_ge(q_low, hd * 4 + 4)
                sp.wait_ge(k_low, hd * 4 + 4)
                sp.dma_start(b_head[:], a["b_qk"][bass.ds(hd + 1, 1)].rearrange("o p n -> (o p) n")).then_inc(w_head_loaded, 16)

            def load_w1(layer, e, i):
                sp.dma_start(w1[i][:], a[("w1_f", "w1_g")[layer]][bass.ds(e, 1)].rearrange("o d f -> (o d) f")).then_inc(w1_loaded[i], 16)

            def load_w2(layer, e, i):
                sp.dma_start(w2[i][:], a[("w2_f", "w2_g")[layer]][bass.ds(e, 1)].rearrange("o (c p) d -> (o p) c d", p=P)).then_inc(w2_loaded[i], 16)

            def load_b1(e, i):
                sp.dma_start(b1[i][:], a["b1_f"][bass.ds(e, 1)].rearrange("o p c -> (o p) c")).then_inc(b1_loaded[i], 16)

            for i in range(2):
                load_w1(0, i, i)
                load_b1(i, i)
                load_w2(0, i, i)
            with sp.Fori(0, E - 3, 2) as e:
                for i in range(2):
                    sp.wait_ge(w1_split, (e + i) * 2 + 2)
                    load_w1(0, e + i + 2, i)
                    sp.wait_ge(hidden_ready[0], (e + i) * GROUPS[0] + GROUPS[0])
                    load_b1(e + i + 2, i)
                    sp.wait_ge(expert_done[0], (e + i) * TILES[0] + TILES[0])
                    load_w2(0, e + i + 2, i)
            for i in range(2):
                sp.wait_ge(w1_split, (E - 2 + i) * 2 + 2)
                load_w1(1, i, i)
                sp.wait_ge(expert_done[0], (E - 1 + i) * TILES[0])
                load_w2(1, i, i)
            for e in range(E - 2):
                sp.wait_ge(w1_split, (E + e) * 2 + 2)
                load_w1(1, e + 2, e % 2)
                if e == 0:
                    sp.wait_ge(h3_ready, NT)
                    sp.dma_start(out[L:, :].rearrange("(t p) d -> p t d", p=P), h[:, TB:, :]).then_inc(stored, 16)
                sp.wait_ge(expert_done[1], e * TILES[1] + TILES[1])
                load_w2(1, e + 2, e % 2)
            sp.wait_ge(acc_ready[1], TB * (E + 1))
            sp.dma_start(out[0:L, :].rearrange("(t p) d -> p t d", p=P), acc_g).then_inc(stored, 16)
            sp.wait_ge(stored, 2 * 16)

        @block.gpsimd
        def _(pool):
            pool.memset(tok_sel[32:VOCAB_AT, :], 0.0).then_inc(tok_cleared, 1)
            pool.wait_ge(tok_cleared, 1)
            pool.memset(tok_tab, 0.0).then_inc(tok_cleared, 1)
            pool.wait_ge(tok_cleared, 2)
            pool.memset(zero[:], 0.0).then_inc(zero_ready, 1)
            pool.wait_ge(zero_ready, 1)
            pool.memset(one[:], 1.0).then_inc(zero_ready, 1)
            pool.wait_ge(zero_ready, 2)

            def fill(to, rows, value, width):
                n = rows.stop - rows.start
                return pool.tensor_tensor(to[rows, :], value[rows, :].broadcast_to([n, width]), zero[rows, :].broadcast_to([n, width]), ALU.add)

            pool.memset(minus_half[:], -0.5).then_inc(pool_const, 1)
            pool.wait_ge(pool_const, 1)
            pool.memset(max_cols[:], 0.0).then_inc(pool_const, 1)
            for i in range(2):
                first = 5 * i + 2
                pool.wait_ge(pool_const, first)
                fill(query_lm[i], slice(DK, P), zero, L).then_inc(pool_const, 1)
                pool.wait_ge(pool_const, first + 1)
                fill(key_h1[i], slice(DK, P), zero, L).then_inc(pool_const, 1)
                pool.wait_ge(pool_const, first + 2)
                fill(key_h1[i], slice(MAX_AT, MAX_END), one, L).then_inc(pool_const, 1)
                pool.wait_ge(pool_const, first + 3)
                pool.memset(v_head[i][:, :, DK + 1:VW], 0.0).then_inc(pool_const, 1)
                pool.wait_ge(pool_const, first + 4)
                pool.memset(v_head[i][:, :, DK:DK + 1], 1.0).then_inc(pool_const, 1)

            def inverse_roots(n):
                b = n % B
                pool.wait_ge(var_ready, n + 1)
                tiles = slice(b * TB, (b + 1) * TB)
                pool.tensor_tensor(rstd[:, tiles], var_eps[:, tiles], minus_half[:, tiles], ALU.pow).then_inc(rstd_ready, 1)

            def split_head(hd=0):
                pool.wait_ge(w_head_loaded, hd * 32 + 32)
                pool.tensor_tensor(w_head_hi[:], w_head[:], zero[:].broadcast_to([P, 2 * P]), ALU.add).then_inc(w_head_split, 1)
                pool.wait_ge(w_head_split, hd * 2 + 1)
                pool.tensor_tensor(w_head_lo[:], w_head[:], w_head_hi[:], ALU.subtract).then_inc(w_head_split, 1)

            inverse_roots(0)
            inverse_roots(1)
            pool.wait_ge(attn_loaded, 6 * 16)
            pool.tensor_copy(w_v_hi, w_v).then_inc(w_v_split, 1)
            pool.wait_ge(w_v_split, 1)
            pool.tensor_tensor(w_v_lo, w_v, w_v_hi, ALU.subtract).then_inc(w_v_split, 1)
            split_head()
            pool.wait_ge(ln_ready, NT)
            pool.tensor_tensor(base[:], h[:], ln[:], ALU.add).then_inc(base_ready, 1)
            pool.wait_ge(base_ready, 1)
            pool.tensor_tensor(base[:], base[:], b_out[:].unsqueeze(1).broadcast_to([P, NT, D]), ALU.add).then_inc(base_ready, 1)

            def copy_values(hd, b):
                pool.tensor_copy(v_head[b][:, :, 0:DK], v_all[:, b * TB:(b + 1) * TB, bass.ds(hd * DK, DK)]).then_inc(v_head_ready, 1)

            def next_values(hd, b):
                pool.wait_ge(pv_done[1], hd * B + b + 1)
                copy_values(hd + b, 1 - b)

            def copy_keys(hd, b):
                n = hd * B + b
                for c in range(2):
                    cols = slice(HALF * c, HALF * (c + 1))
                    pool.wait_ge(k_high, n * 2 + c + 1)
                    pool.tensor_tensor(key_h1[b][0:DK, cols], key_hl[b][0:DK, cols], zero[0:DK, :].broadcast_to([DK, HALF]), ALU.add).then_inc(k_copied, 1)

            copy_keys(0, 0)
            pool.wait_ge(v_ready, NT)
            copy_values(0, 0)
            with pool.Fori(0, H - 1) as hd:
                next_values(hd, 0)
                copy_keys(hd, 1)
                pool.wait_ge(k_done, hd * 4 + 4)
                split_head(hd=hd + 1)
                next_values(hd, 1)
                copy_keys(hd + 1, 0)
            next_values(H - 1, 0)
            copy_keys(H - 1, 1)

            inverse_roots(2)
            inverse_roots(3)
            fill(h_hi[:, NF:FT * P], slice(0, P), zero, FT * P - NF).then_inc(pad_cleared, 1)
            pool.wait_ge(pad_cleared, 1)
            fill(h_lo[:, NF:FT * P], slice(0, P), zero, FT * P - NF).then_inc(pad_cleared, 1)
            pool.wait_ge(pad_cleared, 2)
            pool.memset(minus_shift[:], -D / 2).then_inc(pad_cleared, 1)
            pool.wait_ge(ln_ready, 2 * NT)
            pool.wait_ge(fourier_loaded, FOURIER_LOADS * 16)
            pool.tensor_tensor(base[:], h[:], ln[:], ALU.add).then_inc(base_f_ready, 1)
            pool.wait_ge(base_f_ready, 1)
            pool.tensor_tensor(base[:], base[:], ln_b[:].unsqueeze(1).broadcast_to([P, NT, D]), ALU.add).then_inc(base_f_ready, 1)

            def split_w1(n, i):
                pool.wait_ge(w1_loaded[i], (n - i) * 8 + 16)
                pool.tensor_tensor(w1_hi[i][:], w1[i][:], zero[:].broadcast_to([P, FF]), ALU.add).then_inc(w1_split, 1)
                pool.wait_ge(w1_split, n * 2 + 1)
                pool.tensor_tensor(w1_lo[i][:], w1[i][:], w1_hi[i][:], ALU.subtract).then_inc(w1_split, 1)

            for i in range(2):
                split_w1(i, i)
            with pool.Fori(0, E - 3, 2) as e:
                for i in range(2):
                    pool.wait_ge(hidden_done[0], (e + i) * GROUPS[0] + GROUPS[0])
                    split_w1(e + i + 2, i)
            inverse_roots(4)
            inverse_roots(5)

            for i in range(2):
                pool.wait_ge(hidden_done[0], (E - 1 + i) * GROUPS[0])
                split_w1(E + i, i)

            inverse_roots(6)
            inverse_roots(7)
            for b in range(B):
                tiles = slice(b * TB, (b + 1) * TB)
                pool.wait_ge(ln_ready, 2 * NT + (b + 1) * TB)
                if b:
                    pool.wait_ge(z_ready, 2)
                pool.tensor_copy(z_one[:, tiles, 0:D], ln[:, tiles, :]).then_inc(z_ready, 1)
                pool.wait_ge(z_ready, 2 * b + 1)
                pool.memset(z_one[:, tiles, D:D + 1], 1.0).then_inc(z_ready, 1)
            inverse_roots(8)
            with pool.Fori(0, E - 3, 2) as e:
                for i in range(2):
                    pool.wait_ge(hidden_done[1], (e + i) * GROUPS[1] + GROUPS[1])
                    split_w1(e + i + (E + 2), i)

        @block.scalar
        def _(act):
            for i in range(4):
                act.wait_ge(dft_done, i + 1)
                half = i % 2
                to = (re_sq, im_sq)[i // 2][:, half * 272:(half + 1) * 272]
                act.activation(to, bank[i][0:N_FREQ, 0:272], ACT.Square).then_inc(squares, 1)
            act.wait_ge(power_ready, 1)
            act.activation(mag.rearrange("p v n -> p (v n)"), re_sq, ACT.Sqrt).then_inc(mag_ready, 1)
            for i in range(4):
                act.wait_ge(tok_done, i + 1)
                act.copy(h[:, 4 * i:4 * i + 4, :], bank[i].rearrange("p (t d) -> p t d", d=D)).then_inc(h_ready, 1)

            def features_down(n):
                for i in range(2):
                    act.wait_ge(turned, 2 * n + i + 1)
                    first = (n % B) * L + HALF * i
                    act.copy(ln_hi[:, first:first + HALF], bank[4 + i][:]).then_inc(ln_hi_ready, 1)

            features_down(0)
            features_down(1)

            def high_parts(hd, b, c, done, which, to, ready):
                n = hd * B + b
                act.wait_ge(done, n * 2 + c + 1)
                act.activation(to[b][:, HALF * c:HALF * (c + 1)], pj[c][:], ACT.Identity, bias=b_head[:, which:which + 1]).then_inc(ready, 1)

            def queries(hd, b):
                for c in range(2):
                    high_parts(hd, b, c, q_done, 0, query_hh, q_high)

            def keys(hd, b, c):
                high_parts(hd, b, c, k_done, 1, key_hl, k_high)

            def exp_head(hd, b, last=False):
                n = hd * B + b
                if not last:
                    queries(hd + b, 1 - b)
                for c, (half, i, first, width) in enumerate(s_chunks):
                    if c in KEYS_BEFORE and not last:
                        keys(hd + b, 1 - b, KEYS_BEFORE.index(c))
                    if c == 0 or s_chunks[c - 1][0] != half:
                        act.wait_ge(pv_done[half], n + 1)
                    act.wait_ge(scores_done, n * NS + c + 1)
                    act.activation(p_t[:, s_first[c]:s_first[c] + width], st[c % 2][:, 0:width], ACT.Exp, scale=DK ** -0.5).then_inc(probs_ready, 1)

            act.wait_ge(attn_loaded, 6 * 16)
            act.wait_ge(pool_const, POOL_CONSTS)
            queries(0, 0)
            for c in range(2):
                keys(0, 0, c)
            with act.Fori(0, H - 1) as hd:
                exp_head(hd, 0)
                exp_head(hd, 1)
            exp_head(H - 1, 0)
            exp_head(H - 1, 1, last=True)

            for t in range(NT):
                act.wait_ge(o_turned, t + 1)
                if t >= 2:
                    act.wait_ge(out_done, t - 1)
                act.copy(o_t[t % 2], bank[t % 2][:]).then_inc(o_t_ready, 1)

            act.wait_ge(fourier_loaded, FOURIER_LOADS * 16)
            spectrum(act.copy, act, 0, spec_ready_a)
            for i in range(3):
                act.wait_ge(pin_done, i + 1)
                act.activation(h_hi[:, FCH * i:FCH * (i + 1)], bank[i][:, 0:FCH], ACT.Identity, bias=pin_b[:]).then_inc(h_hi_ready, 1)
            def hidden(layer, e, i):
                for g in range(GROUPS[layer]):
                    act.wait_ge(hidden_done[layer], e * GROUPS[layer] + g + 1)
                    c, k = g % FC, g // FC
                    if layer == 0 and g == 0:
                        act.wait_ge(b1_loaded[i], (e - i) * 8 + 16)
                    to = (hid_f if layer == 0 else hid_g)[i][:, c, COLS[layer] * k:COLS[layer] * (k + 1)]
                    bias = {"bias": b1[i][:, c:c + 1]} if layer == 0 else {}
                    act.activation(to, bank[g % 2][:, 0:COLS[layer]], ACT.Gelu, **bias).then_inc(hidden_ready[layer], 1)

            def hidden_rest(layer):
                hidden(layer, 1, 1)
                with act.Fori(0, E - 3, 2) as e:
                    for i in range(2):
                        act.wait_ge(expert_done[layer], (e + i) * TILES[layer] + TILES[layer])
                        hidden(layer, e + i + 2, i)

            hidden(0, 0, 0)
            act.wait_ge(gap_ready, 1)
            act.activation(odds[:], gap[:], ACT.Exp).then_inc(odds_ready, 1)
            for i in range(3):
                act.wait_ge(wsel_turned, i + 1)
                n = min(4, FT - 4 * i) * P
                act.copy(wsel_t[:, 4 * i * P:4 * i * P + n], bank[4 + i][0:E, 0:n]).then_inc(wsel_t_ready, 1)

            hidden_rest(0)
            for i in range(3):
                act.wait_ge(moe_turned, i + 1)
                n = min(4 * P, NF - 4 * i * P)
                act.copy(moe_t[:, 4 * i * P:4 * i * P + n], bank[i][:, 0:n]).then_inc(moe_t_ready, 1)
            for i in range(2):
                act.wait_ge(inv_done, i + 1)
                act.copy(comb[:, 2 * i:2 * i + 2], bank[4 + i].rearrange("p (o b d) -> p o b d", o=2, b=B)).then_inc(comb_ready_a, 1)

            features_down(2)
            features_down(3)
            act.wait_ge(pad_cleared, 3)
            for b in range(B):
                for c in range(2 * TB):
                    act.wait_ge(scores2_done, b * 2 * TB + c + 1)
                    act.activation(p_2[b][:, c % TB, HALF * (c // TB):HALF * (c // TB + 1)], bank[c % 2][:], ACT.Exp, bias=minus_shift[:]).then_inc(probs2_ready, 1)
            features_down(4)
            hidden(1, 0, 0)
            hidden_rest(1)

        @block.vector
        def _(dve):
            dve.wait_ge(ids_loaded, 5 * 16)
            dve.tensor_tensor(seen, frames_i.unsqueeze(1).broadcast_to([N_FFT, VOCAB, NFR]), vocab_row[:].unsqueeze(2).broadcast_to([N_FFT, VOCAB, NFR]), ALU.is_equal).then_inc(seen_ready, 1)
            dve.tensor_scalar(tok_sel[VOCAB_AT:SEL_K, :], ids_i, vocab_col[VOCAB_AT:SEL_K, :], None, ALU.is_equal).then_inc(sel_ready, 1)
            dve.wait_ge(squares, 4)
            dve.scalar_tensor_tensor(out=re_sq, in0=re_sq, scalar=1e-33, in1=im_sq, op0=ALU.max, op1=ALU.add).then_inc(power_ready, 1)
            dve.wait_ge(tok_loaded, 4 * 16)
            dve.wait_ge(enc_done, 1)
            dve.tensor_tensor(tok_tab[0:NFR, D_EMB:D], bank[4][0:NFR, 0:D_STFT], proj_b, ALU.add).then_inc(tab_ready, 1)

            def statistics(n, rows=h):
                b = n % B
                for t in range(b * TB, (b + 1) * TB):
                    dve.bn_stats(stats[:, t, :], rows[:, t, :]).then_inc(stats_done, 1)
                for i, t in enumerate(range(b * TB, (b + 1) * TB)):
                    dve.wait_ge(stats_done, TB * n + i + 1)
                    dve.bn_aggr(mv[:, t, :], stats[:, t, :]).then_inc(mean_done, 1)
                dve.wait_ge(mean_done, TB * (n + 1))
                tiles = slice(b * TB, (b + 1) * TB)
                dve.tensor_scalar(var_eps[:, tiles], mv[:, tiles, 1], LN_EPS, None, ALU.add).then_inc(var_ready, 1)

            def normalise(n, rows=h, to=ln, ready=ln_ready):
                b = n % B
                dve.wait_ge(rstd_ready, n + 1)
                for t in range(b * TB, (b + 1) * TB):
                    dve.tensor_scalar(to[:, t, :], rows[:, t, :], mv[:, t, 0:1], rstd[:, t:t + 1], ALU.subtract, ALU.mult).then_inc(ready, 1)

            dve.wait_ge(h_ready, 2)
            statistics(0)
            dve.wait_ge(h_ready, 4)
            statistics(1)
            normalise(0)
            normalise(1)

            def low_features(n):
                for i in range(2):
                    dve.wait_ge(ln_hi_ready, 2 * n + i + 1)
                    first = (n % B) * L + HALF * i
                    cols = slice(first, first + HALF)
                    dve.tensor_tensor(ln_lo[:, cols], bank[4 + i][:], ln_hi[:, cols], ALU.subtract).then_inc(ln_lo_ready, 1)

            low_features(0)
            low_features(1)
            dve.wait_ge(attn_loaded, 6 * 16)
            dve.tensor_copy(mask_b[:], mask_f).then_inc(consts_b, 1)
            dve.tensor_copy(ident_b[:], ident[:]).then_inc(consts_b, 1)
            for t in range(NT):
                dve.wait_ge(v_done, t + 1)
                dve.tensor_tensor(v_all[:, t, :], bank[t % 4][:], b_v, ALU.add).then_inc(v_ready, 1)

            def low_queries(hd, b):
                n = hd * B + b
                for c in range(2):
                    cols = slice(HALF * c, HALF * (c + 1))
                    dve.wait_ge(q_high, n * 2 + c + 1)
                    dve.scalar_tensor_tensor(out=query_lm[b][0:DK, cols], in0=pj[c][0:DK, :], scalar=b_head[0:DK, 0:1], in1=query_hh[b][0:DK, cols], op0=ALU.add, op1=ALU.subtract).then_inc(q_low, 1)

            def low_keys(hd, b):
                n = hd * B + b
                for c in range(2):
                    cols = slice(HALF * c, HALF * (c + 1))
                    dve.wait_ge(k_high, n * 2 + c + 1)
                    dve.scalar_tensor_tensor(out=key_hl[b][DK:P, cols], in0=pj[c][DK:P, :], scalar=b_head[DK:P, 1:2], in1=key_hl[b][DK:P, cols], op0=ALU.add, op1=ALU.subtract).then_inc(k_low, 1)

            def maxima(hd, b):
                n = hd * B + b
                for m, (j, c, width) in enumerate(m_chunks):
                    dve.wait_ge(rows_done, n * NM + m + 1)
                    if j < 4:
                        to = max_cols[:, MAX_AT + j:MAX_AT + j + 1]
                    else:
                        to = max_part[:, 2 * (j - 4) + c:2 * (j - 4) + c + 1]
                    dve.tensor_reduce(to, sm[m % 2][:, 0:width], AX.X, ALU.max, negate=True).then_inc(rows_used, 1)
                dve.wait_ge(rows_used, n * NM + NM)
                pairs = max_part[:].rearrange("p (j c) -> p j c", c=2)
                dve.tensor_tensor(max_cols[:, MAX_AT + 4:MAX_END].unsqueeze(2), pairs[:, :, 0:1], pairs[:, :, 1:2], ALU.min).then_inc(max_ready, 1)

            def max_rows(hd, b):
                dve.wait_ge(max_turned, hd * B + b + 1)
                to = query_lm[b][MAX_AT:MAX_END, :].rearrange("p (t q) -> p t q", q=P)
                diagonal = ident[MAX_AT:MAX_END, MAX_AT:MAX_END].unsqueeze(2).broadcast_to([TB, TB, P])
                dve.tensor_tensor(to, sm[0][MAX_AT:MAX_END, 0:P].unsqueeze(1).broadcast_to([TB, TB, P]), diagonal, ALU.mult).then_inc(max_row_ready, 1)

            def divide(hd, b, half):
                n = hd * B + b
                dve.wait_ge(pv_done[half], n + 2)
                got = pv[half][:, 0:4 * VW].rearrange("p (t w) -> p t w", w=VW)
                scale = o_scale[:, 4 * half:4 * half + 4].unsqueeze(2)
                dve.reciprocal(scale, got[:, :, DK:DK + 1]).then_inc(den_ready[half], 1)
                dve.wait_ge(den_ready[half], n + 1)
                to = o_all[:, b * TB + 4 * half:b * TB + 4 * half + 4, bass.ds(hd * DK, DK)]
                dve.tensor_tensor(to, got[:, :, 0:DK], scale.broadcast_to([P, 4, DK]), ALU.mult).then_inc(o_ready[half], 1)

            def vector_head(hd, b, last=False):
                if not last:
                    low_queries(hd + b, 1 - b)
                    low_keys(hd + b, 1 - b)
                divide(hd, b, 0)
                if not last:
                    maxima(hd + b, 1 - b)
                    max_rows(hd + b, 1 - b)
                divide(hd, b, 1)

            for half in range(2):
                dve.memset(o_scale[:, 4 * half:4 * half + 4], 1.0).then_inc(o_ready[half], 1)
            dve.wait_ge(pool_const, POOL_CONSTS)
            low_queries(0, 0)
            low_keys(0, 0)
            maxima(0, 0)
            max_rows(0, 0)
            with dve.Fori(0, H - 1) as hd:
                vector_head(hd, 0)
                vector_head(hd, 1)
            vector_head(H - 1, 0)
            vector_head(H - 1, 1, last=True)

            dve.wait_ge(base_ready, 2)
            for i in range(4):
                dve.wait_ge(out_done, 4 * i + 4)
                dve.tensor_tensor(h[:, 4 * i:4 * i + 4, :], bank[4 + i].rearrange("p (t d) -> p t d", d=D), base[:, 4 * i:4 * i + 4, :], ALU.add).then_inc(h_ready, 1)
            dve.wait_ge(h_ready, 6)
            statistics(2)
            dve.wait_ge(h_ready, 8)
            statistics(3)
            normalise(2)
            normalise(3)

            dve.wait_ge(ln_ready, 2 * NT)
            x8 = ln[:].rearrange("p (b j) d -> p b j d", b=B)
            dve.tensor_tensor(sum4, x8[:, :, 0:4], x8[:, :, 4:8], ALU.add).then_inc(fold1, 1)
            dve.tensor_tensor(dif4, x8[:, :, 0:4], x8[:, :, 4:8], ALU.subtract).then_inc(fold1, 1)
            dve.wait_ge(fold1, 2)
            dve.tensor_tensor(ev2, sum4[:, :, 0:2], sum4[:, :, 2:4], ALU.add).then_inc(fold2, 1)
            dve.tensor_tensor(od2, sum4[:, :, 0:2], sum4[:, :, 2:4], ALU.subtract).then_inc(fold2, 1)
            dve.tensor_tensor(dd, dif4[:, :, 1], dif4[:, :, 3], ALU.subtract).then_inc(fold2, 1)
            dve.tensor_tensor(gg, dif4[:, :, 1], dif4[:, :, 3], ALU.add).then_inc(fold2, 1)
            dve.wait_ge(fold2, 4)
            dve.tensor_tensor(y[:, 0], ev2[:, :, 0], ev2[:, :, 1], ALU.add).then_inc(y_ready, 1)
            dve.tensor_tensor(y[:, 1], ev2[:, :, 0], ev2[:, :, 1], ALU.subtract).then_inc(y_ready, 1)
            for i, (pair, sign, rest) in enumerate(((dd, C8, 0), (dd, -C8, 0), (gg, C8, 2), (gg, -C8, 2))):
                dve.scalar_tensor_tensor(out=y[:, 2 + i], in0=pair, scalar=sign, in1=dif4[:, :, rest], op0=ALU.mult, op1=ALU.add).then_inc(y_ready, 1)
            spectrum(dve.tensor_copy, dve, 1, spec_ready_v)
            for i in range(3):
                cols = slice(FCH * i, FCH * (i + 1))
                dve.wait_ge(h_hi_ready, i + 1)
                dve.scalar_tensor_tensor(out=h_lo[:, cols], in0=bank[i][:, 0:FCH], scalar=pin_b[:], in1=h_hi[:, cols], op0=ALU.add, op1=ALU.subtract).then_inc(h_lo_ready, 1)

            dve.wait_ge(fourier_loaded, FOURIER_LOADS * 16)
            dve.wait_ge(router_done, 1)
            dve.tensor_tensor(logits[:], bank[3][:, 0:FT * E].rearrange("p (t e) -> p t e", e=E), router_b[:].unsqueeze(1).broadcast_to([P, FT, E]), ALU.add).then_inc(logits_ready, 1)
            dve.wait_ge(logits_ready, 1)
            for t in range(FT):
                dve.max(top8[:, t, :], logits[:, t, :]).then_inc(top_ready, 1)
            dve.wait_ge(top_ready, FT)
            dve.tensor_tensor(gap[:], top8[:, :, 1:2], top8[:, :, 0:1], ALU.subtract).then_inc(gap_ready, 1)
            for t in range(FT):
                dve.max_index(idx8[:, t, :], top8[:, t, :], logits[:, t, :]).then_inc(idx_ready, 1)
            dve.wait_ge(idx_ready, FT)
            dve.tensor_copy(choice[:], idx8[:, :, 0:2]).then_inc(route, 1)
            dve.wait_ge(odds_ready, 1)
            dve.tensor_scalar(odds1[:], odds[:], 1.0, None, ALU.add).then_inc(route, 1)
            dve.wait_ge(route, 2)
            dve.reciprocal(share[:, :, 0:1], odds1[:]).then_inc(route, 1)
            dve.wait_ge(route, 3)
            dve.tensor_tensor(share[:, :, 1:2], odds[:], share[:, :, 0:1], ALU.mult).then_inc(route, 1)
            dve.wait_ge(route, 4)

            def weights_of(chosen, shares, nt, to, sig, first, ready):
                numbers = expert_no[:].unsqueeze(1).broadcast_to([P, nt, E])
                for k in range(2):
                    dve.tensor_tensor(pick[k][:, 0:nt], numbers, chosen[:, :, k:k + 1].broadcast_to([P, nt, E]), ALU.is_equal).then_inc(sig, 1)
                for k in range(2):
                    dve.wait_ge(sig, first + k + 1)
                    dve.tensor_tensor(pick[k][:, 0:nt], pick[k][:, 0:nt], shares[:, :, k:k + 1].broadcast_to([P, nt, E]), ALU.mult).then_inc(sig, 1)
                dve.wait_ge(sig, first + 4)
                dve.tensor_tensor(to[:], pick[0][:, 0:nt], pick[1][:, 0:nt], ALU.add).then_inc(ready, 1)

            weights_of(choice[:], share[:], FT, wsel_f, route, 4, wsel_ready)
            for t in range(FT):
                dve.wait_ge(bias_done, t + 1)
                dve.tensor_copy(acc_f[:, t, :], bank[2 + 5 * (t % 2)][:, 0:D]).then_inc(acc_ready[0], 1)

            def accumulate(layer, e, nt, acc, wsel):
                for t in range(nt):
                    rows = 2 if layer == 0 and t == FT - 1 else P
                    dve.wait_ge(acc_ready[layer], e * nt + t + 1)
                    dve.wait_ge(expert_done[layer], e * nt + t + 1)
                    dve.scalar_tensor_tensor(out=acc[0:rows, t, :], in0=bank[2 + t % RING[layer]][0:rows, 0:D], scalar=wsel[0:rows, t, bass.ds(e, 1)], in1=acc[0:rows, t, :], op0=ALU.mult, op1=ALU.add).then_inc(acc_ready[layer], 1)

            dve.wait_ge(wsel_ready, 1)
            with dve.Fori(0, E) as e:
                accumulate(0, e, FT, acc_f, wsel_f)

            for i in range(4):
                dve.wait_ge(of_done, i + 1)
                for k in range(2):
                    which = 0 if i == 0 and k == 0 else 1
                    dve.tensor_tensor(of[:, 2 * i + k], bank[i][:, 256 * k:256 * (k + 1)].rearrange("p (b d) -> p b d", b=B), pout_b[:, which, :].unsqueeze(1).broadcast_to([P, B, D]), ALU.add).then_inc(of_ready, 1)
            for i in range(2, 4):
                dve.wait_ge(inv_done, i + 1)
                dve.tensor_copy(comb[:, 2 * i:2 * i + 2], bank[4 + i].rearrange("p (o b d) -> p o b d", o=2, b=B)).then_inc(comb_ready_v, 1)
            dve.wait_ge(comb_ready_a, 2)
            dve.wait_ge(comb_ready_v, 2)
            a0, a4, a1, b1_, a2, b2_, a3, b3_ = (comb[:, i] for i in range(8))
            for i, (u, v, op) in enumerate(((a0, a4, ALU.add), (a0, a4, ALU.subtract), (a1, a3, ALU.add), (b3_, b1_, ALU.subtract), (a1, a3, ALU.subtract), (b1_, b3_, ALU.add))):
                dve.tensor_tensor(inv[:, i], u, v, op).then_inc(unfold1, 1)
            dve.wait_ge(unfold1, 6)
            p0, m0, d0, d2, u0, v0 = (inv[:, i] for i in range(6))
            for i, (u, v, op) in enumerate(((p0, a2, ALU.add), (m0, b2_, ALU.subtract), (p0, a2, ALU.subtract), (m0, b2_, ALU.add), (u0, v0, ALU.subtract), (u0, v0, ALU.add))):
                dve.tensor_tensor(inv[:, 6 + i], u, v, op).then_inc(unfold2, 1)
            dve.wait_ge(unfold2, 6)
            e0, e1, e2, e3, d1, d3 = (inv[:, i] for i in range(6, 12))
            o8 = ot.rearrange("p (b j) d -> p b j d", b=B)
            for j, (even, odd, scale) in enumerate(((e0, d0, 1.0), (e1, d1, C8), (e2, d2, 1.0), (e3, d3, -C8))):
                dve.scalar_tensor_tensor(out=o8[:, :, j], in0=odd, scalar=scale, in1=even, op0=ALU.mult, op1=ALU.add).then_inc(ot_ready, 1)
                dve.scalar_tensor_tensor(out=o8[:, :, j + 4], in0=odd, scalar=-scale, in1=even, op0=ALU.mult, op1=ALU.add).then_inc(ot_ready, 1)
            dve.wait_ge(ot_ready, 8)
            statistics(4, ot)
            statistics(5, ot)
            normalise(4, ot, ot, ot_norm)
            normalise(5, ot, ot, ot_norm)
            dve.wait_ge(ot_norm, NT)
            dve.tensor_tensor(ot, ot, ln_g[:].unsqueeze(1).broadcast_to([P, NT, D]), ALU.mult).then_inc(ot_scaled, 1)
            dve.wait_ge(ot_scaled, 1)
            dve.wait_ge(base_f_ready, 2)
            dve.tensor_tensor(h[:], ot, base[:], ALU.add).then_inc(h2_ready, 1)

            dve.wait_ge(h2_ready, 1)
            statistics(6)
            statistics(7)
            normalise(6)
            normalise(7)
            low_features(2)
            low_features(3)
            for b in range(B):
                for j in range(TB):
                    t = b * TB + j
                    dve.wait_ge(pv2_done, t + 1)
                    dve.reciprocal(den2[:, t:t + 1], bank[4 + j % 2][:, D:D + 1]).then_inc(den2_ready, 1)
                    dve.wait_ge(den2_ready, t + 1)
                    dve.scalar_tensor_tensor(out=h[:, t, :], in0=bank[4 + j % 2][:, 0:D], scalar=den2[:, t:t + 1], in1=h[:, t, :], op0=ALU.mult, op1=ALU.add).then_inc(h3_ready, 1)

            dve.wait_ge(h3_ready, NT)
            statistics(8)
            normalise(8)
            low_features(4)
            dve.tensor_copy(gate_no[:], gate_i[:]).then_inc(gates, 1)
            dve.wait_ge(gates, 1)
            weights_of(gate_no[:], gate_w[:], TB, wsel_g, gates, 1, wsel_ready)
            for t in range(TB):
                dve.tensor_copy(acc_g[:, t, :], h[:, t, :]).then_inc(acc_ready[1], 1)
            dve.wait_ge(wsel_ready, 2)
            with dve.Fori(0, E) as e:
                accumulate(1, e, TB, acc_g, wsel_g)

        @block.tensor
        def _(pe):
            pe.wait_ge(seen_ready, 1)
            for i in range(4):
                half = i % 2
                pe.matmul(bank[i][0:N_FREQ, 0:272], dft64[:, i // 2, :], seen[:, 8 * half:8 * half + 8, :], start=True, stop=True).then_inc(dft_done, 1)
            pe.wait_ge(mag_ready, 1)
            pe.wait_ge(tok_loaded, 4 * 16)
            for v in range(VOCAB):
                mm = pe.matmul(bank[4][0:NFR, 0:D_STFT], mag[:, v, :], proj_w[:, v, :], start=(v == 0), stop=(v == VOCAB - 1))
            mm.then_inc(enc_done, 1)
            pe.wait_ge(tab_ready, 1)
            pe.wait_ge(sel_ready, 1)
            for t in range(NT):
                mm = pe.matmul(bank[t // 4][:, D * (t % 4):D * (t % 4 + 1)], tok_sel[:, P * t:P * (t + 1)], tok_tab, start=True, stop=True)
                if t % 4 == 3:
                    mm.then_inc(tok_done, 1)

            def product3(to, left, right, start=True, stop=True):
                pe.matmul(to, left[0], right[1], start=start, stop=False)
                pe.matmul(to, left[1], right[0], start=False, stop=False)
                return pe.matmul(to, left[0], right[0], start=False, stop=stop)

            def turn_rows(n, batch):
                for i in range(2):
                    if n >= 1:
                        pe.wait_ge(ln_lo_ready, 2 * n + i - 1)
                    for k in range(4):
                        t = (n % B) * TB + 4 * i + k
                        pe.wait_ge(ln_ready, TB * batch + 4 * i + k + 1)
                        mm = pe.transpose(bank[4 + i][:, P * k:P * (k + 1)], ln[:, t, :], ident[:])
                    mm.then_inc(turned, 1)

            pe.wait_ge(attn_loaded, 6 * 16)
            turn_rows(0, 0)
            turn_rows(1, 1)
            pe.wait_ge(h_ready, 4)
            pe.wait_ge(w_v_split, 2)
            for t in range(NT):
                pe.wait_ge(ln_lo_ready, t // 4 + 1)
                if t >= 4:
                    pe.wait_ge(v_ready, t - 3)
                product3(bank[t % 4][:], (ln_hi[:, P * t:P * (t + 1)], ln_lo[:, P * t:P * (t + 1)]), (w_v_hi, w_v_lo)).then_inc(v_done, 1)

            def project(hd, b, c, which):
                w, x = slice(P * which, P * (which + 1)), slice(b * L + HALF * c, b * L + HALF * (c + 1))
                return product3(pj[c][:], (w_head_hi[:, w], w_head_lo[:, w]), (ln_hi[:, x], ln_lo[:, x]))

            def project_q(hd, b, first=False):
                n = hd * B + b
                for c in range(2):
                    if not first:
                        pe.wait_ge(k_low, n * 2 + c - 1)
                    project(hd, b, c, 0).then_inc(q_done, 1)

            def project_k(hd, b, c):
                pe.wait_ge(q_low, (hd * B + b) * 2 + c + 1)
                project(hd, b, c, 1).then_inc(k_done, 1)

            def score_rows(hd, b, m, first=False):
                n = hd * B + b
                j, c, width = m_chunks[m]
                if m == 0:
                    pe.wait_ge(k_low, n * 2 + 2)
                if m == 0 and not first:
                    pe.wait_ge(max_row_ready, n)
                elif m >= 2 or not first:
                    pe.wait_ge(rows_used, n * NM + m - 1)
                to = sm[m % 2]
                on_diag = P * j < HALF * c + width and P * j >= HALF * c
                mm = pe.matmul(to[:, 0:width], query_hh[b][:, P * j:P * (j + 1)], key_hl[b][:, HALF * c:HALF * c + width], start=True, stop=not on_diag)
                if on_diag:
                    mm = pe.matmul(to[:, width - P:width], ident_b[:], mask_b[:], start=False, stop=True)
                mm.then_inc(rows_done, 1)

            def turn_maxima(hd, b):
                pe.wait_ge(max_ready, hd * B + b + 1)
                pe.transpose(sm[0][0:MAX_END, 0:P], max_cols[:], ident[:]).then_inc(max_turned, 1)

            def scores(hd, b, c):
                n = hd * B + b
                half, i, first, width = s_chunks[c]
                if c == 0:
                    pe.wait_ge(max_row_ready, n + 1)
                    pe.wait_ge(k_copied, n * 2 + 2)
                if c >= 2:
                    pe.wait_ge(probs_ready, n * NS + c - 1)
                to, on_diag = st[c % 2][:, 0:width], first == P * i
                keys, queries = slice(P * i, P * (i + 1)), slice(first, first + width)
                pe.matmul(to, key_h1[b][:, keys], query_lm[b][:, queries], start=True, stop=False)
                mm = pe.matmul(to, key_hl[b][:, keys], query_hh[b][:, queries], start=False, stop=not on_diag)
                if on_diag:
                    mm = pe.matmul(st[c % 2][:, 0:P], mask_b[:], ident_b[:], start=False, stop=True)
                mm.then_inc(scores_done, 1)

            def weigh(hd, b, j):
                n = hd * B + b
                half = j // 4
                if j == 0:
                    pe.wait_ge(v_head_ready, n + 1)
                if j % 4 == 0:
                    pe.wait_ge(o_ready[half], n + 1)
                c = chunk_of[half, j]
                pe.wait_ge(probs_ready, n * NS + c + 1)
                for i in range(j + 1):
                    c = chunk_of[half, i]
                    at = s_first[c] + P * j - s_chunks[c][2]
                    mm = pe.matmul(pv[half][:, VW * (j % 4):VW * (j % 4 + 1)], p_t[:, at:at + P], v_head[b][:, i, :], start=(i == 0), stop=(i == j))
                if j % 4 == 3:
                    mm.then_inc(pv_done[half], 1)

            def tensor_head(hd, b, last=False):
                nh, nb = hd + b, 1 - b

                def rows(*ms):
                    if not last:
                        for m in ms:
                            score_rows(nh, nb, m)

                if not last:
                    if b == 1:
                        pe.wait_ge(w_head_split, nh * 2 + 2)
                    project_q(nh, nb)
                scores(hd, b, 0)
                scores(hd, b, 1)
                weigh(hd, b, 0)
                scores(hd, b, 2)
                weigh(hd, b, 1)
                scores(hd, b, 3)
                if not last:
                    project_k(nh, nb, 0)
                weigh(hd, b, 2)
                scores(hd, b, 4)
                if not last:
                    project_k(nh, nb, 1)
                weigh(hd, b, 3)
                scores(hd, b, 5)
                scores(hd, b, 6)
                rows(0, 1)
                scores(hd, b, 7)
                rows(2)
                scores(hd, b, 8)
                rows(3)
                scores(hd, b, 9)
                rows(4)
                scores(hd, b, 10)
                rows(5)
                scores(hd, b, 11)
                rows(6, 7)
                weigh(hd, b, 4)
                rows(8, 9)
                weigh(hd, b, 5)
                rows(10, 11)
                weigh(hd, b, 6)
                if not last:
                    turn_maxima(nh, nb)
                weigh(hd, b, 7)

            pe.wait_ge(v_ready, NT)
            pe.wait_ge(w_head_split, 2)
            pe.wait_ge(pool_const, POOL_CONSTS)
            pe.wait_ge(consts_b, 2)
            project_q(0, 0, first=True)
            for c in range(2):
                project_k(0, 0, c)
            for c in range(2):
                pe.matmul(pv[c][:, 0:P], ident_b[:], ident_b[:], start=True, stop=True).then_inc(pv_done[c], 1)
            for m in range(NM):
                score_rows(0, 0, m, first=True)
            turn_maxima(0, 0)
            with pe.Fori(0, H - 1) as hd:
                tensor_head(hd, 0)
                tensor_head(hd, 1)
            tensor_head(H - 1, 0)
            tensor_head(H - 1, 1, last=True)

            def turn_heads(t):
                pe.wait_ge(o_ready[(t % TB) // 4], (H - 1) * B + t // TB + 2)
                if t >= 2:
                    pe.wait_ge(o_t_ready, t - 1)
                for k in range(4):
                    mm = pe.transpose(bank[t % 2][:, P * k:P * (k + 1)], o_all[:, t, P * k:P * (k + 1)], ident[:])
                mm.then_inc(o_turned, 1)

            turn_heads(0)
            for t in range(NT):
                if t + 1 < NT:
                    turn_heads(t + 1)
                pe.wait_ge(o_t_ready, t + 1)
                for k in range(4):
                    mm = pe.matmul(bank[4 + t // 4][:, D * (t % 4):D * (t % 4 + 1)], o_t[t % 2][:, P * k:P * (k + 1)], w_out[:, k, :], start=(k == 0), stop=(k == 3))
                mm.then_inc(out_done, 1)


            pe.wait_ge(h_ready, 8)
            pe.wait_ge(fourier_loaded, FOURIER_LOADS * 16)
            pe.wait_ge(y_ready, 6)
            for b in range(B):
                pe.matmul(bank[4 * b][:, 0:130], y[:, 0, b, :], fwd_single[:, 0:130], start=True, stop=True)
                pe.matmul(bank[4 * b][:, 256:384], y[:, 1, b, :], fwd_single[:, 130:258], start=True, stop=True).then_inc(spec_done, 1)
                for r, (re, im) in enumerate(((y[:, 2, b], y[:, 4, b]), (od2[:, b, 0], od2[:, b, 1]), (y[:, 3, b], y[:, 5, b]))):
                    pe.matmul(bank[4 * b + 1 + r][:, 0:256], re, fwd_pair[:, 2 * r, :], start=True, stop=False)
                    pe.matmul(bank[4 * b + 1 + r][:, 0:256], im, fwd_pair[:, 2 * r + 1, :], start=False, stop=True).then_inc(spec_done, 1)
            pe.wait_ge(spec_ready_a, 6)
            pe.wait_ge(spec_ready_v, 6)
            for i in range(3):
                cols = slice(FCH * i, FCH * (i + 1))
                pe.matmul(bank[i][:, 0:FCH], pin_w[:, 0, :], xf[:, 0, cols], start=True, stop=False)
                pe.matmul(bank[i][:, 0:FCH], pin_w[:, 1, :], xf[:, 1, cols], start=False, stop=True).then_inc(pin_done, 1)
            pe.wait_ge(h_lo_ready, 3)
            pe.wait_ge(pad_cleared, 2)
            for t in range(FT):
                rows = slice(P * t, P * (t + 1))
                pe.matmul(bank[3][:, E * t:E * (t + 1)], h_lo[:, rows].bitcast(F32), router_w[:], start=True, stop=False)
                mm = pe.matmul(bank[3][:, E * t:E * (t + 1)], h_hi[:, rows].bitcast(F32), router_w[:], start=False, stop=True)
            mm.then_inc(router_done, 1)
            def up(layer, e, i, g, first=False):
                c, k = g % FC, g // FC
                x_hi, x_lo = ((h_hi, h_lo), (ln_hi, ln_lo))[layer]
                if g == 0:
                    pe.wait_ge(w1_split, (e + layer * E) * 2 + 2)
                if g >= 2 or not first:
                    pe.wait_ge(hidden_ready[layer], e * GROUPS[layer] + g - 1)
                w, x = slice(P * c, P * (c + 1)), slice(COLS[layer] * k, COLS[layer] * (k + 1))
                product3(bank[g % 2][:, 0:COLS[layer]], (w1_hi[i][:, w], w1_lo[i][:, w]), (x_hi[:, x], x_lo[:, x])).then_inc(hidden_done[layer], 1)

            def down(layer, e, i, t):
                if t == 0:
                    pe.wait_ge(hidden_ready[layer], e * GROUPS[layer] + GROUPS[layer])
                    pe.wait_ge(w2_loaded[i], (e - i + layer * E) * 8 + 16)
                pe.wait_ge(acc_ready[layer], (e + 1) * TILES[layer] + t + 1 - RING[layer])
                hid = (hid_f if layer == 0 else hid_g)[i]
                rows = 2 if layer == 0 and t == FT - 1 else P
                for c in range(FC):
                    mm = pe.matmul(bank[2 + t % RING[layer]][0:rows, 0:D], hid[:, c, P * t:P * t + rows], w2[i][:, c, :], start=(c == 0), stop=(c == FC - 1))
                mm.then_inc(expert_done[layer], 1)

            def first_up(layer):
                for g in range(GROUPS[layer]):
                    up(layer, 0, 0, g, first=True)

            def experts(layer):
                def step(e, i, last=False):
                    for g in range(max(GROUPS[layer], TILES[layer])):
                        if g < GROUPS[layer] and not last:
                            up(layer, e + 1, 1 - i, g)
                        if g < TILES[layer]:
                            down(layer, e, i, g)

                with pe.Fori(0, E - 3, 2) as e:
                    step(e, 0)
                    step(e + 1, 1)
                step(E - 2, 0)
                step(E - 1, 1, last=True)

            first_up(0)
            pe.wait_ge(wsel_ready, 1)
            for t in range(FT):
                mm = pe.transpose(bank[4 + t // 4][0:E, P * (t % 4):P * (t % 4 + 1)], wsel_f[:, t, :], ident[:])
                if t % 4 == 3 or t == FT - 1:
                    mm.then_inc(wsel_turned, 1)
            pe.wait_ge(wsel_t_ready, 3)
            for t in range(FT):
                if t >= 2:
                    pe.wait_ge(acc_ready[0], t - 1)
                pe.matmul(bank[2 + 5 * (t % 2)][:, 0:D], wsel_t[:, P * t:P * (t + 1)], b2[:], start=True, stop=True).then_inc(bias_done, 1)
            pe.wait_ge(acc_ready[0], FT)

            experts(0)

            pe.wait_ge(acc_ready[0], FT * (E + 1))
            for t in range(FT):
                rows = 2 if t == FT - 1 else P
                mm = pe.transpose(bank[t // 4][:, P * (t % 4):P * (t % 4) + rows], acc_f[0:rows, t, :], ident[0:rows, 0:rows])
                if t % 4 == 3 or t == FT - 1:
                    mm.then_inc(moe_turned, 1)
            pe.wait_ge(moe_t_ready, 3)
            for r in range(RES):
                for b in range(B):
                    at = (r % 2) * B * D + b * D
                    rows = moe_t[:, (b * RES + r) * M64:(b * RES + r + 1) * M64]
                    pe.matmul(bank[r // 2][0:M64, at:at + D], rows, pout_w[:, 0, :], start=True, stop=True)
                    mm = pe.matmul(bank[r // 2][M64:P, at:at + D], rows, pout_w[:, 1, :], start=True, stop=True)
                    if r == 0:
                        mm = pe.matmul(bank[0][M64:M64 + 1, at:at + D], moe_t[:, NYQ + b:NYQ + b + 1], pout_w[:, 0, :], start=True, stop=True)
                if r % 2:
                    mm.then_inc(of_done, 1)

            pe.wait_ge(of_ready, 8)
            plan = [[(0, 0)], [(1, 4)]] + [[(2 + 4 * (r - 1) + 2 * k + s, (r, 8 - r)[s]) for s in range(2)] for r in range(1, 4) for k in range(2)]
            for o, terms in enumerate(plan):
                for n, (table, r) in enumerate(terms):
                    mm = pe.matmul(bank[4 + o // 2][:, 256 * (o % 2):256 * (o % 2 + 1)], inverse[:, table, :], of[:, r], start=(n == 0), stop=(n == len(terms) - 1))
                if o % 2:
                    mm.then_inc(inv_done, 1)

            pe.wait_ge(comb_ready_a, 2)
            pe.wait_ge(comb_ready_v, 2)
            turn_rows(2, 4)
            turn_rows(3, 5)

            def scores2(b, c):
                half, i = c // TB, c % TB
                if c >= 2 or b:
                    pe.wait_ge(probs2_ready, b * 2 * TB + c - 1)
                keys, queries = slice(b * L + P * i, b * L + P * (i + 1)), slice(b * L + HALF * half, b * L + HALF * (half + 1))
                product3(bank[c % 2][:], (ln_hi[:, keys], ln_lo[:, keys]), (ln_hi[:, queries], ln_lo[:, queries])).then_inc(scores2_done, 1)

            def weigh2(b, j):
                t = b * TB + j
                pe.wait_ge(probs2_ready, b * 2 * TB + TB * (j // 4 + 1))
                pe.wait_ge(z_ready, 2 * (b + 1))
                if j >= 2 or b:
                    pe.wait_ge(h3_ready, t - 1)
                for i in range(TB):
                    mm = pe.matmul(bank[4 + j % 2][:, 0:D + 1], p_2[b][:, i, P * j:P * (j + 1)], z_one[:, b * TB + i, 0:D + 1], start=(i == 0), stop=(i == TB - 1))
                mm.then_inc(pv2_done, 1)

            pe.wait_ge(ln_lo_ready, 8)
            for c in range(TB):
                scores2(0, c)
            for n in range(2 * B):
                b, half = n // 2, n % 2
                for k in range(TB):
                    if n + 1 < 2 * B:
                        scores2((n + 1) // 2, (n + 1) % 2 * TB + k)
                    if k % 2:
                        weigh2(b, 4 * half + k // 2)

            pe.wait_ge(h3_ready, NT)
            turn_rows(4, 6)
            pe.wait_ge(ln_lo_ready, 10)
            pe.wait_ge(acc_ready[1], TB)
            first_up(1)
            experts(1)


def frame_tables():
    w = np.arange(N_FFT)
    window = 0.5 - 0.5 * np.cos(2 * np.pi * w / N_FFT)
    angle = 2 * np.pi * np.outer(w, np.arange(N_FREQ)) / N_FFT
    return np.stack([window[:, None] * np.cos(angle), window[:, None] * -np.sin(angle)], 1).astype(np.float32)


def fourier_tables():
    p = np.arange(P)
    m = np.arange(M64)
    angle = lambda k: 2 * np.pi * np.outer(p, k) / L
    cos = lambda r: np.cos(angle(RES * m + r))
    sin = lambda r: np.sin(angle(RES * m + r))
    norm = 1 / np.sqrt(L)
    nyq = np.stack([(-1.0) ** p, 0 * p], 1)
    single = np.concatenate([cos(0), -sin(0), nyq, cos(4), -sin(4)], 1)
    pair = []
    for r in range(1, 4):
        q = RES - r
        s = 1.0 if r == 3 else -1.0
        pair.append(np.concatenate([cos(r), -sin(r), cos(q), -sin(q)], 1))
        pair.append(s * np.concatenate([sin(r), cos(r), -sin(q), -cos(q)], 1))
    weight = lambda r: np.where((m == 0) & (r == 0), 1.0, 2.0)

    def part_a(r):
        top, low = weight(r) * cos(r), -weight(r) * sin(r)
        if r == 0:
            low[:, 0] = nyq[:, 0]
        return np.concatenate([top, low], 1).T

    def part_b(r, sign):
        return sign * np.concatenate([weight(r) * sin(r), weight(r) * cos(r)], 1).T

    inv = [part_a(0), part_a(4)]
    for r in range(1, 4):
        inv += [part_a(r), part_a(RES - r), part_b(r, 1.0), part_b(RES - r, -1.0)]
    f = lambda v: np.ascontiguousarray(norm * v).astype(np.float32)
    return f(single), f(np.stack(pair, 1)), f(np.stack(inv, 1))


def constants():
    sel = np.zeros((NFR, B * L), np.float32)
    for b in range(B):
        l = np.arange(L)
        sel[b * N_FRAMES + l * N_FRAMES // L, b * L + l] = 1
    single, pair, inv = fourier_tables()
    return {
        "fwd_single": single, "fwd_pair": pair, "inverse": inv,
        "expert_no": np.tile(np.arange(E, dtype=np.float32), (P, 1)),
        "vocab_row": np.tile(np.arange(VOCAB, dtype=np.float32), (N_FFT, 1)),
        "vocab_col": (np.arange(P, dtype=np.float32) - VOCAB_AT)[:, None].copy(),
        "dft64": frame_tables(),
        "upsample": sel,
        "ident": np.eye(P, dtype=np.float32),
        "mask": np.triu(np.full((P, P), NEG, np.float32), 1),
    }


def layouts(x):
    c = np.ascontiguousarray
    ids = np.asarray(x["x"])
    pad = N_FFT // 2
    padded = np.pad(ids, ((0, 0), (pad, pad)), mode="reflect")
    frames = np.stack([padded[b, N_FFT * f:N_FFT * (f + 1)] for b in range(B) for f in range(N_FRAMES)], 1)
    w_in = np.asarray(x["L0_attn_W_in"]).reshape(D, H, 3, DK)
    b_in = np.asarray(x["L0_attn_b_in"]).reshape(H, 3, DK)
    w_qk = np.concatenate([w_in[:, :, part, :].transpose(1, 0, 2) for part in (0, 0, 1, 1)], 2)
    b_qk = np.concatenate([b_in[:, :2, :], b_in[:, :2, :]], 2).transpose(0, 2, 1)
    rows = lambda v: np.tile(np.asarray(v).reshape(1, -1), (P, 1))
    real, imag = np.asarray(x["L0_ffn_pout_b"]).reshape(2, D)
    pout_b = np.stack([np.stack([real] * (M64 + 1) + [imag] * (M64 - 1)), np.stack([real] * M64 + [imag] * M64)], 1)
    return {
        "ids_frames": c(frames),
        "ids_bcast": np.tile(ids.reshape(1, -1), (VOCAB, 1)),
        "proj_w": x["L0_tok_proj_w"],
        "proj_b": rows(x["L0_tok_proj_b"])[:NFR],
        "emb_table": x["L0_tok_emb_table"],
        "w_qk": c(w_qk), "b_qk": c(b_qk),
        "w_v": c(w_in[:, :, 2, :].reshape(D, H * DK)),
        "b_v": rows(b_in[:, 2, :]),
        "w_out": x["L0_attn_W_out"],
        "b_out": rows(x["L0_attn_b_out"]),
        "pin_w": x["L0_ffn_pin_w"], "pin_b": np.asarray(x["L0_ffn_pin_b"]).reshape(P, 1),
        "router_w": x["L0_ffn_router_w"], "router_b": rows(x["L0_ffn_router_b"]),
        "w1_f": x["L0_ffn_w1"], "w2_f": x["L0_ffn_w2"], "b2": x["L0_ffn_b2"],
        "b1_f": c(np.asarray(x["L0_ffn_b1"]).reshape(E, FC, P).transpose(0, 2, 1)),
        "pout_w": x["L0_ffn_pout_w"], "pout_b": pout_b,
        "ln_g": rows(x["L0_ffn_ln_g"]), "ln_b": rows(x["L0_ffn_ln_b"]),
        "gate_w": c(np.asarray(x["L1_ffn_expert_weights"]).reshape(TB, P, 2).transpose(1, 0, 2)),
        "gate_i": c(np.asarray(x["L1_ffn_expert_indices"]).reshape(TB, P, 2).transpose(1, 0, 2)),
        "w1_g": x["L1_ffn_w1"], "w2_g": x["L1_ffn_w2"],
    }


def kernel(**inputs):
    import concourse.bacc as bacc
    from concourse.bass_utils import run_bass_kernel_spmd

    nc = bacc.Bacc("TRN2", target_bir_lowering=False, num_devices=1)
    arrays = {k: np.ascontiguousarray(v) for k, v in (layouts(inputs) | constants()).items()}
    aps = {k: nc.dram_tensor("in_" + k, v.shape, mybir.dt.from_np(v.dtype), kind="ExternalInput").ap() for k, v in arrays.items()}
    out = nc.dram_tensor("hidden", (B * L, D), F32, kind="ExternalOutput").ap()
    tower(nc, aps, out)
    got = run_bass_kernel_spmd(nc, [{"in_" + k: v for k, v in arrays.items()}], core_ids=[0])
    return got.results[0]["hidden"].reshape(B, L, D)
```

```python
from contextlib import ExitStack

import numpy as np

import concourse.bass as bass
from concourse import mybir

P = 128
B, L, D = 2, 1024, 128
VOCAB, D_EMB, D_STFT = 16, 89, 39
N_FFT, N_FREQ, N_FRAMES = 64, 33, 17
NFR = B * N_FRAMES
H, DK = 8, 64
LN_EPS = 1e-5
TB = L // P
NT = B * TB
HALF = 512
VOCAB_AT = 64
SEL_K = VOCAB_AT + VOCAB
VW = 96
MAX_AT = 64
MAX_END = MAX_AT + TB
NEG = -1.0e9
E, FF = 8, 512
FC = FF // P
RES = 8
M64 = L // 2 // RES
NYQ = B * RES * M64
NF = NYQ + B
FT = 9
C8 = float(np.sqrt(0.5))
POOL_CONSTS = 12
FAST = 256
FIRST_LOW_AT = 8
DIVIDE_AT = 6
FOURIER_LOADS = 15
TILES = (FT, TB)
PARTS = (((0, HALF), (HALF, HALF // 2), (HALF * 3 // 2, NF - HALF * 3 // 2)), ((0, HALF), (HALF, HALF)))
GROUPS = (FC * 3, FC * 2)
UP_BANK = ((0, 1), (0, 1, 6, 7))
PIN_BANK = (2, 3, 2)
WSEL_BANK = (6, 7, 5)
MOE_BANK = (0, 1, 5)
OF_BANK = ((6, 7), (2, 3))
INV_BANK = ((0, 5), (6, 7))
ORDER = ((0, 1, 2, 3, 8, 4, 5, 6, 7), tuple(range(TB)))
EARLY = 5
ROUTER_AT = 384
RING = (3, 4)

F32 = mybir.dt.float32
F32R = mybir.dt.float32r
BF16 = mybir.dt.bfloat16
I32 = mybir.dt.int32
U32 = mybir.dt.uint32
ALU = mybir.AluOpType
ACT = mybir.ActivationFunctionType
AX = mybir.AxisListType


def max_chunks():
    return [(j, c, min(HALF, P * (j + 1) - HALF * c)) for j in range(TB) for c in range(2)
            if P * (j + 1) > HALF * c]


def score_chunks():
    out = []
    for half in range(2):
        for i in range(TB):
            first = max(P * i, HALF * half)
            if first < HALF * (half + 1):
                out.append((half, i, first, HALF * (half + 1) - first))
    return out


def tower(nc, a, out):
    m_chunks = max_chunks()
    s_chunks = score_chunks()
    NM, NS = len(m_chunks), len(s_chunks)
    s_first = [sum(c[3] for c in s_chunks[:n]) for n in range(NS + 1)]
    chunk_of = {(half, i): n for n, (half, i, _, _) in enumerate(s_chunks)}

    with ExitStack() as ctx:
        def sb(name, shape, dt=F32):
            return ctx.enter_context(nc.sbuf_tensor(name, shape, dt))

        def sem(name):
            return ctx.enter_context(nc.semaphore(name))

        bank = [ctx.enter_context(nc.psum_tensor(f"bank{i}", [P, HALF], F32)) for i in range(8)]

        h = sb("h", [P, NT, D])
        ln = sb("ln", [P, NT, D])
        ln_hi = sb("ln_hi", [P, B * L], F32R)
        ln_lo = sb("ln_lo", [P, B * L], F32R)
        base = sb("base", [P, NT, D])
        ident = sb("ident", [P, P])
        stats = sb("stats", [P, NT, 6])
        mv = sb("mv", [P, NT, 2])
        var_eps = sb("var_eps", [P, NT])
        minus_half = sb("minus_half", [P, NT])
        zero = sb("zero", [P, 1])
        one = sb("one", [P, 1])
        gate = sb("gate", [P, 1])
        rstd = sb("rstd", [P, NT])

        ARENA = 22528
        arena = sb("arena", [P, ARENA])

        def part(first, *shape, rows=slice(0, P)):
            n = int(np.prod(shape))
            assert first + n <= ARENA, (first, shape)
            view = arena[rows, first:first + n]
            if len(shape) == 2:
                view = view.rearrange("p (a b) -> p a b", b=shape[1])
            if len(shape) == 3:
                view = view.rearrange("p (a b c) -> p a b c", b=shape[1], c=shape[2])
            return view

        arena_r = sb("arena_r", [P, 8 * L], F32R)

        v_all = part(0, NT, H * DK)
        o_all = part(8192, NT, H * DK)
        p_t = part(16384, s_first[NS])
        v_head = [part(20992 + 768 * i, TB, VW) for i in range(2)]
        query_hh = [arena_r[:, L * i:L * (i + 1)] for i in range(0, 2)]
        query_lm = [arena_r[:, L * i:L * (i + 1)] for i in range(2, 4)]
        key_hl = [arena_r[:, L * i:L * (i + 1)] for i in range(4, 6)]
        key_h1 = [arena_r[:, L * i:L * (i + 1)] for i in range(6, 8)]
        o_t = [part(16384 + 512 * i, HALF) for i in range(2)]
        tok_sel = part(8192, B * L)
        tok_tab = part(10240, D)
        seen = part(10368, VOCAB, NFR, rows=slice(0, N_FFT))
        re_sq = part(10912, VOCAB * NFR, rows=slice(0, N_FREQ))
        im_sq = part(11456, VOCAB * NFR, rows=slice(0, N_FREQ))
        mag = part(12000, VOCAB, NFR, rows=slice(0, N_FREQ))
        proj_w = part(12544, VOCAB, D_STFT, rows=slice(0, N_FREQ))
        proj_b = part(13184, D_STFT, rows=slice(0, NFR))
        dft64 = part(13248, 2, N_FREQ, rows=slice(0, N_FFT))
        w_v = part(16384, H * DK)
        b_v = part(16896, 4, P)
        mask_f = part(17408, P)
        ids_i = part(14016, B * L, rows=slice(VOCAB_AT, SEL_K)).bitcast(I32)
        frames_i = part(16064, NFR, rows=slice(0, N_FFT)).bitcast(I32)

        vocab_row = sb("vocab_row", [N_FFT, VOCAB])
        vocab_col = sb("vocab_col", [P, 1])
        w_head = sb("w_head", [P, P])
        w_head_hi = sb("w_head_hi", [P, P], F32R)
        w_head_lo = sb("w_head_lo", [P, P], F32R)
        b_head = sb("b_head", [P, 1])
        k_high_up = sb("k_high_up", [P, L], F32R)
        max_cols = sb("max_cols", [P, MAX_END])
        w_out = sb("w_out", [P, 4, D])
        b_out = sb("b_out", [P, D])
        mask_b = sb("mask_b", [P, P], BF16)
        ident_b = sb("ident_b", [P, P], BF16)
        max_part = sb("max_part", [P, TB])
        o_scale = sb("o_scale", [P, TB])

        y = part(0, 6, B, D)
        sum4 = part(1536, B, 4, D)
        dif4 = part(2560, B, 4, D)
        ev2 = part(3584, B, 2, D)
        od2 = part(4096, B, 2, D)
        dd = part(4608, B, D)
        gg = part(4864, B, D)
        xf = part(5632, 2, NF)
        h_hi = arena_r[:, 0:FT * P]
        h_lo = arena_r[:, FT * P:2 * FT * P]
        hid_f = [part(8840 + 4104 * i, FC, NF) for i in range(2)]
        acc_f = part(17048, FT, D)
        moe_t = part(18200, FT * P)
        wsel_t = part(19352, FT * P, rows=slice(0, E))
        of = part(0, B, RES, D)
        comb = part(8192, B, 8, D)
        ot = part(10240, NT, D)
        inv = part(12288, 12, B, D)
        p_2 = [part(8192 * i, TB, L) for i in range(2)]
        z_one = part(16384, NT, 130)
        hid_g = [part(4096 * i, FC, L) for i in range(2)]
        acc_g = part(18464, TB, D)

        fwd_single = sb("fwd_single", [P, 258])
        fwd_pair = sb("fwd_pair", [P, 6, 256])
        inverse = sb("inverse", [P, 14, P])
        w1 = [sb(f"w1_{i}", [P, FF]) for i in range(2)]
        w1_hi = [sb(f"w1_hi_{i}", [P, FF], F32R) for i in range(2)]
        w1_lo = [sb(f"w1_lo_{i}", [P, FF], F32R) for i in range(2)]
        w_v_hi, w_v_lo = w1_hi[0][:], w1_lo[0][:]
        w2 = [sb(f"w2_{i}", [P, FC, D]) for i in range(2)]
        b1 = [sb(f"b1_{i}", [P, FC]) for i in range(2)]
        pin_w = sb("pin_w", [P, 2, D])
        pin_b = sb("pin_b", [P, 1])
        router_w = sb("router_w", [P, E])
        router_b = sb("router_b", [P, E])
        b2 = sb("b2", [E, D])
        pout_w = sb("pout_w", [P, 2, D])
        pout_b = sb("pout_b", [P, 2, D])
        ln_g = sb("ln_g", [P, D])
        ln_b = sb("ln_b", [P, D])
        expert_no = sb("expert_no", [P, E])
        logits = sb("logits", [P, FT, E])
        top8 = sb("top8", [P, FT, 8])
        idx8 = sb("idx8", [P, FT, 8], U32)
        choice = sb("choice", [P, FT, 2])
        gap = sb("gap", [P, FT, 1])
        odds = sb("odds", [P, FT, 1])
        euler = sb("euler", [P, FT, 1])
        odds1 = sb("odds1", [P, FT, 1])
        share = sb("share", [P, FT, 2])
        pick = [sb(f"pick{i}", [P, FT, E]) for i in range(2)]
        wsel_f = sb("wsel_f", [P, FT, E])
        gate_w = sb("gate_w", [P, TB, 2])
        gate_i = sb("gate_i", [P, TB, 2], I32)
        gate_no = sb("gate_no", [P, TB, 2])
        wsel_g = sb("wsel_g", [P, TB, E])
        minus_shift = sb("minus_shift", [P, 1])
        den2 = sb("den2", [P, NT])

        ids_loaded = sem("ids_loaded")
        tok_loaded = sem("tok_loaded")
        attn_loaded = sem("attn_loaded")
        w_head_loaded = sem("w_head_loaded")
        pool_const = sem("pool_const")
        zero_ready = sem("zero_ready")
        tok_cleared = sem("tok_cleared")
        seen_ready = sem("seen_ready")
        dft_done = sem("dft_done")
        squares = sem("squares")
        power_ready = sem("power_ready")
        mag_ready = sem("mag_ready")
        enc_done = sem("enc_done")
        tab_ready = sem("tab_ready")
        sel_ready = sem("sel_ready")
        tok_done = sem("tok_done")
        h_ready = sem("h_ready")
        stats_done = sem("stats_done")
        mean_done = sem("mean_done")
        var_ready = sem("var_ready")
        rstd_ready = sem("rstd_ready")
        ln_ready = sem("ln_ready")
        turned = sem("turned")
        ln_hi_ready = sem("ln_hi_ready")
        ln_lo_ready = sem("ln_lo_ready")
        consts_b = sem("consts_b")
        v_done = sem("v_done")
        v_ready = sem("v_ready")
        v_head_ready = sem("v_head_ready")
        qk_done = sem("qk_done")
        q_high = sem("q_high")
        q_low = sem("q_low")
        k_high = sem("k_high")
        k_low = sem("k_low")
        gate_passed = sem("gate_passed")
        q_moved = sem("q_moved")
        k_moved = sem("k_moved")
        k_moved_h1 = sem("k_moved_h1")
        w_v_split = sem("w_v_split")
        w_head_split = sem("w_head_split")
        rows_done = sem("rows_done")
        rows_used = sem("rows_used")
        max_ready = sem("max_ready")
        max_turned = sem("max_turned")
        max_row_ready = sem("max_row_ready")
        scores_done = sem("scores_done")
        probs_ready = sem("probs_ready")
        pv_done = [sem("pv_done0"), sem("pv_done1")]
        den_ready = [sem("den_ready0"), sem("den_ready1")]
        o_ready = [sem("o_ready0"), sem("o_ready1")]
        b_v_out_done = sem("b_v_out_done")
        b_out_ready = sem("b_out_ready")
        base_ready = sem("base_ready")
        o_turned = sem("o_turned")
        o_t_ready = sem("o_t_ready")
        out_done = sem("out_done")
        stored = sem("stored")
        fourier_loaded = sem("fourier_loaded")
        pad_cleared = sem("pad_cleared")
        base_f_ready = sem("base_f_ready")
        fold1 = sem("fold1")
        fold2 = sem("fold2")
        y_ready = sem("y_ready")
        spec_done = sem("spec_done")
        spec_ready_a = sem("spec_ready_a")
        spec_ready_v = sem("spec_ready_v")
        pin_done = sem("pin_done")
        h_hi_ready = sem("h_hi_ready")
        h_lo_ready = sem("h_lo_ready")
        router_done = sem("router_done")
        logits_ready = sem("logits_ready")
        top_ready = sem("top_ready")
        idx_ready = sem("idx_ready")
        gap_ready = sem("gap_ready")
        odds_ready = sem("odds_ready")
        route = sem("route")
        wsel_ready = sem("wsel_ready")
        wsel_turned = sem("wsel_turned")
        wsel_t_ready = sem("wsel_t_ready")
        moe_turned = sem("moe_turned")
        moe_t_ready = sem("moe_t_ready")
        of_done = sem("of_done")
        of_ready = sem("of_ready")
        inv_done = sem("inv_done")
        comb_ready_a = sem("comb_ready_a")
        comb_ready_v = sem("comb_ready_v")
        unfold1 = sem("unfold1")
        unfold2 = sem("unfold2")
        ot_ready = sem("ot_ready")
        ot_scaled = sem("ot_scaled")
        h2_ready = sem("h2_ready")
        w1_loaded = [sem("w1_loaded0"), sem("w1_loaded1")]
        w2_loaded = [sem("w2_loaded0"), sem("w2_loaded1")]
        b1_loaded = [sem("b1_loaded0"), sem("b1_loaded1")]
        w1_split = sem("w1_split")
        hidden_done = [sem("hidden_done0"), sem("hidden_done1")]
        hidden_ready = [sem("hidden_ready0"), sem("hidden_ready1")]
        expert_done = [sem("expert_done0"), sem("expert_done1")]
        acc_ready = [sem("acc_ready0"), sem("acc_ready1")]
        z_ready = sem("z_ready")
        scores2_done = sem("scores2_done")
        probs2_ready = sem("probs2_ready")
        pv2_done = sem("pv2_done")
        den2_ready = sem("den2_ready")
        h3_ready = sem("h3_ready")
        gates = sem("gates")

        def v_bank(t):
            return ((2, 3, 6, 7), (4, 5, 6, 7))[t // TB][t % 4]

        def turn_bank(n, i):
            return bank[(4 if n <= B else 6) + i]

        pj, sm, st, pv = bank[0:2], bank[2:4], bank[4:6], bank[6:8]

        def spectrum(copy, eng, b, ready):
            grouped = xf[:, :, 0:NYQ].rearrange("p c (g m) -> p c g m", m=M64)
            eng.wait_ge(spec_done, 4 * b + 1)
            copy(grouped[:, :, b * RES, :], bank[4 * b][:, 0:2 * M64].rearrange("p (c m) -> p c m", c=2)).then_inc(ready, 1)
            copy(grouped[:, :, b * RES + 4, :], bank[4 * b][:, 256:256 + 2 * M64].rearrange("p (c m) -> p c m", c=2)).then_inc(ready, 1)
            copy(xf[:, :, NYQ + b:NYQ + b + 1], bank[4 * b][:, 2 * M64:2 * M64 + 2].unsqueeze(2)).then_inc(ready, 1)
            for r in range(1, 4):
                eng.wait_ge(spec_done, 4 * b + r + 1)
                pair = grouped[:, :, b * RES + r:b * RES + 9 - r:8 - 2 * r, :]
                copy(pair, bank[4 * b + r][:, 0:4 * M64].rearrange("p (k c m) -> p c k m", k=2, c=2)).then_inc(ready, 1)

        block = ctx.enter_context(nc.Block())

        @block.sync
        def _(sp):
            sp.dma_start(frames_i, a["ids_frames"]).then_inc(ids_loaded, 16)
            sp.dma_start(vocab_row[:], a["vocab_row"]).then_inc(ids_loaded, 16)
            sp.dma_start(dft64, a["dft64"]).then_inc(ids_loaded, 16)
            sp.dma_start(ids_i, a["ids_bcast"]).then_inc(ids_loaded, 16)
            sp.dma_start(vocab_col[:], a["vocab_col"]).then_inc(ids_loaded, 16)
            sp.dma_start(proj_w, a["proj_w"].rearrange("(f v) o -> f v o", v=VOCAB)).then_inc(tok_loaded, 16)
            sp.dma_start(proj_b, a["proj_b"]).then_inc(tok_loaded, 16)
            sp.wait_ge(tok_cleared, 2)
            sp.dma_start(tok_tab[VOCAB_AT:SEL_K, 0:D_EMB], a["emb_table"]).then_inc(tok_loaded, 16)
            sp.dma_start(tok_sel[0:NFR, :], a["upsample"]).then_inc(tok_loaded, 16)
            sp.dma_start(ident[:], a["ident"]).then_inc(attn_loaded, 16)
            sp.dma_start(mask_f, a["mask"]).then_inc(attn_loaded, 16)
            sp.dma_start(w_v, a["w_v"]).then_inc(attn_loaded, 16)
            sp.dma_start(b_v, a["b_v"]).then_inc(attn_loaded, 16)
            sp.dma_start(w_out[:], a["w_out"].rearrange("(c p) d -> p c d", p=P)).then_inc(attn_loaded, 16)
            sp.dma_start(b_out[:], a["b_out"]).then_inc(attn_loaded, 16)
            sp.dma_start(w_head[:], a["w_qk"][0]).then_inc(w_head_loaded, 16)
            sp.dma_start(b_head[:], a["b_qk"][0]).then_inc(w_head_loaded, 16)
            for to, name in ((fwd_single[:], "fwd_single"), (fwd_pair[:], "fwd_pair"), (inverse[:], "inverse"),
                             (pin_b[:], "pin_b"), (router_w[:], "router_w"), (router_b[:], "router_b"), (b2[:], "b2"),
                             (pout_b[:], "pout_b"), (ln_g[:], "ln_g"), (ln_b[:], "ln_b"), (expert_no[:], "expert_no"),
                             (gate_w[:], "gate_w"), (gate_i[:], "gate_i")):
                sp.dma_start(to, a[name]).then_inc(fourier_loaded, 16)
            sp.dma_start(pin_w[:], a["pin_w"].rearrange("(c p) d -> p c d", p=P)).then_inc(fourier_loaded, 16)
            sp.dma_start(pout_w[:], a["pout_w"].rearrange("p (c d) -> p c d", d=D)).then_inc(fourier_loaded, 16)

            with sp.Fori(0, H - 1) as hd:
                sp.wait_ge(w_head_split, hd * 2 + 2)
                sp.dma_start(w_head[:], a["w_qk"][bass.ds(hd + 1, 1)].rearrange("o p n -> (o p) n")).then_inc(w_head_loaded, 16)
                sp.wait_ge(q_low, hd * 4 + 4)
                sp.wait_ge(k_low, hd * 4 + 4)
                sp.dma_start(b_head[:], a["b_qk"][bass.ds(hd + 1, 1)].rearrange("o p n -> (o p) n")).then_inc(w_head_loaded, 16)

            def load_w1(layer, e, i):
                sp.dma_start(w1[i][:], a[("w1_f", "w1_g")[layer]][bass.ds(e, 1)].rearrange("o d f -> (o d) f")).then_inc(w1_loaded[i], 16)

            def load_w2(layer, e, i):
                sp.dma_start(w2[i][:], a[("w2_f", "w2_g")[layer]][bass.ds(e, 1)].rearrange("o (c p) d -> (o p) c d", p=P)).then_inc(w2_loaded[i], 16)

            def load_b1(e, i):
                sp.dma_start(b1[i][:], a["b1_f"][bass.ds(e, 1)].rearrange("o p c -> (o p) c")).then_inc(b1_loaded[i], 16)

            for i in range(2):
                load_w1(0, i, i)
                load_b1(i, i)
                load_w2(0, i, i)
            with sp.Fori(0, E - 3, 2) as e:
                for i in range(2):
                    sp.wait_ge(w1_split, (e + i) * 2 + 2)
                    load_w1(0, e + i + 2, i)
                    sp.wait_ge(hidden_ready[0], (e + i) * GROUPS[0] + GROUPS[0])
                    load_b1(e + i + 2, i)
                    sp.wait_ge(expert_done[0], (e + i) * TILES[0] + TILES[0])
                    load_w2(0, e + i + 2, i)
            for i in range(2):
                sp.wait_ge(w1_split, (E - 2 + i) * 2 + 2)
                load_w1(1, i, i)
                sp.wait_ge(expert_done[0], (E - 1 + i) * TILES[0])
                load_w2(1, i, i)
            for e in range(E - 2):
                sp.wait_ge(w1_split, (E + e) * 2 + 2)
                load_w1(1, e + 2, e % 2)
                if e == 0:
                    sp.wait_ge(h3_ready, NT)
                    sp.dma_start(out[L:, :].rearrange("(t p) d -> p t d", p=P), h[:, TB:, :]).then_inc(stored, 16)
                sp.wait_ge(expert_done[1], e * TILES[1] + TILES[1])
                load_w2(1, e + 2, e % 2)
            sp.wait_ge(acc_ready[1], TB * (E + 1))
            sp.dma_start(out[0:L, :].rearrange("(t p) d -> p t d", p=P), acc_g).then_inc(stored, 16)
            sp.wait_ge(stored, 2 * 16)

        @block.gpsimd
        def _(pool):
            pool.memset(tok_sel[32:VOCAB_AT, :], 0.0).then_inc(tok_cleared, 1)
            pool.wait_ge(tok_cleared, 1)
            pool.memset(tok_tab, 0.0).then_inc(tok_cleared, 1)
            pool.wait_ge(tok_cleared, 2)
            pool.memset(tok_sel[VOCAB_AT:P, :], 0.0).then_inc(tok_cleared, 1)
            pool.wait_ge(tok_cleared, 3)
            pool.memset(zero[:], 0.0).then_inc(zero_ready, 1)
            pool.wait_ge(zero_ready, 1)
            pool.memset(one[:], 1.0).then_inc(zero_ready, 1)
            pool.wait_ge(zero_ready, 2)

            def fill(to, rows, value, width):
                n = rows.stop - rows.start
                return pool.tensor_tensor(to[rows, :], value[rows, :].broadcast_to([n, width]), zero[rows, :].broadcast_to([n, width]), ALU.add)

            pool.memset(minus_half[:], -0.5).then_inc(pool_const, 1)
            pool.wait_ge(pool_const, 1)
            pool.memset(max_cols[:], 0.0).then_inc(pool_const, 1)
            for i in range(2):
                first = 5 * i + 2
                pool.wait_ge(pool_const, first)
                fill(query_lm[i], slice(DK, P), zero, L).then_inc(pool_const, 1)
                pool.wait_ge(pool_const, first + 1)
                fill(key_h1[i], slice(DK, P), zero, L).then_inc(pool_const, 1)
                pool.wait_ge(pool_const, first + 2)
                fill(key_h1[i], slice(MAX_AT, MAX_END), one, L).then_inc(pool_const, 1)
                pool.wait_ge(pool_const, first + 3)
                pool.memset(v_head[i][:, :, DK + 1:VW], 0.0).then_inc(pool_const, 1)
                pool.wait_ge(pool_const, first + 4)
                pool.memset(v_head[i][:, :, DK:DK + 1], 1.0).then_inc(pool_const, 1)

            def inverse_roots(n, b):
                pool.wait_ge(var_ready, n + 1)
                tiles = slice(b * TB, (b + 1) * TB)
                pool.tensor_tensor(rstd[:, tiles], var_eps[:, tiles], minus_half[:, tiles], ALU.pow).then_inc(rstd_ready, 1)

            def split_head(hd=0):
                pool.wait_ge(w_head_loaded, hd * 32 + 32)
                pool.tensor_tensor(w_head_hi[:], w_head[:], zero[:].broadcast_to([P, P]), ALU.add).then_inc(w_head_split, 1)
                pool.wait_ge(w_head_split, hd * 2 + 1)
                pool.tensor_tensor(w_head_lo[:], w_head[:], w_head_hi[:], ALU.subtract).then_inc(w_head_split, 1)

            pool.wait_ge(attn_loaded, 6 * 16)
            pool.tensor_copy(w_v_hi, w_v).then_inc(w_v_split, 1)
            pool.wait_ge(w_v_split, 1)
            pool.tensor_tensor(w_v_lo, w_v, w_v_hi, ALU.subtract).then_inc(w_v_split, 1)
            split_head()
            inverse_roots(0, 0)
            inverse_roots(1, 1)
            def copy_values(hd, b):
                pool.tensor_copy(v_head[b][:, :, 0:DK], v_all[:, b * TB:(b + 1) * TB, bass.ds(hd * DK, DK)]).then_inc(v_head_ready, 1)

            def next_values(hd, b):
                pool.wait_ge(pv_done[1], hd * B + b + 1)
                copy_values(hd + b, 1 - b)

            def passed(sig, count, n, i, first=False):
                if not first:
                    pool.wait_ge(gate_passed, n * 2 + i)
                pool.wait_ge(sig, count)
                pool.tensor_tensor(gate[:], zero[:], zero[:], ALU.add).then_inc(gate_passed, 1)

            def move_parts(hd, b, first=False):
                n = hd * B + b
                passed(q_high, n * 2 + 2, n, 0, first)
                pool.dma_start(query_hh[b][DK:P, :], query_hh[b][0:DK, :]).then_inc(q_moved, 16)
                passed(k_high, n * 2 + 2, n, 1)
                pool.dma_start(key_hl[b][0:DK, :], k_high_up[DK:P, :]).then_inc(k_moved, 16)
                pool.dma_start(key_h1[b][0:DK, :], k_high_up[DK:P, :]).then_inc(k_moved_h1, 16)

            move_parts(0, 0, first=True)
            move_parts(0, 1)
            pool.wait_ge(v_ready, NT)
            copy_values(0, 0)
            pool.wait_ge(ln_ready, NT)
            pool.tensor_tensor(base[:], h[:], ln[:], ALU.add).then_inc(base_ready, 1)
            pool.wait_ge(base_ready, 1)
            pool.wait_ge(b_out_ready, 1)
            pool.tensor_tensor(base[:], base[:], b_out[:].unsqueeze(1).broadcast_to([P, NT, D]), ALU.add).then_inc(base_ready, 1)
            with pool.Fori(0, H - 1) as hd:
                next_values(hd, 0)
                pool.wait_ge(qk_done, hd * 4 + 4)
                split_head(hd=hd + 1)
                move_parts(hd + 1, 0)
                next_values(hd, 1)
                move_parts(hd + 1, 1)
            next_values(H - 1, 0)

            def split_w1(n, i):
                pool.wait_ge(w1_loaded[i], (n - i) * 8 + 16)
                pool.tensor_tensor(w1_hi[i][:], w1[i][:], zero[:].broadcast_to([P, FF]), ALU.add).then_inc(w1_split, 1)
                pool.wait_ge(w1_split, n * 2 + 1)
                pool.tensor_tensor(w1_lo[i][:], w1[i][:], w1_hi[i][:], ALU.subtract).then_inc(w1_split, 1)

            for i in range(2):
                split_w1(i, i)
            inverse_roots(2, 0)
            inverse_roots(3, 1)
            fill(h_hi[:, NF:FT * P], slice(0, P), zero, FT * P - NF).then_inc(pad_cleared, 1)
            pool.wait_ge(pad_cleared, 1)
            fill(h_lo[:, NF:FT * P], slice(0, P), zero, FT * P - NF).then_inc(pad_cleared, 1)
            pool.wait_ge(pad_cleared, 2)
            pool.memset(minus_shift[:], -D / 2).then_inc(pad_cleared, 1)
            pool.wait_ge(pad_cleared, 3)
            pool.memset(euler[:], float(np.e)).then_inc(pad_cleared, 1)
            pool.wait_ge(pad_cleared, 4)
            pool.wait_ge(gap_ready, 1)
            pool.tensor_tensor(odds[:], euler[:], gap[:], ALU.pow).then_inc(odds_ready, 1)
            pool.wait_ge(ln_ready, 2 * NT)
            pool.wait_ge(fourier_loaded, FOURIER_LOADS * 16)
            pool.tensor_tensor(base[:], h[:], ln[:], ALU.add).then_inc(base_f_ready, 1)
            pool.wait_ge(base_f_ready, 1)
            pool.tensor_tensor(base[:], base[:], ln_b[:].unsqueeze(1).broadcast_to([P, NT, D]), ALU.add).then_inc(base_f_ready, 1)

            with pool.Fori(0, E - 3, 2) as e:
                for i in range(2):
                    pool.wait_ge(hidden_done[0], (e + i) * GROUPS[0] + GROUPS[0])
                    split_w1(e + i + 2, i)

            for i in range(2):
                pool.wait_ge(hidden_done[0], (E - 1 + i) * GROUPS[0])
                split_w1(E + i, i)

            for b in range(B):
                inverse_roots(4 + 2 * b, b)
                inverse_roots(5 + 2 * b, b)
                tiles = slice(b * TB, (b + 1) * TB)
                pool.wait_ge(ln_ready, 2 * NT + (b + 1) * TB)
                if b:
                    pool.wait_ge(z_ready, 2)
                pool.tensor_copy(z_one[:, tiles, 0:D], ln[:, tiles, :]).then_inc(z_ready, 1)
                pool.wait_ge(z_ready, 2 * b + 1)
                pool.memset(z_one[:, tiles, D:D + 1], 1.0).then_inc(z_ready, 1)
            inverse_roots(8, 0)
            with pool.Fori(0, E - 3, 2) as e:
                for i in range(2):
                    pool.wait_ge(hidden_done[1], (e + i) * GROUPS[1] + GROUPS[1])
                    split_w1(e + i + (E + 2), i)

        @block.scalar
        def _(act):
            for i in range(4):
                act.wait_ge(dft_done, i + 1)
                half = i % 2
                to = (re_sq, im_sq)[i // 2][:, half * 272:(half + 1) * 272]
                act.activation(to, bank[i][0:N_FREQ, 0:272], ACT.Square).then_inc(squares, 1)
            act.wait_ge(power_ready, 1)
            act.activation(mag.rearrange("p v n -> p (v n)"), re_sq, ACT.Sqrt).then_inc(mag_ready, 1)
            for i in range(4):
                act.wait_ge(tok_done, i + 1)
                act.copy(h[:, 4 * i:4 * i + 4, :], bank[i].rearrange("p (t d) -> p t d", d=D)).then_inc(h_ready, 1)

            def features_down(n, b):
                for i in range(2):
                    act.wait_ge(turned, 2 * n + i + 1)
                    first = b * L + HALF * i
                    act.copy(ln_hi[:, first:first + HALF], turn_bank(n, i)[:]).then_inc(ln_hi_ready, 1)

            def copy_v(t):
                act.wait_ge(v_done, t + 1)
                act.copy(v_all[:, t, :], bank[v_bank(t)][:]).then_inc(v_ready, 1)


            def queries_keys(hd, b, c, first=False):
                n = hd * B + b
                cols = slice(HALF * c, HALF * (c + 1))
                act.wait_ge(qk_done, n * 2 + c + 1)
                act.activation(query_hh[b][0:DK, cols], pj[c][0:DK, :], ACT.Identity, bias=b_head[0:DK, :]).then_inc(q_high, 1)
                if not first and c == 0:
                    act.wait_ge(k_moved, n * 16)
                    act.wait_ge(k_moved_h1, n * 16)
                act.activation(k_high_up[DK:P, cols], pj[c][DK:P, :], ACT.Identity, bias=b_head[DK:P, :]).then_inc(k_high, 1)

            def exp_head(hd, b, last=False):
                n = hd * B + b
                for c, (half, i, first, width) in enumerate(s_chunks):
                    if c == 0 or s_chunks[c - 1][0] != half:
                        act.wait_ge(pv_done[half], n + 1)
                    act.wait_ge(scores_done, n * NS + c + 1)
                    before = max(FAST - width, 0)
                    act.activation(p_t[:, s_first[c]:s_first[c] + width], st[c % 2][:, before:before + width], ACT.Exp, scale=DK ** -0.5).then_inc(probs_ready, 1)
                if not last:
                    for c in range(2):
                        queries_keys(hd + 1, b, c)

            features_down(0, 0)
            act.wait_ge(w_head_loaded, 32)
            act.wait_ge(pool_const, POOL_CONSTS)
            for c in range(2):
                queries_keys(0, 0, c, first=True)
            for t in range(TB):
                copy_v(t)
            features_down(1, 1)
            for c in range(2):
                queries_keys(0, 1, c)
            for t in range(TB, NT):
                copy_v(t)
            with act.Fori(0, H - 1) as hd:
                exp_head(hd, 0)
                exp_head(hd, 1)
            exp_head(H - 1, 0, last=True)
            exp_head(H - 1, 1, last=True)

            for t in range(NT):
                act.wait_ge(o_turned, t + 1)
                if t >= 2:
                    act.wait_ge(out_done, t - 1)
                act.copy(o_t[t % 2], bank[t % 2][:]).then_inc(o_t_ready, 1)

            act.wait_ge(fourier_loaded, FOURIER_LOADS * 16)
            spectrum(act.copy, act, 0, spec_ready_a)

            def project_in(i):
                act.wait_ge(pin_done, i + 1)
                first, n = PARTS[0][i]
                act.activation(h_hi[:, first:first + n], bank[PIN_BANK[i]][:, 0:n], ACT.Identity, bias=pin_b[:]).then_inc(h_hi_ready, 1)

            project_in(0)
            def hidden(layer, e, i, groups=None):
                for g in groups or range(GROUPS[layer]):
                    act.wait_ge(hidden_done[layer], e * GROUPS[layer] + g + 1)
                    c, k = g % FC, g // FC
                    if layer == 0 and g == 0:
                        act.wait_ge(b1_loaded[i], (e - i) * 8 + 16)
                    first, n = PARTS[layer][k]
                    to = (hid_f if layer == 0 else hid_g)[i][:, c, first:first + n]
                    bias = {"bias": b1[i][:, c:c + 1]} if layer == 0 else {}
                    act.activation(to, bank[UP_BANK[layer][g % len(UP_BANK[layer])]][:, 0:n], ACT.Gelu, **bias).then_inc(hidden_ready[layer], 1)

            def hidden_rest(layer):
                hidden(layer, 1, 1)
                with act.Fori(0, E - 3, 2) as e:
                    for i in range(2):
                        act.wait_ge(expert_done[layer], (e + i) * TILES[layer] + TILES[layer])
                        hidden(layer, e + i + 2, i)

            hidden(0, 0, 0, range(FC))
            project_in(1)
            project_in(2)
            hidden(0, 0, 0, range(FC, GROUPS[0]))
            hidden_rest(0)
            for i in range(3):
                act.wait_ge(wsel_turned, i + 1)
                n = min(4, FT - 4 * i) * P
                act.copy(wsel_t[:, 4 * i * P:4 * i * P + n], bank[WSEL_BANK[i]][0:E, 0:n]).then_inc(wsel_t_ready, 1)

            def results_down(i, count):
                act.wait_ge(moe_turned, count)
                n = min(4 * P, NF - 4 * i * P)
                act.copy(moe_t[:, 4 * i * P:4 * i * P + n], bank[MOE_BANK[i]][:, 0:n]).then_inc(moe_t_ready, 1)

            def inverse_parts(b):
                act.wait_ge(inv_done, 2 * b + 1)
                act.copy(comb[:, b, 0:4], bank[INV_BANK[b][0]].rearrange("p (o d) -> p o d", d=D)).then_inc(comb_ready_a, 1)

            results_down(0, 1)
            results_down(2, 2)
            inverse_parts(0)
            results_down(1, 3)
            inverse_parts(1)
            act.wait_ge(pad_cleared, 3)
            for b in range(B):
                features_down(2 + b, b)
                for c in range(2 * TB):
                    act.wait_ge(scores2_done, b * 2 * TB + c + 1)
                    act.activation(p_2[b][:, c % TB, HALF * (c // TB):HALF * (c // TB + 1)], bank[c % 2][:], ACT.Exp, bias=minus_shift[:]).then_inc(probs2_ready, 1)
            features_down(4, 0)
            hidden(1, 0, 0)
            hidden_rest(1)

        @block.vector
        def _(dve):
            dve.wait_ge(ids_loaded, 5 * 16)
            dve.tensor_tensor(seen, frames_i.unsqueeze(1).broadcast_to([N_FFT, VOCAB, NFR]), vocab_row[:].unsqueeze(2).broadcast_to([N_FFT, VOCAB, NFR]), ALU.is_equal).then_inc(seen_ready, 1)
            dve.wait_ge(tok_cleared, 3)
            dve.tensor_scalar(tok_sel[VOCAB_AT:SEL_K, :], ids_i, vocab_col[VOCAB_AT:SEL_K, :], None, ALU.is_equal).then_inc(sel_ready, 1)
            dve.wait_ge(squares, 4)
            dve.scalar_tensor_tensor(out=re_sq, in0=re_sq, scalar=1e-33, in1=im_sq, op0=ALU.max, op1=ALU.add).then_inc(power_ready, 1)
            dve.wait_ge(tok_loaded, 4 * 16)
            dve.wait_ge(enc_done, 1)
            dve.tensor_tensor(tok_tab[0:NFR, D_EMB:D], bank[4][0:NFR, 0:D_STFT], proj_b, ALU.add).then_inc(tab_ready, 1)

            def statistics(n, b, rows=h):
                for t in range(b * TB, (b + 1) * TB):
                    dve.bn_stats(stats[:, t, :], rows[:, t, :]).then_inc(stats_done, 1)
                for i, t in enumerate(range(b * TB, (b + 1) * TB)):
                    dve.wait_ge(stats_done, TB * n + i + 1)
                    dve.bn_aggr(mv[:, t, :], stats[:, t, :]).then_inc(mean_done, 1)
                dve.wait_ge(mean_done, TB * (n + 1))
                tiles = slice(b * TB, (b + 1) * TB)
                dve.tensor_scalar(var_eps[:, tiles], mv[:, tiles, 1], LN_EPS, None, ALU.add).then_inc(var_ready, 1)

            def normalise(n, b):
                dve.wait_ge(rstd_ready, n + 1)
                for t in range(b * TB, (b + 1) * TB):
                    dve.tensor_scalar(ln[:, t, :], h[:, t, :], mv[:, t, 0:1], rstd[:, t:t + 1], ALU.subtract, ALU.mult).then_inc(ln_ready, 1)

            dve.wait_ge(h_ready, 2)
            def low_features(n, b):
                for i in range(2):
                    dve.wait_ge(ln_hi_ready, 2 * n + i + 1)
                    first = b * L + HALF * i
                    cols = slice(first, first + HALF)
                    dve.tensor_tensor(ln_lo[:, cols], turn_bank(n, i)[:], ln_hi[:, cols], ALU.subtract).then_inc(ln_lo_ready, 1)

            statistics(0, 0)
            dve.wait_ge(h_ready, 4)
            statistics(1, 1)
            normalise(0, 0)
            normalise(1, 1)
            low_features(0, 0)

            def low_parts(hd, b):
                n = hd * B + b
                for c in range(2):
                    cols = slice(HALF * c, HALF * (c + 1))
                    dve.wait_ge(q_high, n * 2 + c + 1)
                    dve.wait_ge(k_high, n * 2 + c + 1)
                    dve.scalar_tensor_tensor(out=query_lm[b][0:DK, cols], in0=pj[c][0:DK, :], scalar=b_head[0:DK, :], in1=query_hh[b][0:DK, cols], op0=ALU.add, op1=ALU.subtract).then_inc(q_low, 1)
                    dve.scalar_tensor_tensor(out=key_hl[b][DK:P, cols], in0=pj[c][DK:P, :], scalar=b_head[DK:P, :], in1=k_high_up[DK:P, cols], op0=ALU.add, op1=ALU.subtract).then_inc(k_low, 1)

            def maxima(hd, b, first, end):
                n = hd * B + b
                for m, (j, c, width) in enumerate(m_chunks[:end]):
                    if m < first:
                        continue
                    dve.wait_ge(rows_done, n * NM + m + 1)
                    if j < 4:
                        to = max_cols[:, MAX_AT + j:MAX_AT + j + 1]
                    else:
                        to = max_part[:, 2 * (j - 4) + c:2 * (j - 4) + c + 1]
                    dve.tensor_reduce(to, sm[m % 2][:, 0:width], AX.X, ALU.max, negate=True).then_inc(rows_used, 1)
                if end < NM:
                    return
                dve.wait_ge(rows_used, n * NM + NM)
                pairs = max_part[:].rearrange("p (j c) -> p j c", c=2)
                dve.tensor_tensor(max_cols[:, MAX_AT + 4:MAX_END].unsqueeze(2), pairs[:, :, 0:1], pairs[:, :, 1:2], ALU.min).then_inc(max_ready, 1)

            def max_rows(hd, b):
                dve.wait_ge(max_turned, hd * B + b + 1)
                to = query_lm[b][MAX_AT:MAX_END, :].rearrange("p (t q) -> p t q", q=P)
                diagonal = ident[MAX_AT:MAX_END, MAX_AT:MAX_END].unsqueeze(2).broadcast_to([TB, TB, P])
                dve.tensor_tensor(to, sm[0][MAX_AT:MAX_END, 0:P].unsqueeze(1).broadcast_to([TB, TB, P]), diagonal, ALU.mult).then_inc(max_row_ready, 1)

            def divide(hd, b, half):
                n = hd * B + b
                dve.wait_ge(pv_done[half], n + 2)
                got = pv[half][:, 0:4 * VW].rearrange("p (t w) -> p t w", w=VW)
                scale = o_scale[:, 4 * half:4 * half + 4].unsqueeze(2)
                dve.reciprocal(scale, got[:, :, DK:DK + 1]).then_inc(den_ready[half], 1)
                dve.wait_ge(den_ready[half], n + 1)
                to = o_all[:, b * TB + 4 * half:b * TB + 4 * half + 4, bass.ds(hd * DK, DK)]
                dve.tensor_tensor(to, got[:, :, 0:DK], scale.broadcast_to([P, 4, DK]), ALU.mult).then_inc(o_ready[half], 1)

            def vector_head(hd, b, last=False):
                n_next = not (last and b == 1)
                if n_next:
                    maxima(hd + b, 1 - b, 0, DIVIDE_AT)
                divide(hd, b, 0)
                if n_next:
                    maxima(hd + b, 1 - b, DIVIDE_AT, NM)
                    max_rows(hd + b, 1 - b)
                if not last:
                    low_parts(hd + 1, b)
                divide(hd, b, 1)

            dve.wait_ge(pool_const, POOL_CONSTS)
            low_parts(0, 0)
            dve.wait_ge(b_v_out_done, 1)
            dve.wait_ge(attn_loaded, 6 * 16)
            dve.tensor_tensor(b_out[:], bank[7][:, 0:D], b_out[:], ALU.add).then_inc(b_out_ready, 1)
            dve.tensor_copy(mask_b[:], mask_f).then_inc(consts_b, 1)
            dve.tensor_copy(ident_b[:], ident[:]).then_inc(consts_b, 1)
            for half in range(2):
                dve.memset(o_scale[:, 4 * half:4 * half + 4], 1.0).then_inc(o_ready[half], 1)
            low_features(1, 1)
            maxima(0, 0, 0, FIRST_LOW_AT)
            low_parts(0, 1)
            maxima(0, 0, FIRST_LOW_AT, NM)
            max_rows(0, 0)
            with dve.Fori(0, H - 1) as hd:
                vector_head(hd, 0)
                vector_head(hd, 1)
            vector_head(H - 1, 0, last=True)
            vector_head(H - 1, 1, last=True)

            dve.wait_ge(base_ready, 2)

            def fold(b):
                dve.wait_ge(ln_ready, 2 * NT - TB + b * TB)
                x = ln[:, b * TB:(b + 1) * TB]
                dve.tensor_tensor(sum4[:, b], x[:, 0:4], x[:, 4:8], ALU.add).then_inc(fold1, 1)
                dve.tensor_tensor(dif4[:, b], x[:, 0:4], x[:, 4:8], ALU.subtract).then_inc(fold1, 1)
                dve.wait_ge(fold1, 2 * b + 2)
                dve.tensor_tensor(ev2[:, b], sum4[:, b, 0:2], sum4[:, b, 2:4], ALU.add).then_inc(fold2, 1)
                dve.tensor_tensor(od2[:, b], sum4[:, b, 0:2], sum4[:, b, 2:4], ALU.subtract).then_inc(fold2, 1)
                dve.tensor_tensor(dd[:, b], dif4[:, b, 1], dif4[:, b, 3], ALU.subtract).then_inc(fold2, 1)
                dve.tensor_tensor(gg[:, b], dif4[:, b, 1], dif4[:, b, 3], ALU.add).then_inc(fold2, 1)
                dve.wait_ge(fold2, 4 * b + 4)
                dve.tensor_tensor(y[:, 0, b], ev2[:, b, 0], ev2[:, b, 1], ALU.add).then_inc(y_ready, 1)
                dve.tensor_tensor(y[:, 1, b], ev2[:, b, 0], ev2[:, b, 1], ALU.subtract).then_inc(y_ready, 1)
                for i, (pair, sign, rest) in enumerate(((dd, C8, 0), (dd, -C8, 0), (gg, C8, 2), (gg, -C8, 2))):
                    dve.scalar_tensor_tensor(out=y[:, 2 + i, b], in0=pair[:, b], scalar=sign, in1=dif4[:, b, rest], op0=ALU.mult, op1=ALU.add).then_inc(y_ready, 1)

            def low_in(i):
                first, n = PARTS[0][i]
                cols = slice(first, first + n)
                dve.wait_ge(h_hi_ready, i + 1)
                dve.scalar_tensor_tensor(out=h_lo[:, cols], in0=bank[PIN_BANK[i]][:, 0:n], scalar=pin_b[:], in1=h_hi[:, cols], op0=ALU.add, op1=ALU.subtract).then_inc(h_lo_ready, 1)

            for b in range(B):
                for i in range(2 * b, 2 * b + 2):
                    dve.wait_ge(out_done, 4 * i + 4)
                    dve.tensor_tensor(h[:, 4 * i:4 * i + 4, :], bank[4 + i].rearrange("p (t d) -> p t d", d=D), base[:, 4 * i:4 * i + 4, :], ALU.add).then_inc(h_ready, 1)
                dve.wait_ge(h_ready, 6 + 2 * b)
                statistics(2 + b, b)
                normalise(2 + b, b)
                if b == 1:
                    low_in(0)
                fold(b)
            spectrum(dve.tensor_copy, dve, 1, spec_ready_v)
            low_in(1)
            low_in(2)

            dve.memset(acc_f, 0.0).then_inc(acc_ready[0], FT)

            dve.wait_ge(fourier_loaded, FOURIER_LOADS * 16)
            dve.wait_ge(router_done, 2)
            dve.tensor_tensor(logits[:], bank[4][:, ROUTER_AT:ROUTER_AT + FT * E].rearrange("p (t e) -> p t e", e=E), router_b[:].unsqueeze(1).broadcast_to([P, FT, E]), ALU.add).then_inc(logits_ready, 1)
            dve.wait_ge(logits_ready, 1)
            for t in range(FT):
                dve.max(top8[:, t, :], logits[:, t, :]).then_inc(top_ready, 1)
            dve.wait_ge(top_ready, FT)
            dve.tensor_tensor(gap[:], top8[:, :, 1:2], top8[:, :, 0:1], ALU.subtract).then_inc(gap_ready, 1)
            for t in range(FT):
                dve.max_index(idx8[:, t, :], top8[:, t, :], logits[:, t, :]).then_inc(idx_ready, 1)
            dve.wait_ge(idx_ready, FT)
            dve.tensor_copy(choice[:], idx8[:, :, 0:2]).then_inc(route, 1)
            dve.wait_ge(odds_ready, 1)
            dve.tensor_scalar(odds1[:], odds[:], 1.0, None, ALU.add).then_inc(route, 1)
            dve.wait_ge(route, 2)
            dve.reciprocal(share[:, :, 0:1], odds1[:]).then_inc(route, 1)
            dve.wait_ge(route, 3)
            dve.tensor_tensor(share[:, :, 1:2], odds[:], share[:, :, 0:1], ALU.mult).then_inc(route, 1)
            dve.wait_ge(route, 4)

            def weights_of(chosen, shares, nt, to, sig, first, ready):
                numbers = expert_no[:].unsqueeze(1).broadcast_to([P, nt, E])
                for k in range(2):
                    dve.tensor_tensor(pick[k][:, 0:nt], numbers, chosen[:, :, k:k + 1].broadcast_to([P, nt, E]), ALU.is_equal).then_inc(sig, 1)
                for k in range(2):
                    dve.wait_ge(sig, first + k + 1)
                    dve.tensor_tensor(pick[k][:, 0:nt], pick[k][:, 0:nt], shares[:, :, k:k + 1].broadcast_to([P, nt, E]), ALU.mult).then_inc(sig, 1)
                dve.wait_ge(sig, first + 4)
                dve.tensor_tensor(to[:], pick[0][:, 0:nt], pick[1][:, 0:nt], ALU.add).then_inc(ready, 1)

            weights_of(choice[:], share[:], FT, wsel_f, route, 4, wsel_ready)

            def accumulate(layer, e, k):
                t, acc, wsel = ORDER[layer][k], (acc_f, acc_g)[layer], (wsel_f, wsel_g)[layer]
                rows = 2 if layer == 0 and t == FT - 1 else P
                dve.wait_ge(acc_ready[layer], e * TILES[layer] + k + 1)
                dve.wait_ge(expert_done[layer], e * TILES[layer] + k + 1)
                dve.scalar_tensor_tensor(out=acc[0:rows, t, :], in0=bank[2 + k % RING[layer]][0:rows, 0:D], scalar=wsel[0:rows, t, bass.ds(e, 1)], in1=acc[0:rows, t, :], op0=ALU.mult, op1=ALU.add).then_inc(acc_ready[layer], 1)

            dve.wait_ge(wsel_ready, 1)
            with dve.Fori(0, E - 1) as e:
                for k in range(FT):
                    accumulate(0, e, k)

            dve.tensor_copy(gate_no[:], gate_i[:]).then_inc(gates, 1)
            dve.wait_ge(gates, 1)
            weights_of(gate_no[:], gate_w[:], TB, wsel_g, gates, 1, wsel_ready)

            def biased(b):
                got = [bank[k].rearrange("p (r d) -> p r d", d=D) for k in OF_BANK[b]]
                dve.wait_ge(of_done, 2 * b + 1)
                dve.tensor_tensor(of[:, b, 0], got[0][:, 0, :], pout_b[:, 0, :], ALU.add).then_inc(of_ready, 1)
                dve.tensor_tensor(of[:, b, 1:4], got[0][:, 1:4], pout_b[:, 1:2, :].broadcast_to([P, 3, D]), ALU.add).then_inc(of_ready, 1)
                dve.wait_ge(of_done, 2 * b + 2)
                dve.tensor_tensor(of[:, b, 4:8], got[1], pout_b[:, 1:2, :].broadcast_to([P, 4, D]), ALU.add).then_inc(of_ready, 1)

            def gather(b):
                dve.wait_ge(inv_done, 2 * b + 2)
                dve.tensor_copy(comb[:, b, 4:8], bank[INV_BANK[b][1]].rearrange("p (o d) -> p o d", d=D)).then_inc(comb_ready_v, 1)
                dve.wait_ge(comb_ready_a, b + 1)
                dve.wait_ge(comb_ready_v, b + 1)

            for k in range(7):
                accumulate(0, E - 1, k)
            biased(0)
            for k in range(7, FT):
                accumulate(0, E - 1, k)

            def unfold(b):
                a0, a4, a1, b1_, a2, b2_, a3, b3_ = (comb[:, b, i] for i in range(8))
                for i, (u, v, op) in enumerate(((a0, a4, ALU.add), (a0, a4, ALU.subtract), (a1, a3, ALU.add), (b3_, b1_, ALU.subtract), (a1, a3, ALU.subtract), (b1_, b3_, ALU.add))):
                    dve.tensor_tensor(inv[:, i, b], u, v, op).then_inc(unfold1, 1)
                dve.wait_ge(unfold1, 6 * b + 6)
                p0, m0, d0, d2, u0, v0 = (inv[:, i, b] for i in range(6))
                for i, (u, v, op) in enumerate(((p0, a2, ALU.add), (m0, b2_, ALU.subtract), (p0, a2, ALU.subtract), (m0, b2_, ALU.add), (u0, v0, ALU.subtract), (u0, v0, ALU.add))):
                    dve.tensor_tensor(inv[:, 6 + i, b], u, v, op).then_inc(unfold2, 1)
                dve.wait_ge(unfold2, 6 * b + 6)
                e0, e1, e2, e3, d1, d3 = (inv[:, i, b] for i in range(6, 12))
                for j, (even, odd, scale) in enumerate(((e0, d0, 1.0), (e1, d1, C8), (e2, d2, 1.0), (e3, d3, -C8))):
                    dve.scalar_tensor_tensor(out=ot[:, b * TB + j], in0=odd, scalar=scale, in1=even, op0=ALU.mult, op1=ALU.add).then_inc(ot_ready, 1)
                    dve.scalar_tensor_tensor(out=ot[:, b * TB + j + 4], in0=odd, scalar=-scale, in1=even, op0=ALU.mult, op1=ALU.add).then_inc(ot_ready, 1)
                dve.wait_ge(ot_ready, 8 * b + 8)

            def add_back(n, b):
                tiles = range(b * TB, (b + 1) * TB)
                for t in tiles:
                    dve.scalar_tensor_tensor(out=ot[:, t, :], in0=ot[:, t, :], scalar=mv[:, t, 0:1], in1=ln_g[:], op0=ALU.subtract, op1=ALU.mult).then_inc(ot_scaled, 1)
                dve.wait_ge(rstd_ready, n + 1)
                dve.wait_ge(base_f_ready, 2)
                for t in tiles:
                    dve.wait_ge(ot_scaled, t + 1)
                    dve.scalar_tensor_tensor(out=h[:, t, :], in0=ot[:, t, :], scalar=rstd[:, t:t + 1], in1=base[:, t, :], op0=ALU.mult, op1=ALU.add).then_inc(h2_ready, 1)
                dve.wait_ge(h2_ready, (b + 1) * TB)

            for b in range(B):
                gather(b)
                unfold(b)
                if b == 0:
                    biased(1)
                statistics(4 + 2 * b, b, ot)
                add_back(4 + 2 * b, b)
                statistics(5 + 2 * b, b)
                normalise(5 + 2 * b, b)
                if b == 0:
                    low_features(2, 0)

            def attended(t):
                dve.wait_ge(pv2_done, t + 1)
                dve.reciprocal(den2[:, t:t + 1], bank[2 + t % 4][:, D:D + 1]).then_inc(den2_ready, 1)
                dve.wait_ge(den2_ready, t + 1)
                dve.scalar_tensor_tensor(out=h[:, t, :], in0=bank[2 + t % 4][:, 0:D], scalar=den2[:, t:t + 1], in1=h[:, t, :], op0=ALU.mult, op1=ALU.add).then_inc(h3_ready, 1)

            for t in range(TB):
                attended(t)
                if t == 2:
                    low_features(3, 1)
            dve.wait_ge(h3_ready, TB)
            statistics(8, 0)
            normalise(8, 0)
            for t in range(TB, TB + 4):
                attended(t)
            low_features(4, 0)
            for t in range(TB + 4, NT):
                attended(t)
            for t in range(TB):
                dve.tensor_copy(acc_g[:, t, :], h[:, t, :]).then_inc(acc_ready[1], 1)
            dve.wait_ge(wsel_ready, 2)
            with dve.Fori(0, E) as e:
                for k in range(TB):
                    accumulate(1, e, k)

        @block.tensor
        def _(pe):
            pe.wait_ge(seen_ready, 1)
            for i in range(4):
                half = i % 2
                pe.matmul(bank[i][0:N_FREQ, 0:272], dft64[:, i // 2, :], seen[:, 8 * half:8 * half + 8, :], start=True, stop=True).then_inc(dft_done, 1)
            pe.wait_ge(mag_ready, 1)
            pe.wait_ge(tok_loaded, 4 * 16)
            for v in range(VOCAB):
                mm = pe.matmul(bank[4][0:NFR, 0:D_STFT], mag[:, v, :], proj_w[:, v, :], start=(v == 0), stop=(v == VOCAB - 1))
            mm.then_inc(enc_done, 1)
            pe.wait_ge(tab_ready, 1)
            pe.wait_ge(sel_ready, 1)
            for t in range(NT):
                mm = pe.matmul(bank[t // 4][:, D * (t % 4):D * (t % 4 + 1)], tok_sel[:, P * t:P * (t + 1)], tok_tab, start=True, stop=True)
                if t % 4 == 3:
                    mm.then_inc(tok_done, 1)

            def product3(to, left, right, start=True, stop=True):
                pe.matmul(to, left[0], right[1], start=start, stop=False)
                pe.matmul(to, left[1], right[0], start=False, stop=False)
                return pe.matmul(to, left[0], right[0], start=False, stop=stop)

            def turn_rows(n, b, batch):
                for i in range(2):
                    if n >= 1:
                        pe.wait_ge(ln_lo_ready, 2 * n + i - 1)
                    for k in range(4):
                        t = b * TB + 4 * i + k
                        pe.wait_ge(ln_ready, TB * batch + 4 * i + k + 1)
                        mm = pe.transpose(turn_bank(n, i)[:, P * k:P * (k + 1)], ln[:, t, :], ident[:])
                    mm.then_inc(turned, 1)

            pe.wait_ge(attn_loaded, 6 * 16)
            for k in range(4):
                mm = pe.matmul(bank[7][:, 0:D], b_v[:, k, :], w_out[:, k, :], start=(k == 0), stop=(k == 3))
            mm.then_inc(b_v_out_done, 1)

            def project_v(t):
                pe.wait_ge(ln_lo_ready, t // 4 + 1)
                if t % TB >= 4:
                    pe.wait_ge(v_ready, t - 3)
                elif t == 3:
                    pe.wait_ge(b_out_ready, 1)
                elif t >= TB:
                    pe.wait_ge(v_ready, TB)
                    pe.wait_ge(ln_lo_ready, 4)
                product3(bank[v_bank(t)][:], (ln_hi[:, P * t:P * (t + 1)], ln_lo[:, P * t:P * (t + 1)]), (w_v_hi, w_v_lo)).then_inc(v_done, 1)

            def project(hd, b, c, first=False):
                n = hd * B + b
                if not first:
                    pe.wait_ge(k_low, n * 2 + c - 1)
                    pe.wait_ge(q_low, n * 2 + c - 1)
                x = slice(b * L + HALF * c, b * L + HALF * (c + 1))
                product3(pj[c][:], (w_head_hi[:], w_head_lo[:]), (ln_hi[:, x], ln_lo[:, x])).then_inc(qk_done, 1)

            def score_rows(hd, b, m, first=False):
                n = hd * B + b
                j, c, width = m_chunks[m]
                if m == 0:
                    pe.wait_ge(k_low, n * 2 + 2)
                    pe.wait_ge(q_moved, n * 16 + 16)
                    pe.wait_ge(k_moved, n * 16 + 16)
                if m == 0 and not first:
                    pe.wait_ge(max_row_ready, n)
                elif m >= 2 or not first:
                    pe.wait_ge(rows_used, n * NM + m - 1)
                to = sm[m % 2]
                on_diag = P * j < HALF * c + width and P * j >= HALF * c
                cols = max(width, FAST)
                mm = pe.matmul(to[:, 0:cols], query_hh[b][:, P * j:P * (j + 1)], key_hl[b][:, HALF * c:HALF * c + cols], start=True, stop=not on_diag)
                if on_diag:
                    mm = pe.matmul(to[:, width - P:width], ident_b[:], mask_b[:], start=False, stop=True)
                mm.then_inc(rows_done, 1)

            def turn_maxima(hd, b):
                pe.wait_ge(max_ready, hd * B + b + 1)
                pe.transpose(sm[0][0:MAX_END, 0:P], max_cols[:], ident[:]).then_inc(max_turned, 1)

            def scores(hd, b, c):
                n = hd * B + b
                half, i, first, width = s_chunks[c]
                if c == 0:
                    pe.wait_ge(max_row_ready, n + 1)
                    pe.wait_ge(k_moved_h1, n * 16 + 16)
                if c >= 2:
                    pe.wait_ge(probs_ready, n * NS + c - 1)
                before = max(FAST - width, 0)
                to, on_diag = st[c % 2][:, 0:before + width], first == P * i
                keys, queries = slice(P * i, P * (i + 1)), slice(first - before, first + width)
                pe.matmul(to, key_h1[b][:, keys], query_lm[b][:, queries], start=True, stop=False)
                mm = pe.matmul(to, key_hl[b][:, keys], query_hh[b][:, queries], start=False, stop=not on_diag)
                if on_diag:
                    mm = pe.matmul(st[c % 2][:, before:before + P], mask_b[:], ident_b[:], start=False, stop=True)
                mm.then_inc(scores_done, 1)

            def weigh(hd, b, j):
                n = hd * B + b
                half = j // 4
                if j == 0:
                    pe.wait_ge(v_head_ready, n + 1)
                if j % 4 == 0:
                    pe.wait_ge(o_ready[half], n + 1)
                c = chunk_of[half, j]
                pe.wait_ge(probs_ready, n * NS + c + 1)
                for i in range(j + 1):
                    c = chunk_of[half, i]
                    at = s_first[c] + P * j - s_chunks[c][2]
                    mm = pe.matmul(pv[half][:, VW * (j % 4):VW * (j % 4 + 1)], p_t[:, at:at + P], v_head[b][:, i, :], start=(i == 0), stop=(i == j))
                if j % 4 == 3:
                    mm.then_inc(pv_done[half], 1)

            def tensor_head(hd, b, last=False):
                final = last and b == 1

                def rows(m):
                    if not final:
                        score_rows(hd + b, 1 - b, m)

                scores(hd, b, 0)
                scores(hd, b, 1)
                rows(0)
                rows(1)
                for j in range(3):
                    weigh(hd, b, j)
                    scores(hd, b, j + 2)
                    rows(j + 2)
                scores(hd, b, 5)
                weigh(hd, b, 3)
                rows(5)
                for c in range(6, NS):
                    scores(hd, b, c)
                    rows(c)
                if not last:
                    if b == 0:
                        pe.wait_ge(w_head_split, hd * 2 + 4)
                    project(hd + 1, b, 0)
                weigh(hd, b, 4)
                if not final:
                    turn_maxima(hd + b, 1 - b)
                if not last:
                    project(hd + 1, b, 1)
                for j in range(5, TB):
                    weigh(hd, b, j)

            turn_rows(0, 0, 0)
            pe.wait_ge(h_ready, 4)
            pe.wait_ge(w_head_split, 2)
            for c in range(2):
                pe.wait_ge(ln_lo_ready, c + 1)
                project(0, 0, c, first=True)
            pe.wait_ge(w_v_split, 2)
            for t in range(TB):
                project_v(t)
            turn_rows(1, 1, 1)
            pe.wait_ge(pool_const, POOL_CONSTS)
            pe.wait_ge(consts_b, 2)
            for c in range(2):
                pe.wait_ge(ln_lo_ready, B + c + 1)
                project(0, 1, c)
            pe.wait_ge(v_ready, TB)
            for m in range(NM):
                score_rows(0, 0, m, first=True)
                if m < TB:
                    project_v(TB + m)
            pe.wait_ge(v_ready, NT)
            for c in range(2):
                pe.matmul(pv[c][:, 0:P], ident_b[:], ident_b[:], start=True, stop=True).then_inc(pv_done[c], 1)
            turn_maxima(0, 0)
            with pe.Fori(0, H - 1) as hd:
                tensor_head(hd, 0)
                tensor_head(hd, 1)
            tensor_head(H - 1, 0, last=True)
            tensor_head(H - 1, 1, last=True)

            def turn_heads(t):
                pe.wait_ge(o_ready[(t % TB) // 4], (H - 1) * B + t // TB + 2)
                if t >= 2:
                    pe.wait_ge(o_t_ready, t - 1)
                for k in range(4):
                    mm = pe.transpose(bank[t % 2][:, P * k:P * (k + 1)], o_all[:, t, P * k:P * (k + 1)], ident[:])
                mm.then_inc(o_turned, 1)

            turn_heads(0)
            for t in range(NT):
                if t + 1 < NT:
                    turn_heads(t + 1)
                pe.wait_ge(o_t_ready, t + 1)
                for k in range(4):
                    mm = pe.matmul(bank[4 + t // 4][:, D * (t % 4):D * (t % 4 + 1)], o_t[t % 2][:, P * k:P * (k + 1)], w_out[:, k, :], start=(k == 0), stop=(k == 3))
                mm.then_inc(out_done, 1)


            pe.wait_ge(fourier_loaded, FOURIER_LOADS * 16)

            def transform(b):
                pe.wait_ge(h_ready, 6 + 2 * b)
                pe.wait_ge(y_ready, 6 * (b + 1))
                pe.matmul(bank[4 * b][:, 0:130], y[:, 0, b, :], fwd_single[:, 0:130], start=True, stop=True)
                pe.matmul(bank[4 * b][:, 256:384], y[:, 1, b, :], fwd_single[:, 130:258], start=True, stop=True).then_inc(spec_done, 1)
                for r, (re, im) in enumerate(((y[:, 2, b], y[:, 4, b]), (od2[:, b, 0], od2[:, b, 1]), (y[:, 3, b], y[:, 5, b]))):
                    pe.matmul(bank[4 * b + 1 + r][:, 0:256], re, fwd_pair[:, 2 * r, :], start=True, stop=False)
                    pe.matmul(bank[4 * b + 1 + r][:, 0:256], im, fwd_pair[:, 2 * r + 1, :], start=False, stop=True).then_inc(spec_done, 1)

            def project_in(i):
                first, n = PARTS[0][i]
                cols = slice(first, first + n)
                if i == 2:
                    pe.wait_ge(h_lo_ready, 1)
                pe.matmul(bank[PIN_BANK[i]][:, 0:n], pin_w[:, 0, :], xf[:, 0, cols], start=True, stop=False)
                pe.matmul(bank[PIN_BANK[i]][:, 0:n], pin_w[:, 1, :], xf[:, 1, cols], start=False, stop=True).then_inc(pin_done, 1)

            def up(layer, e, i, g, first=False):
                c, k = g % FC, g // FC
                x_hi, x_lo = ((h_hi, h_lo), (ln_hi, ln_lo))[layer]
                if g == 0:
                    pe.wait_ge(w1_split, (e + layer * E) * 2 + 2)
                if layer == 0 and first and c == 0:
                    pe.wait_ge(h_lo_ready, k + 1)
                ring = len(UP_BANK[layer])
                if g >= ring or not first:
                    pe.wait_ge(hidden_ready[layer], e * GROUPS[layer] + g + 1 - ring)
                begin, n = PARTS[layer][k]
                w, x = slice(P * c, P * (c + 1)), slice(begin, begin + n)
                product3(bank[UP_BANK[layer][g % ring]][:, 0:n], (w1_hi[i][:, w], w1_lo[i][:, w]), (x_hi[:, x], x_lo[:, x])).then_inc(hidden_done[layer], 1)

            def down(layer, e, i, k):
                t = ORDER[layer][k]
                if k == 0:
                    pe.wait_ge(hidden_ready[layer], e * GROUPS[layer] + GROUPS[layer])
                    pe.wait_ge(w2_loaded[i], (e - i + layer * E) * 8 + 16)
                pe.wait_ge(acc_ready[layer], (e + 1) * TILES[layer] + k + 1 - RING[layer])
                hid = (hid_f if layer == 0 else hid_g)[i]
                rows = 2 if layer == 0 and t == FT - 1 else P
                for c in range(FC):
                    mm = pe.matmul(bank[2 + k % RING[layer]][0:rows, 0:D], hid[:, c, P * t:P * t + rows], w2[i][:, c, :], start=(c == 0), stop=(c == FC - 1))
                mm.then_inc(expert_done[layer], 1)

            def first_up(layer, *groups):
                for g in groups or range(GROUPS[layer]):
                    up(layer, 0, 0, g, first=True)

            def experts(layer):
                def step(e, i, last=False):
                    for g in range(max(GROUPS[layer], TILES[layer])):
                        if g < GROUPS[layer] and not last:
                            up(layer, e + 1, 1 - i, g)
                        if g < TILES[layer]:
                            down(layer, e, i, g)

                with pe.Fori(0, E - 3, 2) as e:
                    step(e, 0)
                    step(e + 1, 1)
                step(E - 2, 0)
                if layer == 1:
                    step(E - 1, 1, last=True)

            def route(tiles):
                for t in tiles:
                    rows = slice(P * t, P * (t + 1))
                    pe.matmul(bank[4][:, ROUTER_AT + E * t:ROUTER_AT + E * (t + 1)], h_lo[:, rows].bitcast(F32), router_w[:], start=True, stop=False)
                    mm = pe.matmul(bank[4][:, ROUTER_AT + E * t:ROUTER_AT + E * (t + 1)], h_hi[:, rows].bitcast(F32), router_w[:], start=False, stop=True)
                mm.then_inc(router_done, 1)

            transform(0)
            pe.wait_ge(spec_ready_a, 6)
            project_in(0)
            first_up(0, *range(FC))
            route(range(TB // 2))
            transform(1)
            pe.wait_ge(spec_ready_v, 6)
            project_in(1)
            project_in(2)
            pe.wait_ge(h_lo_ready, 3)
            pe.wait_ge(pad_cleared, 2)
            route(range(TB // 2, FT))
            first_up(0, *range(FC, GROUPS[0]))

            def turn_weights():
                pe.wait_ge(wsel_ready, 1)
                for t in range(FT):
                    mm = pe.transpose(bank[WSEL_BANK[t // 4]][0:E, P * (t % 4):P * (t % 4 + 1)], wsel_f[:, t, :], ident[:])
                    if t % 4 == 3 or t == FT - 1:
                        mm.then_inc(wsel_turned, 1)

            def expert_biases():
                pe.wait_ge(wsel_t_ready, 3)
                for i in range(3):
                    n = min(HALF, NF - HALF * i)
                    pe.matmul(bank[MOE_BANK[i]][:, 0:n], b2[:], wsel_t[:, HALF * i:HALF * i + n], start=True, stop=False)

            pe.wait_ge(logits_ready, 1)
            experts(0)

            def turn_results(i):
                for t in range(4 * i, min(4 * i + 4, FT)):
                    rows = 2 if t == FT - 1 else P
                    ends = t % 4 == 3 or t == FT - 1
                    mm = pe.matmul(bank[MOE_BANK[i]][:, P * (t % 4):P * (t % 4) + rows], acc_f[0:rows, t, :], ident[0:rows, 0:rows], start=False, stop=ends)
                mm.then_inc(moe_turned, 1)

            def project_out(b):
                for r in range(RES):
                    to, at = bank[OF_BANK[b][r // 4]], D * (r % 4)
                    rows = moe_t[:, (b * RES + r) * M64:(b * RES + r + 1) * M64]
                    pe.matmul(to[0:M64, at:at + D], rows, pout_w[:, 0, :], start=True, stop=True)
                    mm = pe.matmul(to[M64:P, at:at + D], rows, pout_w[:, 1, :], start=True, stop=True)
                    if r == 0:
                        mm = pe.matmul(to[M64:M64 + 1, at:at + D], moe_t[:, NYQ + b:NYQ + b + 1], pout_w[:, 0, :], start=True, stop=True)
                    if r % 4 == 3:
                        mm.then_inc(of_done, 1)

            plan = [[(0, 0)], [(1, 4)]] + [[(2 + 4 * (r - 1) + 2 * k + s, (r, 8 - r)[s]) for s in range(2)] for r in range(1, 4) for k in range(2)]

            def transform_back(b):
                pe.wait_ge(of_ready, 3 * b + 3)
                for o, terms in enumerate(plan):
                    for n, (table, r) in enumerate(terms):
                        mm = pe.matmul(bank[INV_BANK[b][o // 4]][:, D * (o % 4):D * (o % 4 + 1)], inverse[:, table, :], of[:, b, r], start=(n == 0), stop=(n == len(terms) - 1))
                    if o % 4 == 3:
                        mm.then_inc(inv_done, 1)

            down(0, E - 1, 1, 0)
            turn_weights()
            down(0, E - 1, 1, 1)
            down(0, E - 1, 1, 2)
            expert_biases()
            down(0, E - 1, 1, 3)
            down(0, E - 1, 1, 4)
            down(0, E - 1, 1, 5)
            pe.wait_ge(acc_ready[0], FT * E + EARLY)
            turn_results(0)
            turn_results(2)
            down(0, E - 1, 1, 6)
            pe.wait_ge(moe_t_ready, 2)
            project_out(0)
            down(0, E - 1, 1, 7)
            down(0, E - 1, 1, 8)
            transform_back(0)
            pe.wait_ge(acc_ready[0], FT * (E + 1))
            turn_results(1)
            pe.wait_ge(moe_t_ready, 3)
            project_out(1)
            transform_back(1)

            pe.wait_ge(comb_ready_a, 1)
            pe.wait_ge(comb_ready_v, 1)
            turn_rows(2, 0, 4)

            def scores2(b, c):
                half, i = c // TB, c % TB
                if c >= 2 or b:
                    pe.wait_ge(probs2_ready, b * 2 * TB + c - 1)
                keys, queries = slice(b * L + P * i, b * L + P * (i + 1)), slice(b * L + HALF * half, b * L + HALF * (half + 1))
                product3(bank[c % 2][:], (ln_hi[:, keys], ln_lo[:, keys]), (ln_hi[:, queries], ln_lo[:, queries])).then_inc(scores2_done, 1)

            def weigh2(b, j):
                t = b * TB + j
                pe.wait_ge(probs2_ready, b * 2 * TB + TB * (j // 4 + 1))
                pe.wait_ge(z_ready, 2 * (b + 1))
                if t >= 4:
                    pe.wait_ge(h3_ready, t - 3)
                for i in range(TB):
                    mm = pe.matmul(bank[2 + t % 4][:, 0:D + 1], p_2[b][:, i, P * j:P * (j + 1)], z_one[:, b * TB + i, 0:D + 1], start=(i == 0), stop=(i == TB - 1))
                mm.then_inc(pv2_done, 1)

            pe.wait_ge(ln_lo_ready, 6)
            for c in range(TB):
                scores2(0, c)
            for n in range(2 * B):
                if n == 1:
                    pe.wait_ge(ln_lo_ready, 8)
                if n == 3:
                    turn_rows(4, 0, 6)
                b, half = n // 2, n % 2
                for k in range(TB):
                    if n == 0 and k == TB - 1:
                        pe.wait_ge(comb_ready_a, 2)
                        pe.wait_ge(comb_ready_v, 2)
                        turn_rows(3, 1, 5)
                    if n + 1 < 2 * B:
                        scores2((n + 1) // 2, (n + 1) % 2 * TB + k)
                    if k % 2:
                        weigh2(b, 4 * half + k // 2)

            pe.wait_ge(ln_lo_ready, 10)
            first_up(1)
            pe.wait_ge(h3_ready, NT)
            pe.wait_ge(acc_ready[1], TB)
            experts(1)


def frame_tables():
    w = np.arange(N_FFT)
    window = 0.5 - 0.5 * np.cos(2 * np.pi * w / N_FFT)
    angle = 2 * np.pi * np.outer(w, np.arange(N_FREQ)) / N_FFT
    return np.stack([window[:, None] * np.cos(angle), window[:, None] * -np.sin(angle)], 1).astype(np.float32)


def fourier_tables():
    p = np.arange(P)
    m = np.arange(M64)
    angle = lambda k: 2 * np.pi * np.outer(p, k) / L
    cos = lambda r: np.cos(angle(RES * m + r))
    sin = lambda r: np.sin(angle(RES * m + r))
    norm = 1 / np.sqrt(L)
    nyq = np.stack([(-1.0) ** p, 0 * p], 1)
    single = np.concatenate([cos(0), -sin(0), nyq, cos(4), -sin(4)], 1)
    pair = []
    for r in range(1, 4):
        q = RES - r
        s = 1.0 if r == 3 else -1.0
        pair.append(np.concatenate([cos(r), -sin(r), cos(q), -sin(q)], 1))
        pair.append(s * np.concatenate([sin(r), cos(r), -sin(q), -cos(q)], 1))
    weight = lambda r: np.where((m == 0) & (r == 0), 1.0, 2.0)

    def part_a(r):
        top, low = weight(r) * cos(r), -weight(r) * sin(r)
        if r == 0:
            low[:, 0] = nyq[:, 0]
        return np.concatenate([top, low], 1).T

    def part_b(r, sign):
        return sign * np.concatenate([weight(r) * sin(r), weight(r) * cos(r)], 1).T

    inv = [part_a(0), part_a(4)]
    for r in range(1, 4):
        inv += [part_a(r), part_a(RES - r), part_b(r, 1.0), part_b(RES - r, -1.0)]
    f = lambda v: np.ascontiguousarray(norm * v).astype(np.float32)
    return f(single), f(np.stack(pair, 1)), f(np.stack(inv, 1))


def constants():
    sel = np.zeros((NFR, B * L), np.float32)
    for b in range(B):
        l = np.arange(L)
        sel[b * N_FRAMES + l * N_FRAMES // L, b * L + l] = 1
    single, pair, inv = fourier_tables()
    return {
        "fwd_single": single, "fwd_pair": pair, "inverse": inv,
        "expert_no": np.tile(np.arange(E, dtype=np.float32), (P, 1)),
        "vocab_row": np.tile(np.arange(VOCAB, dtype=np.float32), (N_FFT, 1)),
        "vocab_col": (np.arange(P, dtype=np.float32) - VOCAB_AT)[:, None].copy(),
        "dft64": frame_tables(),
        "upsample": sel,
        "ident": np.eye(P, dtype=np.float32),
        "mask": np.triu(np.full((P, P), NEG, np.float32), 1),
    }


def layouts(x):
    c = np.ascontiguousarray
    ids = np.asarray(x["x"])
    pad = N_FFT // 2
    padded = np.pad(ids, ((0, 0), (pad, pad)), mode="reflect")
    frames = np.stack([padded[b, N_FFT * f:N_FFT * (f + 1)] for b in range(B) for f in range(N_FRAMES)], 1)
    w_in = np.asarray(x["L0_attn_W_in"]).reshape(D, H, 3, DK)
    b_in = np.asarray(x["L0_attn_b_in"]).reshape(H, 3, DK)
    w_qk = w_in[:, :, :2, :].reshape(D, H, 2 * DK).transpose(1, 0, 2)
    b_qk = b_in[:, :2, :].reshape(H, 2 * DK, 1)
    rows = lambda v: np.tile(np.asarray(v).reshape(1, -1), (P, 1))
    real, imag = np.asarray(x["L0_ffn_pout_b"]).reshape(2, D)
    pout_b = np.stack([np.stack([real] * (M64 + 1) + [imag] * (M64 - 1)), np.stack([real] * M64 + [imag] * M64)], 1)
    return {
        "ids_frames": c(frames),
        "ids_bcast": np.tile(ids.reshape(1, -1), (VOCAB, 1)),
        "proj_w": x["L0_tok_proj_w"],
        "proj_b": rows(x["L0_tok_proj_b"])[:NFR],
        "emb_table": x["L0_tok_emb_table"],
        "w_qk": c(w_qk), "b_qk": c(b_qk),
        "w_v": c(w_in[:, :, 2, :].reshape(D, H * DK)),
        "b_v": c(np.broadcast_to(b_in[:, 2, :].reshape(4, P, 1), (4, P, P)).transpose(1, 0, 2)),
        "w_out": x["L0_attn_W_out"],
        "b_out": rows(x["L0_attn_b_out"]),
        "pin_w": x["L0_ffn_pin_w"], "pin_b": np.asarray(x["L0_ffn_pin_b"]).reshape(P, 1),
        "router_w": x["L0_ffn_router_w"], "router_b": rows(x["L0_ffn_router_b"]),
        "w1_f": x["L0_ffn_w1"], "w2_f": x["L0_ffn_w2"], "b2": x["L0_ffn_b2"],
        "b1_f": c(np.asarray(x["L0_ffn_b1"]).reshape(E, FC, P).transpose(0, 2, 1)),
        "pout_w": x["L0_ffn_pout_w"], "pout_b": pout_b,
        "ln_g": rows(x["L0_ffn_ln_g"]), "ln_b": rows(x["L0_ffn_ln_b"]),
        "gate_w": c(np.asarray(x["L1_ffn_expert_weights"]).reshape(TB, P, 2).transpose(1, 0, 2)),
        "gate_i": c(np.asarray(x["L1_ffn_expert_indices"]).reshape(TB, P, 2).transpose(1, 0, 2)),
        "w1_g": x["L1_ffn_w1"], "w2_g": x["L1_ffn_w2"],
    }


def kernel(**inputs):
    import concourse.bacc as bacc
    from concourse.bass_utils import run_bass_kernel_spmd

    nc = bacc.Bacc("TRN2", target_bir_lowering=False, num_devices=1)
    arrays = {k: np.ascontiguousarray(v) for k, v in (layouts(inputs) | constants()).items()}
    aps = {k: nc.dram_tensor("in_" + k, v.shape, mybir.dt.from_np(v.dtype), kind="ExternalInput").ap() for k, v in arrays.items()}
    out = nc.dram_tensor("hidden", (B * L, D), F32, kind="ExternalOutput").ap()
    tower(nc, aps, out)
    got = run_bass_kernel_spmd(nc, [{"in_" + k: v for k, v in arrays.items()}], core_ids=[0])
    return got.results[0]["hidden"].reshape(B, L, D)
```
